# Optimizing a Trainium2 kernel written in Bass

```python
import numpy as np
import jax
import jax.numpy as jnp

def _softmax(x, axis=-1):
    return jax.nn.softmax(x, axis=axis)

def _gelu(x):
    return jax.nn.gelu(x, approximate=True)

def _silu(x):
    return jax.nn.silu(x)

def _sigmoid(x):
    return jax.nn.sigmoid(x)

def _layernorm(x, axis=-1, eps=1e-05):
    m = jnp.mean(x, axis=axis, keepdims=True)
    v = jnp.var(x, axis=axis, keepdims=True)
    return (x - m) / jnp.sqrt(v + eps)

def _scatter_add(tgt, idx, src, axis=0):
    return tgt.at[idx].add(src)

def _segment_sum(src, seg, n):
    return jax.ops.segment_sum(src, seg, n)
kernel_name = 'mk_gnn_resnorm_d4_gnn_r64_c6857a'

def setup_inputs(seed: int=0):
    np.random.seed(seed)
    _w = jnp.asarray

    def _rec_inputs():
        import jax
        import jax.numpy as jnp
        _gk = jax.random.key(seed)
        x = -0.000202 + 1 * jax.random.normal(jax.random.fold_in(_gk, 1), (50000, 128), jnp.float32)
        src = jax.random.randint(jax.random.fold_in(_gk, 2), (25000,), 0, 50000, jnp.int32)
        dst = jax.random.randint(jax.random.fold_in(_gk, 3), (25000,), 0, 50000, jnp.int32)
        _o = jnp.argsort(dst, stable=True)
        src = src[_o]
        dst = dst[_o]
        edge_type_8 = jax.random.randint(jax.random.fold_in(_gk, 13), (25000,), 0, 8, jnp.int32)
        edge_weight = jax.random.uniform(jax.random.fold_in(_gk, 14), (25000,), jnp.float32, 0.0, 0.999998)
        return (x, src, dst, edge_type_8, edge_weight)
    x, src, dst, edge_type_8, edge_weight = _rec_inputs()

    def _L0_gnn_setup():
        import jax, jax.numpy as jnp
        import numpy as np
        N, IN, H, D = (50000, 128, 4, 32)
        HID = H * D
        E = 12500
        key = jax.random.key(seed)
        ks = jax.random.split(key, 16)
        s_in = 1.0 / np.sqrt(IN)
        s_g = 1.0 / np.sqrt(3 * HID)
        inp = {'feat': jax.random.normal(ks[0], (N, IN), jnp.float32), 'src': jax.random.randint(ks[1], (E,), 0, N, jnp.int32), 'dst': jax.random.randint(ks[2], (E,), 0, N, jnp.int32), 'Wq': jax.random.normal(ks[3], (IN, HID), jnp.float32) * s_in, 'bq': jnp.zeros((HID,), jnp.float32), 'Wk': jax.random.normal(ks[4], (IN, HID), jnp.float32) * s_in, 'bk': jnp.zeros((HID,), jnp.float32), 'Wv': jax.random.normal(ks[5], (IN, HID), jnp.float32) * s_in, 'bv': jnp.zeros((HID,), jnp.float32), 'Ws': jax.random.normal(ks[6], (IN, HID), jnp.float32) * s_in, 'bs': jnp.zeros((HID,), jnp.float32), 'Wg': jax.random.normal(ks[7], (3 * HID, 1), jnp.float32) * s_g, 'bg': jnp.zeros((1,), jnp.float32), 'gamma': jnp.ones((HID,), jnp.float32), 'beta': jnp.zeros((HID,), jnp.float32), 'alpha': jnp.asarray(0.25, jnp.float32)}
        return inp
    _L0_gnn_all = _L0_gnn_setup()
    _L0_gnn_in = {k: v for k, v in _L0_gnn_all.items() if k in ('Wq', 'bq', 'Wk', 'bk', 'Wv', 'bv', 'Ws', 'bs', 'Wg', 'bg', 'gamma', 'beta', 'alpha')}
    del _L0_gnn_all

    def _L1_gnn_setup():
        import jax, jax.numpy as jnp
        import numpy as np
        N_NODES = 50000
        N_EDGES = 12500
        D = 128
        LN_EPS = 1e-05
        key = jax.random.key(seed)
        ks = jax.random.split(key, 8)
        x = jax.random.normal(ks[0], (N_NODES, D), dtype=jnp.float32)
        edge_index = jax.random.randint(ks[1], (2, N_EDGES), 0, N_NODES, dtype=jnp.int64)
        edge_weight = jax.random.uniform(ks[2], (N_EDGES,), dtype=jnp.float32)
        s = 0.05
        ew1 = jax.random.normal(ks[3], (3, 2 * D + 1, D), dtype=jnp.float32) * s
        ew2 = jax.random.normal(ks[4], (3, D, D), dtype=jnp.float32) * s
        nw1 = jax.random.normal(ks[5], (3, 2 * D, D), dtype=jnp.float32) * s
        nw2 = jax.random.normal(ks[6], (3, D, D), dtype=jnp.float32) * s
        zb = jnp.zeros((3, D), dtype=jnp.float32)
        return {'x': x, 'edge_index': edge_index, 'edge_weight': edge_weight, 'ew1': ew1, 'eb1': zb, 'ew2': ew2, 'eb2': zb, 'nw1': nw1, 'nb1': zb, 'nw2': nw2, 'nb2': zb, 'gamma': jnp.ones((D,), dtype=jnp.float32), 'beta': jnp.zeros((D,), dtype=jnp.float32)}
    _L1_gnn_all = _L1_gnn_setup()
    _L1_gnn_in = {k: v for k, v in _L1_gnn_all.items() if k in ('ew1', 'eb1', 'ew2', 'eb2', 'nw1', 'nb1', 'nw2', 'nb2', 'gamma', 'beta')}
    del _L1_gnn_all

    def _L2_gnn_setup():
        import jax, jax.numpy as jnp
        import numpy as np
        N_NODES = 50000
        N_EDGES = 12500
        IN_DIM = 128
        OUT_DIM = 128
        N_REL = 8
        key = jax.random.key(seed)
        k1, k2, k3, k4, k5 = jax.random.split(key, 5)
        x = jax.random.normal(k1, (N_NODES, IN_DIM), dtype=jnp.float32)
        edge_index = jax.random.randint(k2, (2, N_EDGES), 0, N_NODES, dtype=jnp.int32).astype(jnp.int64)
        edge_type = jax.random.randint(k3, (N_EDGES,), 0, N_REL, dtype=jnp.int32).astype(jnp.int64)
        W = jax.random.normal(k4, (N_REL, IN_DIM, OUT_DIM), dtype=jnp.float32) * 0.02
        W0 = jax.random.normal(k5, (IN_DIM, OUT_DIM), dtype=jnp.float32) * 0.02
        return {'x': x, 'edge_index': edge_index, 'edge_type': edge_type, 'num_nodes': N_NODES, 'W': W, 'W0': W0}
    _L2_gnn_all = _L2_gnn_setup()
    _L2_gnn_in = {k: v for k, v in _L2_gnn_all.items() if k in ('W', 'W0')}
    del _L2_gnn_all

    def _L3_gnn_setup():
        import jax, jax.numpy as jnp
        import numpy as np
        N, E, D_IN, H, D_OUT = (20000, 5000, 128, 4, 128)
        NEG_SLOPE = 0.2
        key = jax.random.key(seed)
        ks = jax.random.split(key, 6)
        x = jax.random.normal(ks[0], (N, D_IN), dtype=jnp.float32)
        W = jax.random.normal(ks[1], (D_IN, H * D_OUT), dtype=jnp.float32) * 0.05
        att_src = jax.random.normal(ks[2], (1, H, D_OUT), dtype=jnp.float32) * 0.05
        att_dst = jax.random.normal(ks[3], (1, H, D_OUT), dtype=jnp.float32) * 0.05
        bias = jax.random.normal(ks[4], (D_OUT,), dtype=jnp.float32) * 0.05
        edge_index = jax.random.randint(ks[5], (2, E), 0, N, dtype=jnp.int64)
        return {'x': x, 'W': W, 'att_src': att_src, 'att_dst': att_dst, 'bias': bias, 'edge_index': edge_index}
    _L3_gnn_all = _L3_gnn_setup()
    _L3_gnn_in = {k: v for k, v in _L3_gnn_all.items() if k in ('W', 'att_src', 'att_dst', 'bias')}
    del _L3_gnn_all
    return {'x': x, 'src': src, 'dst': dst, 'edge_type_8': edge_type_8, 'edge_weight': edge_weight, 'L0_gnn_Wq': _L0_gnn_in['Wq'], 'L0_gnn_bq': _L0_gnn_in['bq'], 'L0_gnn_Wk': _L0_gnn_in['Wk'], 'L0_gnn_bk': _L0_gnn_in['bk'], 'L0_gnn_Wv': _L0_gnn_in['Wv'], 'L0_gnn_bv': _L0_gnn_in['bv'], 'L0_gnn_Ws': _L0_gnn_in['Ws'], 'L0_gnn_bs': _L0_gnn_in['bs'], 'L0_gnn_Wg': _L0_gnn_in['Wg'], 'L0_gnn_bg': _L0_gnn_in['bg'], 'L0_gnn_gamma': _L0_gnn_in['gamma'], 'L0_gnn_beta': _L0_gnn_in['beta'], 'L0_gnn_alpha': _L0_gnn_in['alpha'], 'L1_gnn_ew1': _L1_gnn_in['ew1'], 'L1_gnn_eb1': _L1_gnn_in['eb1'], 'L1_gnn_ew2': _L1_gnn_in['ew2'], 'L1_gnn_eb2': _L1_gnn_in['eb2'], 'L1_gnn_nw1': _L1_gnn_in['nw1'], 'L1_gnn_nb1': _L1_gnn_in['nb1'], 'L1_gnn_nw2': _L1_gnn_in['nw2'], 'L1_gnn_nb2': _L1_gnn_in['nb2'], 'L1_gnn_gamma': _L1_gnn_in['gamma'], 'L1_gnn_beta': _L1_gnn_in['beta'], 'L2_gnn_W': _L2_gnn_in['W'], 'L2_gnn_W0': _L2_gnn_in['W0'], 'L3_gnn_W': _L3_gnn_in['W'], 'L3_gnn_att_src': _L3_gnn_in['att_src'], 'L3_gnn_att_dst': _L3_gnn_in['att_dst'], 'L3_gnn_bias': _L3_gnn_in['bias']}

def reference(x, src, dst, edge_type_8, edge_weight, L0_gnn_Wq, L0_gnn_bq, L0_gnn_Wk, L0_gnn_bk, L0_gnn_Wv, L0_gnn_bv, L0_gnn_Ws, L0_gnn_bs, L0_gnn_Wg, L0_gnn_bg, L0_gnn_gamma, L0_gnn_beta, L0_gnn_alpha, L1_gnn_ew1, L1_gnn_eb1, L1_gnn_ew2, L1_gnn_eb2, L1_gnn_nw1, L1_gnn_nb1, L1_gnn_nw2, L1_gnn_nb2, L1_gnn_gamma, L1_gnn_beta, L2_gnn_W, L2_gnn_W0, L3_gnn_W, L3_gnn_att_src, L3_gnn_att_dst, L3_gnn_bias):
    import jax
    import jax.numpy as jnp

    def _L0_gnn_ref(feat, src, dst, Wq, bq, Wk, bk, Wv, bv, Ws, bs, Wg, bg, gamma, beta, alpha):
        import jax, jax.numpy as jnp
        import numpy as np
        N, IN, H, D = (50000, 128, 4, 32)
        HID = H * D
        E = 12500
        n = feat.shape[0]
        q = (feat @ Wq + bq).reshape(n, H, D)
        k = (feat @ Wk + bk).reshape(n, H, D)
        v = (feat @ Wv + bv).reshape(n, H, D)
        a = jnp.einsum('ehd,ehd->eh', q[src], k[dst]) / jnp.sqrt(jnp.float32(D))
        m = jax.ops.segment_max(a, dst, num_segments=n)
        m = jax.lax.stop_gradient(jnp.where(jnp.isfinite(m), m, 0.0))
        ex = jnp.exp(a - m[dst])
        denom = jax.ops.segment_sum(ex, dst, num_segments=n)
        denom = jnp.where(denom > 0, denom, 1.0)
        sa = ex / denom[dst]
        msg = v[src] * sa[:, :, None]
        agg = jax.ops.segment_sum(msg, dst, num_segments=n).reshape(n, HID)
        skip = feat @ Ws + bs
        g = jax.nn.sigmoid(jnp.concatenate([skip, agg, skip - agg], axis=-1) @ Wg + bg)
        rst = g * skip + (1.0 - g) * agg
        mu = rst.mean(-1, keepdims=True)
        var = rst.var(-1, keepdims=True)
        rst = (rst - mu) * jax.lax.rsqrt(var + 1e-05) * gamma + beta
        rst = jnp.where(rst >= 0, rst, alpha * rst)
        return rst

    def _L1_gnn_ref(x, edge_index, edge_weight, ew1, eb1, ew2, eb2, nw1, nb1, nw2, nb2, gamma, beta):
        import jax, jax.numpy as jnp
        import numpy as np
        N_NODES = 50000
        N_EDGES = 12500
        D = 128
        LN_EPS = 1e-05
        src = edge_index[0]
        dst = edge_index[1]
        ea = edge_weight[:, None]
        n = x.shape[0]
        cnt = jax.ops.segment_sum(jnp.ones((dst.shape[0],), x.dtype), dst, num_segments=n)
        denom = jnp.maximum(cnt, 1.0)[:, None]
        for l in range(ew1.shape[0]):
            x_i = x[dst]
            x_j = x[src]
            m = jnp.concatenate([x_i, x_j, ea], axis=-1)
            m = jax.nn.relu(m @ ew1[l] + eb1[l])
            m = jax.nn.relu(m @ ew2[l] + eb2[l])
            aggr = jax.ops.segment_sum(m, dst, num_segments=n) / denom
            h = jnp.concatenate([x, aggr], axis=-1)
            h = jax.nn.relu(h @ nw1[l] + nb1[l])
            x = jax.nn.relu(h @ nw2[l] + nb2[l])
            x = jax.nn.relu(x)
        mu = jnp.mean(x, axis=-1, keepdims=True)
        var = jnp.var(x, axis=-1, keepdims=True)
        x = (x - mu) * jax.lax.rsqrt(var + LN_EPS) * gamma + beta
        return x

    def _L2_gnn_ref(x, edge_index, edge_type, num_nodes, W, W0):
        import jax, jax.numpy as jnp
        import numpy as np
        N_NODES = 50000
        N_EDGES = 12500
        IN_DIM = 128
        OUT_DIM = 128
        N_REL = 8
        src = edge_index[0]
        dst = edge_index[1]
        xW = jnp.einsum('nd,rdo->rno', x, W)
        msgs = xW[edge_type, src]
        agg = jax.ops.segment_sum(msgs, dst, num_segments=num_nodes)
        out = x @ W0 + agg
        deg = jax.ops.segment_sum(jnp.ones_like(dst, dtype=out.dtype), dst, num_segments=num_nodes)
        deg = jnp.maximum(deg, 1.0)
        return out / deg[:, None]

    def _L3_gnn_ref(x, W, att_src, att_dst, bias, edge_index):
        import jax, jax.numpy as jnp
        import numpy as np
        N, E, D_IN, H, D_OUT = (20000, 5000, 128, 4, 128)
        NEG_SLOPE = 0.2
        n = x.shape[0]
        h = (x @ W).reshape(n, H, D_OUT)
        loop = jnp.arange(n, dtype=edge_index.dtype)
        src = jnp.concatenate([edge_index[0], loop])
        dst = jnp.concatenate([edge_index[1], loop])
        a_src = (h * att_src).sum(-1)
        a_dst = (h * att_dst).sum(-1)
        logits = a_src[src] + a_dst[dst]
        logits = jnp.where(logits >= 0, logits, NEG_SLOPE * logits)
        m = jax.ops.segment_max(logits, dst, num_segments=n)
        e = jnp.exp(logits - m[dst])
        denom = jax.ops.segment_sum(e, dst, num_segments=n)
        alpha = e / denom[dst]
        msg = alpha[:, :, None] * h[src]
        out = jax.ops.segment_sum(msg, dst, num_segments=n)
        out = out.mean(axis=1) + bias
        return jax.nn.relu(out)
    edge_index = jnp.stack([src, dst])
    x = _layernorm(x + _L0_gnn_ref(x, src, dst, L0_gnn_Wq, L0_gnn_bq, L0_gnn_Wk, L0_gnn_bk, L0_gnn_Wv, L0_gnn_bv, L0_gnn_Ws, L0_gnn_bs, L0_gnn_Wg, L0_gnn_bg, L0_gnn_gamma, L0_gnn_beta, L0_gnn_alpha), axis=-1)
    x = _layernorm(x + _L1_gnn_ref(x, edge_index, edge_weight, L1_gnn_ew1, L1_gnn_eb1, L1_gnn_ew2, L1_gnn_eb2, L1_gnn_nw1, L1_gnn_nb1, L1_gnn_nw2, L1_gnn_nb2, L1_gnn_gamma, L1_gnn_beta), axis=-1)
    x = _layernorm(x + _L2_gnn_ref(x, edge_index, edge_type_8, 50000, L2_gnn_W, L2_gnn_W0), axis=-1)
    x = _layernorm(x + _L3_gnn_ref(x, L3_gnn_W, L3_gnn_att_src, L3_gnn_att_dst, L3_gnn_bias, edge_index), axis=-1)
    return x

_drawn_inputs = setup_inputs


def setup_inputs(seed=0):
    import zlib

    import numpy as np

    out = dict(_drawn_inputs(seed))
    spreads = {'L0_gnn_bq': (0.0, 0.8),
     'L0_gnn_bk': (0.0, 0.8),
     'L0_gnn_bv': (0.0, 0.36),
     'L0_gnn_bs': (0.0, 0.1),
     'L0_gnn_gamma': (1.0, 0.2),
     'L0_gnn_beta': (0.0, 0.1),
     'L1_gnn_eb1': (0.0, 0.284),
     'L1_gnn_eb2': (0.0, 0.1),
     'L1_gnn_nb1': (0.0, 0.1),
     'L1_gnn_nb2': (0.0, 0.1),
     'L1_gnn_gamma': (1.0, 0.2),
     'L1_gnn_beta': (0.0, 0.1)}
    factors = {'edge_weight': 8.0, 'L3_gnn_att_src': 8.0, 'L3_gnn_att_dst': 8.0}
    for name, (base, spread) in spreads.items():
        noise = np.random.default_rng([zlib.crc32(name.encode()), seed]).standard_normal(out[name].shape)
        drawn = base * np.exp(spread * noise) if base else spread * noise
        out[name] = jnp.asarray(drawn.astype(out[name].dtype))
    for name, factor in factors.items():
        out[name] = (out[name] * factor).astype(out[name].dtype)
    return out
```

```python
from contextlib import ExitStack

import concourse.bass as bass
from concourse import mybir

ALU = mybir.AluOpType
ACT = mybir.ActivationFunctionType
F32 = mybir.dt.float32
I32 = mybir.dt.int32

D = 128
N = 50000
E = 25000
ET, TILES = 125, 4
EC = ET * TILES
E_ITERS = E // (2 * EC)
NC_ = 4 * D
N_ITERS = -(-N // (2 * NC_))
SLOT1_START = N - N_ITERS * NC_
ROW = 132
H0, H3 = 4, 4
EPS = 1e-5
FAR = 1.0e30
SKIP = 65536
SLOTS = (0, 1)


class Steps:

    def __init__(self, *names):
        self.order = []
        for name in names:
            step, _, slot = name.partition("/")
            self.order += [(step, int(slot))] if slot else [(step, 0), (step, 1)]
        self.per_iteration = len(self.order)

    def before(self, name, i, u):
        return i * self.per_iteration + (self.order.index((name, u)) + 1)

    def done(self, name, i, u):
        return i * self.per_iteration + (self.per_iteration + self.order.index((name, u)) + 1)


class Pass:

    def __init__(self, nc, sems, ctx, tag):
        self.nc, self.sems, self.ctx, self.tag = nc, sems, ctx, tag

    def sb(self, name, shape, dt=F32):
        return self.ctx.enter_context(self.nc.sbuf_tensor(f"{self.tag}_{name}", shape, dt))

    def bank(self, name):
        return self.ctx.enter_context(self.nc.psum_tensor(f"{self.tag}_{name}", [128, 512], F32))

    def sem(self, name):
        return self.sems.enter_context(self.nc.semaphore(f"{self.tag}_{name}"))

    def pair(self, make, name, *args):
        return [make(f"{name}{u}", *args) for u in SLOTS]


def settled(eng, passed):
    eng.sem_inc(passed, 1)


def as_rows(dram, i, u, width=D):
    start = u * SLOT1_START + i * NC_
    return dram[bass.ds(start, NC_), :].rearrange("(p j) d -> p j d", j=4)



def setup_pass(nc, sems, keep, t):
    with ExitStack() as ctx:
        p = Pass(nc, sems, ctx, "setup")
        gidx, sidx, ident = keep["gather_index"], keep["scatter_index"], keep["ident"]
        src = p.sb("src", [ET, E // ET], I32)
        dst = p.sb("dst", [ET, E // ET], I32)
        nxt = p.sb("nxt", [ET, E // ET], I32)
        same = p.sb("same", [ET, E // ET], I32)
        zeros = p.sb("zeros", [96, N * ROW // 96 // 10])
        loaded, zeroed, did, filled = (p.sem(s) for s in ("loaded", "zeroed", "did", "filled"))
        chunked = lambda a: a[:].rearrange("p (c j) -> p c j", j=TILES)
        with nc.Block() as block:
            @block.sync
            def _(sp):
                for tile, dram in ((src, t["src_tiles"]), (dst, t["dst_tiles"]), (nxt, t["next_tiles"]),
                                   (ident, t["ident"])):
                    sp.dma_start(tile[:], dram).then_inc(loaded, 16)
                sp.wait_ge(zeroed, 1)
                flat = t["agg_rows"].rearrange("n r -> (n r)").rearrange("(k p f) -> k p f", k=10, p=96)
                for k in range(10):
                    sp.dma_start(flat[k], zeros[:]).then_inc(filled, 16)
                sp.wait_ge(filled, 160)

            @block.vector
            def _(dve):
                nc.vector.memset(zeros[:], 0.0).then_inc(zeroed, 1)
                dve.wait_ge(loaded, 64)
                nc.vector.tensor_copy(gidx[:, :, 0:TILES], chunked(src))
                nc.vector.tensor_copy(gidx[:, :, TILES:2 * TILES], chunked(dst))
                nc.vector.tensor_tensor(same[:], dst[:], nxt[:], ALU.is_equal).then_inc(did, 1)
                dve.wait_ge(did, 1)
                nc.vector.scalar_tensor_tensor(out=sidx[:], in0=chunked(same), scalar=float(SKIP),
                                               in1=chunked(dst), op0=ALU.mult, op1=ALU.add).then_inc(did, 1)



class EdgePass(Pass):
    def __init__(self, nc, sems, ctx, tag, keep, table, agg, ends):
        super().__init__(nc, sems, ctx, tag)
        self.keep, self.table, self.agg, self.ends = keep, table, agg, ends
        self.end_rows = self.pair(self.sb, "rows_of_ends", [ET, 4 * ends, D])
        self.gi = self.pair(self.sb, "gi", [ET, 4 * ends], I32)
        self.si = self.pair(self.sb, "si", [ET, TILES], I32)
        self.out_rows = self.pair(self.sb, "out_rows", [ET, TILES, ROW])
        self.dst = self.pair(self.sb, "dst", [128, EC], I32)
        self.prev = self.pair(self.sb, "prev", [128, EC], I32)
        self.flag = self.pair(self.sb, "same_as_before", [128, EC])
        self.gathered = self.pair(self.sem, "gathered")
        self.scattered = self.pair(self.sem, "scattered")
        self.streamed = self.pair(self.sem, "streamed")
        self.weights = self.sem("weights")
        self.passed = self.sem("passed")
        self.first = self.pair(self.sb, "first", [16, 16])
        self.pe_did, self.act_did, self.dve_did, self.pool_did = (
            self.sem(s) for s in ("pe_did", "act_did", "dve_did", "pool_did"))

    def pool_program(self, gp, PE, ACTS, E_=E_ITERS):
        nc = self.nc
        gidx, sidx = self.keep["gather_index"], self.keep["scatter_index"]
        k = 4 * self.ends
        def after_waits():
            settled(gp, self.passed)

        def gathers(i, u, copies, first=False):
            if not first:
                gp.wait_ge(self.pe_did, PE.before("turn", i, u))
                gp.wait_ge(self.gathered[u], 16 * k * i)
                after_waits()
            nc.gpsimd.tensor_copy(self.gi[u][:], gidx[:, bass.ds(2 * i + u, 1), 0:k].rearrange(
                "p a j -> p (a j)")).then_inc(self.pool_did, 1)
            gp.wait_ge(self.pool_did, copies + (u + 1))
            after_waits()
            for j in range(k):
                gp.indirect_dma_start(self.end_rows[u][:, j, :], None, self.table,
                                      bass.IndirectOffsetOnAxis(ap=self.gi[u][:, j:j + 1], axis=0)
                                      ).then_inc(self.gathered[u], 16)

        def scatters(i, u, copies):
            gp.wait_ge(self.scattered[u], i * (16 * TILES) + 16)
            gp.wait_ge(self.act_did, ACTS.done("rows", i, u))
            after_waits()
            nc.gpsimd.tensor_copy(self.si[u][:], sidx[:, bass.ds(2 * i + u, 1), :].rearrange(
                "p a j -> p (a j)")).then_inc(self.pool_did, 1)
            gp.wait_ge(self.pool_did, copies + (u + 1))
            after_waits()
            for j in range(TILES):
                gp.indirect_dma_start(self.agg, bass.IndirectOffsetOnAxis(ap=self.si[u][:, j:j + 1], axis=0),
                                      self.out_rows[u][:, j, :], None, bounds_check=N - 1,
                                      oob_is_err=False).then_inc(self.scattered[u], 16)

        for u in SLOTS:
            gp.dma_start(self.first[u][:], self.keep["small"]).then_inc(self.scattered[u], 16)
            gathers(0, u, 0, first=True)
        with gp.Fori(0, E_ - 1) as i:
            for u in SLOTS:
                gathers(i + 1, u, i * 4 + 2)
            for u in SLOTS:
                scatters(i, u, i * 4 + 4)
        for u in SLOTS:
            scatters(E_ - 1, u, 4 * E_ - 2)
        for u in SLOTS:
            gp.wait_ge(self.scattered[u], 16 * TILES * E_ + 16)
        after_waits()

    def stream(self, sp, i, u, t, extra=()):
        at = 2 * i + u
        settled(sp, self.passed)
        sp.dma_start(self.dst[u][:], t["dst_rows"][bass.ds(at, 1), :].broadcast_to([128, EC])
                     ).then_inc(self.streamed[u], 16)
        sp.dma_start(self.prev[u][:], t["prev_rows"][bass.ds(at, 1), :].broadcast_to([128, EC])
                     ).then_inc(self.streamed[u], 16)
        for tile, rows, lanes in extra:
            sp.dma_start(tile, rows[bass.ds(at, 1), :].broadcast_to([lanes, EC])
                         ).then_inc(self.streamed[u], 16)

    def turn(self, pe, i, u, banks, PE):
        for end in range(self.ends):
            for j in range(TILES):
                last = self.nc.tensor.transpose(banks[end][:, j * ET:(j + 1) * ET],
                                                self.end_rows[u][:, end * TILES + j, :],
                                                self.keep["ident"][0:ET, 0:ET])
        last.then_inc(self.pe_did, 1)


def tile_of(a, j):
    return a[:, j * ET:(j + 1) * ET]



def layer0_edges(nc, sems, keep, t):
    with ExitStack() as ctx:
        p = EdgePass(nc, sems, ctx, "e0", keep, t["x"], t["agg_rows"], 2)
        ident = keep["ident"]
        wq, wk, wv = (p.sb(n, [D, D]) for n in ("wq", "wk", "wv"))
        bq, bk, bv = (p.sb(n, [D, 1]) for n in ("bq", "bk", "bv"))
        heads = p.sb("heads", [D, H0])
        spread = p.sb("spread", [H0, D])
        wg = p.sb("wg", [D, 3])
        gate_agg = p.sb("gate_agg", [D, 1])
        xs, xd, qs, pr, vb, wv_ = (p.pair(p.sb, n, [D, EC]) for n in ("xs", "xd", "qs", "pr", "vb", "wv_"))
        num, agg = p.pair(p.sb, "num", [D, EC]), p.pair(p.sb, "agg", [D, EC])
        pen = p.pair(p.sb, "pen", [H0, EC])
        m = p.pair(p.sb, "m", [H0, EC + 1])
        de, ce = p.pair(p.sb, "de", [H0, 2, EC]), p.pair(p.sb, "ce", [H0, 2, EC])
        den, rden = p.pair(p.sb, "den", [H0, EC]), p.pair(p.sb, "rden", [H0, EC])
        A, B, C, DD = (p.pair(p.bank, n) for n in "ABCD")
        PE = Steps("turn", "qkv", "logits", "spread_ce", "spread_den", "rows")
        AC = Steps("xs", "q", "v", "exp", "rows")
        DV = Steps("flag", "pen", "xd", "product", "carry/0", "max/0", "carry/1", "max/1", "drop", "differences", "den", "rden",
                   "weighted", "num", "agg")
        pe_did, act_did, dve_did, streamed = p.pe_did, p.act_did, p.dve_did, p.streamed
        WEIGHTS = 16 * 9
        with nc.Block() as block:
            @block.sync
            def _(sp):
                for tile, dram in ((wq, t["L0_Wq"]), (wk, t["L0_Wk"]), (wv, t["L0_Wv"]), (bq, t["L0_bq"]),
                                   (bk, t["L0_bk"]), (bv, t["L0_bv"]), (heads, t["head_mask"]),
                                   (spread, t["head_spread"]), (wg, t["L0_Wg"])):
                    sp.dma_start(tile[:], dram).then_inc(p.weights, 16)
                with sp.Fori(0, E_ITERS) as i:
                    for u in SLOTS:
                        sp.wait_ge(dve_did, DV.before("flag", i, u))
                        p.stream(sp, i, u, t)

            @block.gpsimd
            def _(gp):
                p.pool_program(gp, PE, AC)

            @block.tensor
            def _(pe):
                pe.sem_inc(pe_did, PE.per_iteration)
                pe.wait_ge(p.weights, WEIGHTS)
                with pe.Fori(0, E_ITERS) as i:
                    for u in SLOTS:
                        pe.wait_ge(p.gathered[u], i * 128 + 128)
                        pe.wait_ge(act_did, AC.before("rows", i, u))
                        p.turn(pe, i, u, (A[u], B[u]), PE)
                    for u in SLOTS:
                        pe.wait_ge(act_did, AC.done("xs", i, u))
                        pe.wait_ge(dve_did, DV.done("xd", i, u))
                        nc.tensor.matmul(C[u][:, 0:EC], wq[:], xs[u][:], start=True, stop=True)
                        nc.tensor.matmul(DD[u][:, 0:EC], wk[:], xd[u][:], start=True, stop=True)
                        nc.tensor.matmul(A[u][:, 0:EC], wv[:], xs[u][:], start=True, stop=True).then_inc(pe_did, 1)
                    for u in SLOTS:
                        pe.wait_ge(dve_did, DV.done("product", i, u))
                        nc.tensor.matmul(B[u][0:H0, 0:EC], heads[:], pr[u][:], start=True, stop=True
                                         ).then_inc(pe_did, 1)
                    for u in SLOTS:
                        pe.wait_ge(act_did, AC.done("exp", i, u))
                        nc.tensor.matmul(C[u][:, 0:EC], spread[:], ce[u][:, 0, :], start=True, stop=True)
                        nc.tensor.matmul(DD[u][:, 0:EC], spread[:], ce[u][:, 1, :], start=True, stop=True
                                         ).then_inc(pe_did, 1)
                    for u in SLOTS:
                        pe.wait_ge(dve_did, DV.done("rden", i, u))
                        nc.tensor.matmul(B[u][:, 0:EC], spread[:], rden[u][:], start=True, stop=True
                                         ).then_inc(pe_did, 1)
                    for u in SLOTS:
                        pe.wait_ge(dve_did, DV.done("agg", i, u))
                        for j in range(TILES):
                            nc.tensor.matmul(A[u][0:ET, j * D:(j + 1) * D], tile_of(agg[u], j), ident[:],
                                             start=True, stop=True)
                        for j in range(TILES):
                            last = nc.tensor.matmul(B[u][0:ET, j:j + 1], tile_of(agg[u], j), gate_agg[:],
                                                    start=True, stop=True)
                        last.then_inc(pe_did, 1)

            @block.scalar
            def _(act):
                act.sem_inc(act_did, AC.per_iteration)
                act.wait_ge(p.weights, WEIGHTS)
                with act.Fori(0, E_ITERS) as i:
                    for u in SLOTS:
                        act.wait_ge(pe_did, PE.done("turn", i, u))
                        nc.scalar.activation(xs[u][:], A[u][:, 0:EC], ACT.Copy).then_inc(act_did, 1)
                    for u in SLOTS:
                        act.wait_ge(pe_did, PE.done("qkv", i, u))
                        act.wait_ge(dve_did, DV.before("product", i, u))
                        nc.scalar.activation(qs[u][:], C[u][:, 0:EC], ACT.Identity, bias=bq[:]).then_inc(act_did, 1)
                    for u in SLOTS:
                        act.wait_ge(dve_did, DV.before("weighted", i, u))
                        nc.scalar.activation(vb[u][:], A[u][:, 0:EC], ACT.Identity, bias=bv[:]).then_inc(act_did, 1)
                    for u in SLOTS:
                        act.wait_ge(dve_did, DV.done("differences", i, u))
                        act.wait_ge(pe_did, PE.before("spread_ce", i, u))
                        nc.scalar.activation(ce[u][:], de[u][:], ACT.Exp).then_inc(act_did, 1)
                    for u in SLOTS:
                        act.wait_ge(pe_did, PE.done("rows", i, u))
                        act.wait_ge(p.scattered[u], i * 64 + 16)
                        nc.scalar.activation(p.out_rows[u][:, :, 0:D],
                                             A[u][0:ET, :].rearrange("p (j d) -> p j d", d=D), ACT.Copy)
                        nc.scalar.activation(p.out_rows[u][:, :, D:D + 1],
                                             B[u][0:ET, 0:TILES].rearrange("p (j a) -> p j a", a=1),
                                             ACT.Copy).then_inc(act_did, 1)

            @block.vector
            def _(dve):
                for u in SLOTS:
                    nc.vector.memset(p.out_rows[u][:], 0.0)
                nc.vector.memset(m[1][:], 0.0)
                nc.vector.memset(den[1][:], 1.0)
                dve.wait_ge(p.weights, WEIGHTS)
                nc.vector.tensor_tensor(gate_agg[:], wg[:, 1:2], wg[:, 2:3], ALU.subtract)
                nc.vector.memset(num[1][:], 0.0).then_inc(dve_did, DV.per_iteration)
                with dve.Fori(0, E_ITERS) as i:
                    for u in SLOTS:
                        dve.wait_ge(streamed[u], i * 32 + 32)
                        nc.vector.tensor_tensor(p.flag[u][:], p.dst[u][:], p.prev[u][:], ALU.is_equal
                                                ).then_inc(dve_did, 1)
                    for u in SLOTS:
                        dve.wait_ge(dve_did, DV.done("flag", i, u))
                        nc.vector.tensor_scalar(pen[u][:], p.flag[u][0:H0, :], FAR, -FAR, ALU.mult, ALU.add
                                                ).then_inc(dve_did, 1)
                    for u in SLOTS:
                        dve.wait_ge(pe_did, PE.done("turn", i, u))
                        nc.vector.tensor_copy(xd[u][:], B[u][:, 0:EC]).then_inc(dve_did, 1)
                    for u in SLOTS:
                        dve.wait_ge(act_did, AC.done("q", i, u))
                        nc.vector.scalar_tensor_tensor(out=pr[u][:], in0=DD[u][:, 0:EC], scalar=bk[:],
                                                       in1=qs[u][:], op0=ALU.add, op1=ALU.mult
                                                       ).then_inc(dve_did, 1)
                    for u in SLOTS:
                        dve.wait_ge(dve_did, DV.before("max", i, 1) if u == 0 else DV.done("max", i, 0))
                        nc.vector.tensor_copy(m[u][:, 0:1], m[1 - u][:, EC:EC + 1]).then_inc(dve_did, 1)
                        dve.wait_ge(pe_did, PE.done("logits", i, u))
                        dve.wait_ge(dve_did, DV.done("carry", i, u))
                        nc.vector.tensor_tensor_scan(m[u][:, 1:EC + 1], pen[u][:], B[u][0:H0, 0:EC], m[u][:, 0:1],
                                                     ALU.add, ALU.max).then_inc(dve_did, 1)
                    for u in SLOTS:
                        dve.wait_ge(dve_did, DV.done("max", i, u))
                        nc.vector.tensor_tensor(de[u][:, 0, :], m[u][:, 0:EC], m[u][:, 1:EC + 1], ALU.subtract
                                                ).then_inc(dve_did, 1)
                    for u in SLOTS:
                        dve.wait_ge(dve_did, DV.done("drop", i, u))
                        nc.vector.tensor_tensor(de[u][:, 0, :], de[u][:, 0, :], pen[u][:], ALU.add)
                        nc.vector.tensor_tensor(de[u][:, 1, :], B[u][0:H0, 0:EC], m[u][:, 1:EC + 1], ALU.subtract
                                                ).then_inc(dve_did, 1)
                    for u in SLOTS:
                        dve.wait_ge(act_did, AC.done("exp", i, u))
                        dve.wait_ge(dve_did, DV.before("den", i, 1) if u == 0 else DV.done("den", i, 0))
                        nc.vector.tensor_tensor_scan(den[u][:], ce[u][:, 0, :], ce[u][:, 1, :],
                                                     den[1 - u][:, EC - 1:EC], ALU.mult, ALU.add
                                                     ).then_inc(dve_did, 1)
                    for u in SLOTS:
                        dve.wait_ge(dve_did, DV.done("den", i, u))
                        dve.wait_ge(pe_did, PE.before("spread_den", i, u))
                        nc.vector.reciprocal(rden[u][:], den[u][:]).then_inc(dve_did, 1)
                    for u in SLOTS:
                        dve.wait_ge(pe_did, PE.done("spread_ce", i, u))
                        dve.wait_ge(act_did, AC.done("v", i, u))
                        nc.vector.tensor_tensor(wv_[u][:], vb[u][:], DD[u][:, 0:EC], ALU.mult
                                                ).then_inc(dve_did, 1)
                    for u in SLOTS:
                        dve.wait_ge(dve_did, DV.done("weighted", i, u))
                        dve.wait_ge(dve_did, DV.before("num", i, 1) if u == 0 else DV.done("num", i, 0))
                        nc.vector.tensor_tensor_scan(num[u][:], C[u][:, 0:EC], wv_[u][:], num[1 - u][:, EC - 1:EC],
                                                     ALU.mult, ALU.add).then_inc(dve_did, 1)
                    for u in SLOTS:
                        dve.wait_ge(dve_did, DV.done("num", i, u))
                        dve.wait_ge(pe_did, PE.done("spread_den", i, u))
                        nc.vector.tensor_tensor(agg[u][:], num[u][:], B[u][:, 0:EC], ALU.mult).then_inc(dve_did, 1)



class NodePass(Pass):

    def __init__(self, nc, sems, ctx, tag, keep, dram_in, dram_agg, dram_out, dram_residual=None):
        super().__init__(nc, sems, ctx, tag)
        self.keep, self.dram_in, self.dram_agg, self.dram_out = keep, dram_in, dram_agg, dram_out
        self.dram_residual = dram_residual
        self.rows = self.pair(self.sb, "rows", [128, 4, D])
        self.sums = self.pair(self.sb, "sums", [128, 4, ROW])
        if dram_residual is not None:
            self.residual = self.pair(self.sb, "residual", [128, 4, D])
        self.out = self.pair(self.sb, "out", [128, 4, D])
        self.loaded = self.pair(self.sem, "loaded")
        self.stored = self.pair(self.sem, "stored")
        self.per_load = 16 * (2 if dram_residual is None else 3)
        self.weights = self.sem("weights")
        self.passed = self.sem("passed")
        self.first = self.pair(self.sb, "first", [16, 16])
        self.pe_did, self.act_did, self.dve_did, self.pool_did = (
            self.sem(s) for s in ("pe_did", "act_did", "dve_did", "pool_did"))
        self.stats = self.pair(self.sb, "stats", [128, 4, 6])
        self.moments = self.pair(self.sb, "moments", [128, 4, 2])
        self.var = self.pair(self.sb, "var", [128, 4])
        self.std = self.pair(self.sb, "std", [128, 4])
        self.rstd = self.pair(self.sb, "rstd", [128, 4])

    def sync_program(self, sp, free, filled):
        def load(i, u, first=False):
            if not first:
                free(i, u)
            sp.dma_start(self.rows[u][:], as_rows(self.dram_in, i, u)).then_inc(self.loaded[u], 16)
            sp.dma_start(self.sums[u][:], as_rows(self.dram_agg, i, u)).then_inc(self.loaded[u], 16)
            if self.dram_residual is not None:
                sp.dma_start(self.residual[u][:], as_rows(self.dram_residual, i, u)
                             ).then_inc(self.loaded[u], 16)

        def store(i, u):
            filled(i, u)
            settled(sp, self.passed)
            sp.dma_start(as_rows(self.dram_out, i, u), self.out[u][:]).then_inc(self.stored[u], 16)

        for u in SLOTS:
            sp.dma_start(self.first[u][:], self.keep["small"]).then_inc(self.stored[u], 16)
            load(0, u, first=True)
        with sp.Fori(0, N_ITERS - 1) as i:
            for u in SLOTS:
                load(i + 1, u)
            for u in SLOTS:
                store(i, u)
        for u in SLOTS:
            store(N_ITERS - 1, u)
        for u in SLOTS:
            sp.wait_ge(self.stored[u], 16 * N_ITERS + 16)

    def turn(self, bank, u):
        for j in range(4):
            last = self.nc.tensor.transpose(bank[:, j * D:(j + 1) * D], self.rows[u][:, j, :],
                                            self.keep["ident"][:])
        last.then_inc(self.pe_did, 1)


    def norm_stats(self, dve, i, x, V, A, k, source):
        nc = self.nc
        for u in SLOTS:
            dve.wait_ge(self.dve_did, V.done(source, i, u))
            for j in range(4):
                last = nc.vector.bn_stats(self.stats[u][:, j, :], x[u][:, j, :])
            last.then_inc(self.dve_did, 1)
        for u in SLOTS:
            dve.wait_ge(self.dve_did, V.done(f"{k}_stats", i, u))
            settled(dve, self.passed)
            for j in range(4):
                last = nc.vector.bn_aggr(self.moments[u][:, j, :], self.stats[u][:, j, :])
            last.then_inc(self.dve_did, 1)
        for u in SLOTS:
            dve.wait_ge(self.dve_did, V.done(f"{k}_moments", i, u))
            nc.vector.tensor_scalar(self.var[u][:], self.moments[u][:, :, 1], EPS, None, ALU.add
                                    ).then_inc(self.dve_did, 1)
        for u in SLOTS:
            dve.wait_ge(self.act_did, A.done(f"{k}_std", i, u))
            nc.vector.reciprocal(self.rstd[u][:], self.std[u][:]).then_inc(self.dve_did, 1)

    def norm_std(self, act, i, V, k):
        for u in SLOTS:
            act.wait_ge(self.dve_did, V.done(f"{k}_var", i, u))
            self.nc.scalar.activation(self.std[u][:], self.var[u][:], ACT.Sqrt).then_inc(self.act_did, 1)

    def norm_apply(self, dve, i, x, y, V, k, wait=None):
        for u in SLOTS:
            dve.wait_ge(self.dve_did, V.done(f"{k}_rstd", i, u))
            if wait:
                wait(i, u)
            for j in range(4):
                last = self.nc.vector.tensor_scalar(y[u][:, j, :], x[u][:, j, :], self.moments[u][:, j, 0:1],
                                                    self.rstd[u][:, j:j + 1], ALU.subtract, ALU.mult)
            last.then_inc(self.dve_did, 1)


def norm_steps(k):
    return f"{k}_stats", f"{k}_moments", f"{k}_var", f"{k}_rstd", f"{k}_apply"


def four(row):
    return row.broadcast_to([128, D])


def each_tile(a):
    return a[:].rearrange("p (a d) -> p a d", a=1).broadcast_to([128, 4, D])


def flat(a):
    return a[:].rearrange("p j d -> p (j d)")


def tiles(bank):
    return bank[:].rearrange("p (j d) -> p j d", d=D)



def layer0_nodes(nc, sems, keep, t):
    with ExitStack() as ctx:
        p = NodePass(nc, sems, ctx, "n0", keep, t["x"], t["agg_rows"], t["x1"])
        ws, wst = p.sb("ws", [D, D]), p.sb("wst", [D, D])
        wg = p.sb("wg", [D, 3])
        bs_one, bs_col = p.sb("bs_one", [D, 1]), p.sb("bs_col", [D, 128])
        bs, gamma, beta = (p.sb(n, [128, D]) for n in ("bs", "gamma", "beta"))
        alpha, bg, rest = (p.sb(n, [128, 1]) for n in ("alpha", "bg", "rest"))
        gate_skip, gate_rows, off = p.sb("gate_skip", [D, 1]), p.sb("gate_rows", [D, 1]), p.sb("off", [128, 1])
        xt = p.pair(p.sb, "xt", [D, NC_])
        less, gap, mix, nrm, aff, pos, res = (p.pair(p.sb, n, [128, 4, D]) for n in (
            "less", "gap", "mix", "nrm", "aff", "pos", "res"))
        z, ez, ez1, g = (p.pair(p.sb, n, [128, 4]) for n in ("z", "ez", "ez1", "g"))
        A, B, C = (p.pair(p.bank, n) for n in "ABC")
        setup_did = p.sem("setup_did")
        PE = Steps("turn", "skip")
        AC = Steps("xt", "exp", "in_std", "relu", "out_std")
        DV = Steps("z", "gap", "ez1", "g", "mix", *norm_steps("in"), "leak", "res", *norm_steps("out"))
        PO = Steps("less", "gamma", "beta")
        pe_did, act_did, dve_did, pool_did = p.pe_did, p.act_did, p.dve_did, p.pool_did
        WEIGHTS = 16 * 9
        with nc.Block() as block:
            @block.sync
            def _(sp):
                for tile, dram in ((ws[:], t["L0_Ws"]), (wst[:], t["L0_Ws_turned"]), (wg[:], t["L0_Wg"]),
                                   (bs_one[:], t["L0_bs"]),
                                   (bs[:], four(t["L0_bs_row"])), (gamma[:], four(t["L0_gamma"])),
                                   (beta[:], four(t["L0_beta"])), (alpha[:], t["L0_alpha"].broadcast_to([128, 1])),
                                   (bg[:], t["L0_bg"].broadcast_to([128, 1]))):
                    sp.dma_start(tile, dram).then_inc(p.weights, 16)

                def free(i, u):
                    sp.wait_ge(dve_did, DV.before("leak", i, u))
                    settled(sp, p.passed)
                    sp.wait_ge(pe_did, PE.before("turn", i, u))
                    settled(sp, p.passed)
                    sp.wait_ge(pool_did, PO.before("less", i, u))
                    settled(sp, p.passed)

                p.sync_program(sp, free, lambda i, u: sp.wait_ge(dve_did, DV.done("out_apply", i, u)))

            @block.gpsimd
            def _(gp):
                gp.sem_inc(pool_did, PO.per_iteration)
                gp.wait_ge(p.weights, WEIGHTS)
                with gp.Fori(0, N_ITERS) as i:
                    for u in SLOTS:
                        gp.wait_ge(p.loaded[u], i * p.per_load + p.per_load)
                        gp.wait_ge(dve_did, DV.before("gap", i, u))
                        nc.gpsimd.tensor_tensor(less[u][:], p.sums[u][:, :, 0:D], each_tile(bs), ALU.subtract
                                                ).then_inc(pool_did, 1)
                    for u in SLOTS:
                        gp.wait_ge(dve_did, DV.done("in_apply", i, u))
                        gp.wait_ge(act_did, AC.before("relu", i, u))
                        nc.gpsimd.tensor_tensor(aff[u][:], nrm[u][:], each_tile(gamma), ALU.mult
                                                ).then_inc(pool_did, 1)
                    for u in SLOTS:
                        gp.wait_ge(pool_did, PO.done("gamma", i, u))
                        nc.gpsimd.tensor_tensor(aff[u][:], aff[u][:], each_tile(beta), ALU.add
                                                ).then_inc(pool_did, 1)

            @block.tensor
            def _(pe):
                pe.sem_inc(pe_did, PE.per_iteration)
                pe.wait_ge(p.weights, WEIGHTS)
                pe.wait_ge(setup_did, 2)
                nc.tensor.matmul(C[0][:, 8:9], wst[:], gate_skip[:], start=True, stop=True)
                nc.tensor.matmul(C[0][:, 9:10], bs_col[:], gate_skip[:], start=True, stop=True
                                 ).then_inc(setup_did, 1)
                pe.wait_ge(setup_did, 5)
                with pe.Fori(0, N_ITERS) as i:
                    for u in SLOTS:
                        pe.wait_ge(p.loaded[u], i * p.per_load + p.per_load)
                        pe.wait_ge(act_did, AC.before("xt", i, u))
                        p.turn(A[u], u)
                    for u in SLOTS:
                        pe.wait_ge(act_did, AC.done("xt", i, u))
                        pe.wait_ge(dve_did, DV.before("gap", i, u))
                        for j in range(4):
                            nc.tensor.matmul(B[u][:, j * D:(j + 1) * D], xt[u][:, j * D:(j + 1) * D], ws[:],
                                             start=True, stop=True)
                        for j in range(4):
                            last = nc.tensor.matmul(C[u][:, j:j + 1], xt[u][:, j * D:(j + 1) * D], gate_rows[:],
                                                    start=True, stop=True)
                        last.then_inc(pe_did, 1)

            @block.scalar
            def _(act):
                act.sem_inc(act_did, AC.per_iteration)
                act.wait_ge(setup_did, 5)
                with act.Fori(0, N_ITERS) as i:
                    for u in SLOTS:
                        act.wait_ge(pe_did, PE.done("turn", i, u))
                        nc.scalar.activation(xt[u][:], A[u][:], ACT.Copy).then_inc(act_did, 1)
                    for u in SLOTS:
                        act.wait_ge(dve_did, DV.done("z", i, u))
                        nc.scalar.activation(ez[u][:], z[u][:], ACT.Exp, bias=off[:], scale=-1.0
                                             ).then_inc(act_did, 1)
                    p.norm_std(act, i, DV, "in")
                    for u in SLOTS:
                        act.wait_ge(pool_did, PO.done("beta", i, u))
                        act.wait_ge(dve_did, DV.before("res", i, u))
                        nc.scalar.activation(pos[u][:], aff[u][:], ACT.Relu).then_inc(act_did, 1)
                    p.norm_std(act, i, DV, "out")

            @block.vector
            def _(dve):
                dve.wait_ge(p.weights, WEIGHTS)
                nc.vector.tensor_scalar(rest[:], alpha[:], -1.0, 1.0, ALU.mult, ALU.add).then_inc(setup_did, 1)
                nc.vector.tensor_copy(bs_col[:], bs_one[:].broadcast_to([D, 128]))
                nc.vector.tensor_tensor(gate_skip[:], wg[:, 0:1], wg[:, 2:3], ALU.add).then_inc(setup_did, 1)
                dve.wait_ge(setup_did, 3)
                nc.vector.tensor_copy(gate_rows[:], C[0][:, 8:9]).then_inc(setup_did, 1)
                nc.vector.scalar_tensor_tensor(out=off[:], in0=C[0][:, 9:10], scalar=-1.0, in1=bg[:],
                                               op0=ALU.mult, op1=ALU.subtract).then_inc(setup_did, 1)
                dve.sem_inc(dve_did, DV.per_iteration)
                with dve.Fori(0, N_ITERS) as i:
                    for u in SLOTS:
                        dve.wait_ge(p.loaded[u], i * p.per_load + p.per_load)
                        dve.wait_ge(pe_did, PE.done("skip", i, u))
                        dve.wait_ge(act_did, AC.before("exp", i, u))
                        nc.vector.tensor_tensor(z[u][:], C[u][:, 0:4], p.sums[u][:, :, D], ALU.add
                                                ).then_inc(dve_did, 1)
                    for u in SLOTS:
                        dve.wait_ge(pool_did, PO.done("less", i, u))
                        nc.vector.tensor_tensor(gap[u][:], tiles(B[u]), less[u][:], ALU.subtract
                                                ).then_inc(dve_did, 1)
                    for u in SLOTS:
                        dve.wait_ge(act_did, AC.done("exp", i, u))
                        nc.vector.tensor_scalar(ez1[u][:], ez[u][:], 1.0, None, ALU.add).then_inc(dve_did, 1)
                    for u in SLOTS:
                        dve.wait_ge(dve_did, DV.done("ez1", i, u))
                        nc.vector.reciprocal(g[u][:], ez1[u][:]).then_inc(dve_did, 1)
                    for u in SLOTS:
                        dve.wait_ge(dve_did, DV.done("g", i, u))
                        for j in range(4):
                            last = nc.vector.scalar_tensor_tensor(
                                out=mix[u][:, j, :], in0=gap[u][:, j, :], scalar=g[u][:, j:j + 1],
                                in1=p.sums[u][:, j, 0:D], op0=ALU.mult, op1=ALU.add)
                        last.then_inc(dve_did, 1)
                    p.norm_stats(dve, i, mix, DV, AC, "in", "mix")
                    p.norm_apply(dve, i, mix, nrm, DV, "in",
                                 lambda i, u: dve.wait_ge(pool_did, PO.before("gamma", i, u)))
                    for u in SLOTS:
                        dve.wait_ge(pool_did, PO.done("beta", i, u))
                        nc.vector.scalar_tensor_tensor(out=flat(res[u]), in0=flat(aff[u]), scalar=alpha[:],
                                                       in1=flat(p.rows[u]), op0=ALU.mult, op1=ALU.add
                                                       ).then_inc(dve_did, 1)
                    for u in SLOTS:
                        dve.wait_ge(act_did, AC.done("relu", i, u))
                        dve.wait_ge(dve_did, DV.done("leak", i, u))
                        nc.vector.scalar_tensor_tensor(out=flat(res[u]), in0=flat(pos[u]), scalar=rest[:],
                                                       in1=flat(res[u]), op0=ALU.mult, op1=ALU.add
                                                       ).then_inc(dve_did, 1)
                    p.norm_stats(dve, i, res, DV, AC, "out", "res")
                    p.norm_apply(dve, i, res, p.out, DV, "out",
                                 lambda i, u: dve.wait_ge(p.stored[u], i * 16 + 16))



def layer1_edges(nc, sems, keep, t, l, table):
    with ExitStack() as ctx:
        p = EdgePass(nc, sems, ctx, f"e1{l}", keep, table, t["agg_rows"], 2)
        w_dst, w_src, w2, w_agg = (p.sb(n, [D, D]) for n in ("w_dst", "w_src", "w2", "w_agg"))
        w_edge = p.sb("w_edge", [1, D])
        b1, b2 = p.sb("b1", [D, 1]), p.sb("b2", [D, 1])
        ones = p.sb("ones", [128, EC])
        weight = p.pair(p.sb, "weight", [1, EC])
        xs, xd, m1, m2, count, share, total, mean = (p.pair(p.sb, n, [D, EC]) for n in (
            "xs", "xd", "m1", "m2", "count", "share", "total", "mean"))
        A, B, C = (p.pair(p.bank, n) for n in "ABC")
        PE = Steps("turn", "m1", "m2", "rows")
        AC = Steps("xs", "m1", "m2", "rows")
        DV = Steps("flag", "xd", "count/0", "count/1", "share", "total/0", "total/1", "mean")
        pe_did, act_did, dve_did = p.pe_did, p.act_did, p.dve_did
        WEIGHTS = 16 * 7
        with nc.Block() as block:
            @block.sync
            def _(sp):
                for tile, dram in ((w_dst, t["L1_ew1"][l, 0:D, :]), (w_src, t["L1_ew1"][l, D:2 * D, :]),
                                   (w_edge, t["L1_ew1"][l, 2 * D:2 * D + 1, :]), (w2, t["L1_ew2"][l, :, :]),
                                   (w_agg, t["L1_nw1"][l, D:2 * D, :]), (b1, t["L1_eb1"][l, :, :]),
                                   (b2, t["L1_eb2"][l, :, :])):
                    sp.dma_start(tile[:], dram).then_inc(p.weights, 16)
                with sp.Fori(0, E_ITERS) as i:
                    for u in SLOTS:
                        sp.wait_ge(pe_did, PE.before("m1", i, u))
                        settled(sp, p.passed)
                        sp.wait_ge(dve_did, DV.before("flag", i, u))
                        p.stream(sp, i, u, t, [(weight[u][:], t["edge_weight_rows"], 1)])

            @block.gpsimd
            def _(gp):
                p.pool_program(gp, PE, AC)

            @block.tensor
            def _(pe):
                pe.sem_inc(pe_did, PE.per_iteration)
                pe.wait_ge(p.weights, WEIGHTS)
                with pe.Fori(0, E_ITERS) as i:
                    for u in SLOTS:
                        pe.wait_ge(p.gathered[u], i * 128 + 128)
                        pe.wait_ge(act_did, AC.before("rows", i, u))
                        p.turn(pe, i, u, (A[u], B[u]), PE)
                    for u in SLOTS:
                        pe.wait_ge(p.streamed[u], i * 48 + 48)
                        pe.wait_ge(act_did, AC.done("xs", i, u))
                        pe.wait_ge(dve_did, DV.done("xd", i, u))
                        nc.tensor.matmul(C[u][:, 0:EC], w_edge[:], weight[u][:], start=True, stop=False)
                        nc.tensor.matmul(C[u][:, 0:EC], w_src[:], xs[u][:], start=False, stop=False)
                        nc.tensor.matmul(C[u][:, 0:EC], w_dst[:], xd[u][:], start=False, stop=True
                                         ).then_inc(pe_did, 1)
                    for u in SLOTS:
                        pe.wait_ge(act_did, AC.done("m1", i, u))
                        nc.tensor.matmul(A[u][:, 0:EC], w2[:], m1[u][:], start=True, stop=True
                                         ).then_inc(pe_did, 1)
                    for u in SLOTS:
                        pe.wait_ge(dve_did, DV.done("mean", i, u))
                        for j in range(TILES):
                            last = nc.tensor.matmul(B[u][0:ET, j * D:(j + 1) * D], tile_of(mean[u], j), w_agg[:],
                                                    start=True, stop=True)
                        last.then_inc(pe_did, 1)

            @block.scalar
            def _(act):
                act.sem_inc(act_did, AC.per_iteration)
                act.wait_ge(p.weights, WEIGHTS)
                with act.Fori(0, E_ITERS) as i:
                    for u in SLOTS:
                        act.wait_ge(pe_did, PE.done("turn", i, u))
                        nc.scalar.activation(xs[u][:], A[u][:, 0:EC], ACT.Copy).then_inc(act_did, 1)
                    for u in SLOTS:
                        act.wait_ge(pe_did, PE.done("m1", i, u))
                        nc.scalar.activation(m1[u][:], C[u][:, 0:EC], ACT.Relu, bias=b1[:]).then_inc(act_did, 1)
                    for u in SLOTS:
                        act.wait_ge(pe_did, PE.done("m2", i, u))
                        act.wait_ge(dve_did, DV.before("total", i, u))
                        nc.scalar.activation(m2[u][:], A[u][:, 0:EC], ACT.Relu, bias=b2[:]).then_inc(act_did, 1)
                    for u in SLOTS:
                        act.wait_ge(pe_did, PE.done("rows", i, u))
                        act.wait_ge(p.scattered[u], i * 64 + 16)
                        nc.scalar.activation(p.out_rows[u][:, :, 0:D], tiles(B[u])[0:ET], ACT.Copy
                                             ).then_inc(act_did, 1)

            @block.vector
            def _(dve):
                for u in SLOTS:
                    nc.vector.memset(p.out_rows[u][:], 0.0)
                nc.vector.memset(ones[:], 1.0)
                nc.vector.memset(count[1][:], 0.0)
                nc.vector.memset(total[1][:], 0.0).then_inc(dve_did, DV.per_iteration)
                with dve.Fori(0, E_ITERS) as i:
                    for u in SLOTS:
                        dve.wait_ge(p.streamed[u], i * 48 + 48)
                        dve.wait_ge(dve_did, DV.before("total", i, u))
                        nc.vector.tensor_tensor(p.flag[u][:], p.dst[u][:], p.prev[u][:], ALU.is_equal
                                                ).then_inc(dve_did, 1)
                    for u in SLOTS:
                        dve.wait_ge(pe_did, PE.done("turn", i, u))
                        nc.vector.tensor_copy(xd[u][:], B[u][:, 0:EC]).then_inc(dve_did, 1)
                    for u in SLOTS:
                        dve.wait_ge(dve_did, DV.before("count", i, 1) if u == 0 else DV.done("count", i, 0))
                        dve.wait_ge(dve_did, DV.done("flag", i, u))
                        nc.vector.tensor_tensor_scan(count[u][:], p.flag[u][:], ones[:], count[1 - u][:, EC - 1:EC],
                                                     ALU.mult, ALU.add).then_inc(dve_did, 1)
                    for u in SLOTS:
                        dve.wait_ge(dve_did, DV.done("count", i, u))
                        nc.vector.reciprocal(share[u][:], count[u][:]).then_inc(dve_did, 1)
                    for u in SLOTS:
                        dve.wait_ge(dve_did, DV.before("total", i, 1) if u == 0 else DV.done("total", i, 0))
                        dve.wait_ge(act_did, AC.done("m2", i, u))
                        nc.vector.tensor_tensor_scan(total[u][:], p.flag[u][:], m2[u][:], total[1 - u][:, EC - 1:EC],
                                                     ALU.mult, ALU.add).then_inc(dve_did, 1)
                    for u in SLOTS:
                        dve.wait_ge(dve_did, DV.done("total", i, u))
                        dve.wait_ge(pe_did, PE.before("rows", i, u))
                        nc.vector.tensor_tensor(mean[u][:], total[u][:], share[u][:], ALU.mult
                                                ).then_inc(dve_did, 1)



def layer1_nodes(nc, sems, keep, t, l, source, target):
    final = l == 2
    with ExitStack() as ctx:
        p = NodePass(nc, sems, ctx, f"n1{l}", keep, source, t["agg_rows"], target, t["x1"] if final else None)
        ident = keep["ident"]
        w1, w2 = p.sb("w1", [D, D]), p.sb("w2", [D, D])
        b1 = p.sb("b1", [D, 1])
        b2, gamma, beta = (p.sb(n, [128, D]) for n in ("b2", "gamma", "beta"))
        xt, ht = p.pair(p.sb, "xt", [D, NC_]), p.pair(p.sb, "ht", [D, NC_])
        biased = p.pair(p.sb, "biased", [128, 4, D])
        A, B, C = (p.pair(p.bank, n) for n in "ABC")
        PE = Steps("turn", "hidden", "update")
        AC = Steps("xt", "hidden", "update", *(("in_std", "out_std") if final else ()))
        DV = Steps("biased", *((*norm_steps("in"), *norm_steps("out")) if final else ()))
        PO = Steps("gamma", "beta", "res")
        pe_did, act_did, dve_did, pool_did = p.pe_did, p.act_did, p.dve_did, p.pool_did
        if final:
            new, nrm, aff, res = (p.pair(p.sb, n, [128, 4, D]) for n in ("new", "nrm", "aff", "res"))
        else:
            new = p.out
        WEIGHTS = 16 * 6
        with nc.Block() as block:
            @block.sync
            def _(sp):
                for tile, dram in ((w1, t["L1_nw1"][l, 0:D, :]), (w2, t["L1_nw2"][l, :, :]),
                                   (b1, t["L1_nb1"][l, :, :]), (b2, four(t["L1_nb2"][l, :, :])),
                                   (gamma, four(t["L1_gamma"])), (beta, four(t["L1_beta"]))):
                    sp.dma_start(tile[:], dram).then_inc(p.weights, 16)

                def free(i, u):
                    sp.wait_ge(pe_did, PE.before("hidden", i, u))
                    settled(sp, p.passed)
                    if final:
                        sp.wait_ge(pool_did, PO.before("res", i, u))
                        settled(sp, p.passed)

                def filled(i, u):
                    if final:
                        sp.wait_ge(dve_did, DV.done("out_apply", i, u))
                    else:
                        sp.wait_ge(act_did, AC.done("update", i, u))

                p.sync_program(sp, free, filled)

            if final:
                @block.gpsimd
                def _(gp):
                    gp.sem_inc(pool_did, PO.per_iteration)
                    gp.wait_ge(p.weights, WEIGHTS)
                    with gp.Fori(0, N_ITERS) as i:
                        for u in SLOTS:
                            gp.wait_ge(dve_did, DV.done("in_apply", i, u))
                            nc.gpsimd.tensor_tensor(aff[u][:], nrm[u][:], each_tile(gamma), ALU.mult
                                                    ).then_inc(pool_did, 1)
                        for u in SLOTS:
                            gp.wait_ge(pool_did, PO.done("gamma", i, u))
                            nc.gpsimd.tensor_tensor(aff[u][:], aff[u][:], each_tile(beta), ALU.add
                                                    ).then_inc(pool_did, 1)
                        for u in SLOTS:
                            gp.wait_ge(pool_did, PO.done("beta", i, u))
                            gp.wait_ge(dve_did, DV.before("out_apply", i, u))
                            gp.wait_ge(p.loaded[u], i * p.per_load + p.per_load)
                            nc.gpsimd.tensor_tensor(res[u][:], aff[u][:], p.residual[u][:], ALU.add
                                                    ).then_inc(pool_did, 1)

            @block.tensor
            def _(pe):
                pe.sem_inc(pe_did, PE.per_iteration)
                pe.wait_ge(p.weights, WEIGHTS)
                with pe.Fori(0, N_ITERS) as i:
                    for u in SLOTS:
                        pe.wait_ge(p.loaded[u], i * p.per_load + p.per_load)
                        pe.wait_ge(act_did, AC.before("xt", i, u))
                        p.turn(A[u], u)
                    for u in SLOTS:
                        pe.wait_ge(act_did, AC.done("xt", i, u))
                        nc.tensor.matmul(B[u][:], w1[:], xt[u][:], start=True, stop=False)
                        for j in range(4):
                            last = nc.tensor.matmul(B[u][:, j * D:(j + 1) * D], p.sums[u][:, j, 0:D], ident[:],
                                                    start=False, stop=(j == 3))
                        last.then_inc(pe_did, 1)
                    for u in SLOTS:
                        pe.wait_ge(act_did, AC.done("hidden", i, u))
                        pe.wait_ge(dve_did, DV.before("biased", i, u))
                        for j in range(4):
                            last = nc.tensor.matmul(C[u][:, j * D:(j + 1) * D], ht[u][:, j * D:(j + 1) * D], w2[:],
                                                    start=True, stop=True)
                        last.then_inc(pe_did, 1)

            @block.scalar
            def _(act):
                act.sem_inc(act_did, AC.per_iteration)
                act.wait_ge(p.weights, WEIGHTS)
                with act.Fori(0, N_ITERS) as i:
                    for u in SLOTS:
                        act.wait_ge(pe_did, PE.done("turn", i, u))
                        nc.scalar.activation(xt[u][:], A[u][:], ACT.Copy).then_inc(act_did, 1)
                    for u in SLOTS:
                        act.wait_ge(pe_did, PE.done("hidden", i, u))
                        nc.scalar.activation(ht[u][:], B[u][:], ACT.Relu, bias=b1[:]).then_inc(act_did, 1)
                    for u in SLOTS:
                        act.wait_ge(dve_did, DV.done("biased", i, u))
                        if not final:
                            act.wait_ge(p.stored[u], i * 16 + 16)
                        nc.scalar.activation(new[u][:], biased[u][:], ACT.Relu).then_inc(act_did, 1)
                    if final:
                        p.norm_std(act, i, DV, "in")
                        p.norm_std(act, i, DV, "out")

            @block.vector
            def _(dve):
                dve.wait_ge(p.weights, WEIGHTS)
                dve.sem_inc(dve_did, DV.per_iteration)
                with dve.Fori(0, N_ITERS) as i:
                    for u in SLOTS:
                        dve.wait_ge(pe_did, PE.done("update", i, u))
                        dve.wait_ge(act_did, AC.before("update", i, u))
                        nc.vector.tensor_tensor(biased[u][:], tiles(C[u]), each_tile(b2), ALU.add
                                                ).then_inc(dve_did, 1)
                    if final:
                        for u in SLOTS:
                            dve.wait_ge(act_did, AC.done("update", i, u))
                        p.norm_stats(dve, i, new, DV, AC, "in", "biased")
                        p.norm_apply(dve, i, new, nrm, DV, "in",
                                     lambda i, u: dve.wait_ge(pool_did, PO.before("gamma", i, u)))
                        for u in SLOTS:
                            dve.wait_ge(pool_did, PO.done("res", i, u))
                        p.norm_stats(dve, i, res, DV, AC, "out", "in_apply")
                        p.norm_apply(dve, i, res, p.out, DV, "out",
                                     lambda i, u: dve.wait_ge(p.stored[u], i * 16 + 16))



def layer2_edges(nc, sems, keep, t):
    relations = t["L2_W"].shape[0]
    with ExitStack() as ctx:
        p = EdgePass(nc, sems, ctx, "e2", keep, t["x2"], t["agg_rows"], 1)
        ident = keep["ident"]
        w = p.sb("w", [D, relations, D])
        ones = p.sb("ones", [128, EC])
        kind = p.pair(p.sb, "kind", [128, EC], I32)
        xs, count, total = (p.pair(p.sb, n, [D, EC]) for n in ("xs", "count", "total"))
        of_kind = p.pair(p.sb, "of_kind", [D, relations, EC])
        A, B, C, DD = (p.pair(p.bank, n) for n in "ABCD")
        PE = Steps("turn", "messages", "rows")
        AC = Steps("xs", "rows")
        DV = Steps("flag", "of_kind", "count/0", "count/1", "total/0", "total/1")
        pe_did, act_did, dve_did = p.pe_did, p.act_did, p.dve_did
        with nc.Block() as block:
            @block.sync
            def _(sp):
                sp.dma_start(w[:], t["L2_W"].rearrange("r i o -> i r o")).then_inc(p.weights, 16)
                with sp.Fori(0, E_ITERS) as i:
                    for u in SLOTS:
                        sp.wait_ge(dve_did, DV.before("of_kind", i, u))
                        p.stream(sp, i, u, t, [(kind[u][:], t["type_rows"], 128)])

            @block.gpsimd
            def _(gp):
                p.pool_program(gp, PE, AC)

            @block.tensor
            def _(pe):
                pe.sem_inc(pe_did, PE.per_iteration)
                pe.wait_ge(p.weights, 16)
                with pe.Fori(0, E_ITERS) as i:
                    for u in SLOTS:
                        pe.wait_ge(p.gathered[u], i * 64 + 64)
                        pe.wait_ge(act_did, AC.before("xs", i, u))
                        p.turn(pe, i, u, (A[u],), PE)
                    for u in SLOTS:
                        pe.wait_ge(dve_did, DV.done("of_kind", i, u))
                        pe.wait_ge(dve_did, DV.before("total", i, u))
                        for r in range(relations):
                            last = nc.tensor.matmul(B[u][:, 0:EC], w[:, r, :], of_kind[u][:, r, :],
                                                    start=(r == 0), stop=(r == relations - 1))
                        last.then_inc(pe_did, 1)
                    for u in SLOTS:
                        pe.wait_ge(dve_did, DV.done("total", i, u))
                        pe.wait_ge(act_did, AC.before("rows", i, u))
                        for j in range(TILES):
                            nc.tensor.matmul(C[u][0:ET, j * D:(j + 1) * D], tile_of(total[u], j), ident[:],
                                             start=True, stop=True)
                        for j in range(TILES):
                            last = nc.tensor.matmul(DD[u][0:ET, j:j + 1], tile_of(count[u], j), ident[:, 0:1],
                                                    start=True, stop=True)
                        last.then_inc(pe_did, 1)

            @block.scalar
            def _(act):
                act.sem_inc(act_did, AC.per_iteration)
                with act.Fori(0, E_ITERS) as i:
                    for u in SLOTS:
                        act.wait_ge(pe_did, PE.done("turn", i, u))
                        act.wait_ge(dve_did, DV.before("of_kind", i, u))
                        nc.scalar.activation(xs[u][:], A[u][:, 0:EC], ACT.Copy).then_inc(act_did, 1)
                    for u in SLOTS:
                        act.wait_ge(pe_did, PE.done("rows", i, u))
                        act.wait_ge(p.scattered[u], i * 64 + 16)
                        nc.scalar.activation(p.out_rows[u][:, :, 0:D], tiles(C[u])[0:ET], ACT.Copy)
                        nc.scalar.activation(p.out_rows[u][:, :, D:D + 1],
                                             DD[u][0:ET, 0:TILES].rearrange("p (j a) -> p j a", a=1),
                                             ACT.Copy).then_inc(act_did, 1)

            @block.vector
            def _(dve):
                for u in SLOTS:
                    nc.vector.memset(p.out_rows[u][:], 0.0)
                nc.vector.memset(ones[:], 1.0)
                nc.vector.memset(count[1][:], 0.0)
                nc.vector.memset(total[1][:], 0.0).then_inc(dve_did, DV.per_iteration)
                with dve.Fori(0, E_ITERS) as i:
                    for u in SLOTS:
                        dve.wait_ge(p.streamed[u], i * 48 + 48)
                        dve.wait_ge(dve_did, DV.before("total", i, u))
                        nc.vector.tensor_tensor(p.flag[u][:], p.dst[u][:], p.prev[u][:], ALU.is_equal
                                                ).then_inc(dve_did, 1)
                    for u in SLOTS:
                        dve.wait_ge(act_did, AC.done("xs", i, u))
                        dve.wait_ge(pe_did, PE.before("messages", i, u))
                        for r in range(relations):
                            last = nc.vector.scalar_tensor_tensor(
                                out=of_kind[u][:, r, :], in0=kind[u][:], scalar=float(r), in1=xs[u][:],
                                op0=ALU.is_equal, op1=ALU.mult)
                        last.then_inc(dve_did, 1)
                    for u in SLOTS:
                        dve.wait_ge(dve_did, DV.before("count", i, 1) if u == 0 else DV.done("count", i, 0))
                        dve.wait_ge(dve_did, DV.done("flag", i, u))
                        dve.wait_ge(pe_did, PE.before("rows", i, u))
                        nc.vector.tensor_tensor_scan(count[u][:], p.flag[u][:], ones[:], count[1 - u][:, EC - 1:EC],
                                                     ALU.mult, ALU.add).then_inc(dve_did, 1)
                    for u in SLOTS:
                        dve.wait_ge(dve_did, DV.before("total", i, 1) if u == 0 else DV.done("total", i, 0))
                        dve.wait_ge(pe_did, PE.done("messages", i, u))
                        nc.vector.tensor_tensor_scan(total[u][:], p.flag[u][:], B[u][:, 0:EC],
                                                     total[1 - u][:, EC - 1:EC], ALU.mult, ALU.add
                                                     ).then_inc(dve_did, 1)



def layer2_nodes(nc, sems, keep, t):
    with ExitStack() as ctx:
        p = NodePass(nc, sems, ctx, "n2", keep, t["x2"], t["agg_rows"], t["x3"])
        w0 = p.sb("w0", [D, D])
        xt = p.pair(p.sb, "xt", [D, NC_])
        both, res = p.pair(p.sb, "both", [128, 4, D]), p.pair(p.sb, "res", [128, 4, D])
        deg, share = p.pair(p.sb, "deg", [128, 4]), p.pair(p.sb, "share", [128, 4])
        A, B = p.pair(p.bank, "A"), p.pair(p.bank, "B")
        PE = Steps("turn", "own")
        AC = Steps("xt", "out_std")
        DV = Steps("deg", "share", "both", "res", *norm_steps("out"))
        pe_did, act_did, dve_did = p.pe_did, p.act_did, p.dve_did
        with nc.Block() as block:
            @block.sync
            def _(sp):
                sp.dma_start(w0[:], t["L2_W0"]).then_inc(p.weights, 16)

                def free(i, u):
                    sp.wait_ge(dve_did, DV.before("res", i, u))
                    settled(sp, p.passed)
                    sp.wait_ge(pe_did, PE.before("turn", i, u))
                    settled(sp, p.passed)

                p.sync_program(sp, free, lambda i, u: sp.wait_ge(dve_did, DV.done("out_apply", i, u)))

            @block.tensor
            def _(pe):
                pe.sem_inc(pe_did, PE.per_iteration)
                pe.wait_ge(p.weights, 16)
                with pe.Fori(0, N_ITERS) as i:
                    for u in SLOTS:
                        pe.wait_ge(p.loaded[u], i * p.per_load + p.per_load)
                        pe.wait_ge(act_did, AC.before("xt", i, u))
                        p.turn(A[u], u)
                    for u in SLOTS:
                        pe.wait_ge(act_did, AC.done("xt", i, u))
                        pe.wait_ge(dve_did, DV.before("both", i, u))
                        for j in range(4):
                            last = nc.tensor.matmul(B[u][:, j * D:(j + 1) * D], xt[u][:, j * D:(j + 1) * D], w0[:],
                                                    start=True, stop=True)
                        last.then_inc(pe_did, 1)

            @block.scalar
            def _(act):
                act.sem_inc(act_did, AC.per_iteration)
                with act.Fori(0, N_ITERS) as i:
                    for u in SLOTS:
                        act.wait_ge(pe_did, PE.done("turn", i, u))
                        nc.scalar.activation(xt[u][:], A[u][:], ACT.Copy).then_inc(act_did, 1)
                    p.norm_std(act, i, DV, "out")

            @block.vector
            def _(dve):
                dve.sem_inc(dve_did, DV.per_iteration)
                with dve.Fori(0, N_ITERS) as i:
                    for u in SLOTS:
                        dve.wait_ge(p.loaded[u], i * p.per_load + p.per_load)
                        nc.vector.tensor_scalar(deg[u][:], p.sums[u][:, :, D], 1.0, None, ALU.max
                                                ).then_inc(dve_did, 1)
                    for u in SLOTS:
                        dve.wait_ge(dve_did, DV.done("deg", i, u))
                        nc.vector.reciprocal(share[u][:], deg[u][:]).then_inc(dve_did, 1)
                    for u in SLOTS:
                        dve.wait_ge(pe_did, PE.done("own", i, u))
                        nc.vector.tensor_tensor(both[u][:], tiles(B[u]), p.sums[u][:, :, 0:D], ALU.add
                                                ).then_inc(dve_did, 1)
                    for u in SLOTS:
                        dve.wait_ge(dve_did, DV.done("both", i, u))
                        for j in range(4):
                            last = nc.vector.scalar_tensor_tensor(
                                out=res[u][:, j, :], in0=both[u][:, j, :], scalar=share[u][:, j:j + 1],
                                in1=p.rows[u][:, j, :], op0=ALU.mult, op1=ALU.add)
                        last.then_inc(dve_did, 1)
                    p.norm_stats(dve, i, res, DV, AC, "out", "res")
                    p.norm_apply(dve, i, res, p.out, DV, "out",
                                 lambda i, u: dve.wait_ge(p.stored[u], i * 16 + 16))



def layer3_edges(nc, sems, keep, t):
    with ExitStack() as ctx:
        p = EdgePass(nc, sems, ctx, "e3", keep, t["x3"], t["agg_rows"], 2)
        w, att = p.sb("w", [D, H3, D]), p.sb("att", [D, 2, H3, D])
        weighed = p.sb("weighed", [D, 2, H3, D])
        to_logit = p.sb("to_logit", [D, 2, H3])
        own_logit = p.sb("own_logit", [D, H3])
        wq4 = p.sb("wq4", [D, H3, D])
        pick = p.sb("pick", [H3, H3, D])
        xs, xd, diff = (p.pair(p.sb, n, [D, EC]) for n in ("xs", "xd", "diff"))
        part, share = p.pair(p.sb, "part", [D, 2, EC]), p.pair(p.sb, "share", [D, 2, EC])
        total = p.pair(p.sb, "total", [D, H3, EC])
        pen, start = p.pair(p.sb, "pen", [H3, EC]), p.pair(p.sb, "start", [H3, EC])
        raw, leaky = p.pair(p.sb, "raw", [H3, 2, EC]), p.pair(p.sb, "leaky", [H3, 2, EC])
        top = p.pair(p.sb, "top", [H3, EC])
        m = p.pair(p.sb, "m", [H3, EC + 1])
        de, ce = p.pair(p.sb, "de", [H3, 3, EC]), p.pair(p.sb, "ce", [H3, 3, EC])
        den, rden = p.pair(p.sb, "den", [H3, EC]), p.pair(p.sb, "rden", [H3, EC])
        A, B, C, DD = (p.pair(p.bank, n) for n in "ABCD")
        heads = range(H3)
        PE = Steps("turn", "logits", *(f"{s}{h}" for h in heads for s in ("spread", "rows")))
        AC = Steps("xs", "raw", "exp", "rows")
        DV = Steps("flag", "pen", "xd", "diff", "leaky", "top", "carry/0", "max/0", "carry/1", "max/1",
                   "drop", "differences", "own", "add_own", "den", "rden",
                   *(f"{s}{h}" for h in heads for s in ("part", "total", "share")))
        pe_did, act_did, dve_did = p.pe_did, p.act_did, p.dve_did
        setup_did = p.sem("setup_did")
        WEIGHTS = 16 * 4
        with nc.Block() as block:
            @block.sync
            def _(sp):
                sp.dma_start(w[:], t["L3_W"].rearrange("i (h o) -> i h o", h=H3)).then_inc(p.weights, 16)
                sp.dma_start(att[:, 0, :, :].rearrange("p h o -> p (h o)"),
                             t["L3_att_src"].broadcast_to([D, H3 * D])).then_inc(p.weights, 16)
                sp.dma_start(att[:, 1, :, :].rearrange("p h o -> p (h o)"),
                             t["L3_att_dst"].broadcast_to([D, H3 * D])).then_inc(p.weights, 16)
                sp.dma_start(pick[:].rearrange("k h o -> k (h o)"), t["head_pick"]).then_inc(p.weights, 16)
                with sp.Fori(0, E_ITERS) as i:
                    for u in SLOTS:
                        sp.wait_ge(dve_did, DV.before("flag", i, u))
                        p.stream(sp, i, u, t)

            @block.gpsimd
            def _(gp):
                p.pool_program(gp, PE, AC)

            @block.tensor
            def _(pe):
                pe.sem_inc(pe_did, PE.per_iteration)
                pe.wait_ge(setup_did, 4)
                with pe.Fori(0, E_ITERS) as i:
                    for u in SLOTS:
                        pe.wait_ge(p.gathered[u], i * 128 + 128)
                        pe.wait_ge(act_did, AC.before("rows", i, u))
                        p.turn(pe, i, u, (A[u], B[u]), PE)
                    for u in SLOTS:
                        pe.wait_ge(act_did, AC.done("xs", i, u))
                        pe.wait_ge(dve_did, DV.done("xd", i, u))
                        nc.tensor.matmul(C[u][0:H3, 0:EC], to_logit[:, 0, :], xs[u][:], start=True, stop=False)
                        nc.tensor.matmul(C[u][0:H3, 0:EC], to_logit[:, 1, :], xd[u][:], start=False, stop=True)
                        nc.tensor.matmul(DD[u][0:H3, 0:EC], own_logit[:], xd[u][:], start=True, stop=True
                                         ).then_inc(pe_did, 1)
                    for h in heads:
                        for u in SLOTS:
                            if h == 0:
                                pe.wait_ge(dve_did, DV.done("rden", i, u))
                            else:
                                pe.wait_ge(dve_did, DV.done(f"share{h - 1}", i, u))
                            nc.tensor.matmul(B[u][:, 0:EC], pick[:, h, :], ce[u][:, 1, :], start=True, stop=True)
                            nc.tensor.matmul(C[u][:, 0:EC], pick[:, h, :], ce[u][:, 0, :], start=True, stop=True)
                            nc.tensor.matmul(DD[u][:, 0:EC], pick[:, h, :], rden[u][:], start=True, stop=True
                                             ).then_inc(pe_did, 1)
                        for u in SLOTS:
                            pe.wait_ge(dve_did, DV.done(f"share{h}", i, u))
                            for j in range(TILES):
                                last = nc.tensor.matmul(A[u][0:ET, j * D:(j + 1) * D],
                                                        share[u][:, h % 2, j * ET:(j + 1) * ET], wq4[:, h, :],
                                                        start=(h == 0 and j == 0), stop=(h == H3 - 1),
                                                        skip_group_check=True)
                            last.then_inc(pe_did, 1)

            @block.scalar
            def _(act):
                act.sem_inc(act_did, AC.per_iteration)
                with act.Fori(0, E_ITERS) as i:
                    for u in SLOTS:
                        act.wait_ge(pe_did, PE.done("turn", i, u))
                        act.wait_ge(dve_did, DV.before("diff", i, u))
                        nc.scalar.activation(xs[u][:], A[u][:, 0:EC], ACT.Copy).then_inc(act_did, 1)
                    for u in SLOTS:
                        act.wait_ge(pe_did, PE.done("logits", i, u))
                        act.wait_ge(dve_did, DV.before("leaky", i, u))
                        nc.scalar.activation(raw[u][:, 0, :], C[u][0:H3, 0:EC], ACT.Copy)
                        nc.scalar.activation(raw[u][:, 1, :], DD[u][0:H3, 0:EC], ACT.Copy).then_inc(act_did, 1)
                    for u in SLOTS:
                        act.wait_ge(dve_did, DV.done("differences", i, u))
                        act.wait_ge(pe_did, PE.before("spread3", i, u))
                        nc.scalar.activation(ce[u][:], de[u][:], ACT.Exp).then_inc(act_did, 1)
                    for u in SLOTS:
                        act.wait_ge(pe_did, PE.done("rows3", i, u))
                        act.wait_ge(p.scattered[u], i * 64 + 16)
                        nc.scalar.activation(p.out_rows[u][:, :, 0:D], tiles(A[u])[0:ET], ACT.Copy
                                             ).then_inc(act_did, 1)

            @block.vector
            def _(dve):
                for u in SLOTS:
                    nc.vector.memset(p.out_rows[u][:], 0.0)
                nc.vector.memset(m[1][:], 0.0)
                nc.vector.memset(den[1][:], 1.0)
                dve.wait_ge(p.weights, WEIGHTS)
                for s in range(2):
                    last = nc.vector.tensor_tensor(weighed[:, s, :, :], w[:], att[:, s, :, :], ALU.mult)
                last.then_inc(setup_did, 1)
                dve.wait_ge(setup_did, 1)
                nc.vector.tensor_reduce(to_logit[:].rearrange("p s h -> p (s h)"),
                                        weighed[:].rearrange("p s h o -> p (s h) o"), mybir.AxisListType.X, ALU.add
                                        ).then_inc(setup_did, 1)
                nc.vector.tensor_scalar(wq4[:], w[:], 1.0 / H3, None, ALU.mult).then_inc(setup_did, 1)
                dve.wait_ge(setup_did, 2)
                nc.vector.tensor_tensor(own_logit[:], to_logit[:, 0, :], to_logit[:, 1, :], ALU.add
                                        ).then_inc(setup_did, 1)
                nc.vector.memset(total[1][:], 0.0).then_inc(dve_did, DV.per_iteration)
                with dve.Fori(0, E_ITERS) as i:
                    for u in SLOTS:
                        dve.wait_ge(p.streamed[u], i * 32 + 32)
                        nc.vector.tensor_tensor(p.flag[u][:], p.dst[u][:], p.prev[u][:], ALU.is_equal
                                                ).then_inc(dve_did, 1)
                    for u in SLOTS:
                        dve.wait_ge(dve_did, DV.done("flag", i, u))
                        nc.vector.tensor_scalar(pen[u][:], p.flag[u][0:H3, :], FAR, -FAR, ALU.mult, ALU.add)
                        nc.vector.tensor_scalar(start[u][:], p.flag[u][0:H3, :], -1.0, 1.0, ALU.mult, ALU.add
                                                ).then_inc(dve_did, 1)
                    for u in SLOTS:
                        dve.wait_ge(pe_did, PE.done("turn", i, u))
                        nc.vector.tensor_copy(xd[u][:], B[u][:, 0:EC]).then_inc(dve_did, 1)
                    for u in SLOTS:
                        dve.wait_ge(act_did, AC.done("xs", i, u))
                        dve.wait_ge(dve_did, DV.done("xd", i, u))
                        nc.vector.tensor_tensor(diff[u][:], xs[u][:], xd[u][:], ALU.subtract).then_inc(dve_did, 1)
                    for u in SLOTS:
                        dve.wait_ge(act_did, AC.done("raw", i, u))
                        nc.vector.scalar_tensor_tensor(
                            out=leaky[u][:].rearrange("p a e -> p (a e)"), in0=raw[u][:].rearrange("p a e -> p (a e)"),
                            scalar=0.2, in1=raw[u][:].rearrange("p a e -> p (a e)"), op0=ALU.mult, op1=ALU.max
                        ).then_inc(dve_did, 1)
                    for u in SLOTS:
                        dve.wait_ge(dve_did, DV.done("leaky", i, u))
                        nc.vector.tensor_tensor(top[u][:], leaky[u][:, 0, :], leaky[u][:, 1, :], ALU.max
                                                ).then_inc(dve_did, 1)
                    for u in SLOTS:
                        dve.wait_ge(dve_did, DV.before("max", i, 1) if u == 0 else DV.done("max", i, 0))
                        nc.vector.tensor_copy(m[u][:, 0:1], m[1 - u][:, EC:EC + 1]).then_inc(dve_did, 1)
                        dve.wait_ge(dve_did, DV.done("carry", i, u))
                        nc.vector.tensor_tensor_scan(m[u][:, 1:EC + 1], pen[u][:], top[u][:], m[u][:, 0:1],
                                                     ALU.add, ALU.max).then_inc(dve_did, 1)
                    for u in SLOTS:
                        dve.wait_ge(dve_did, DV.done("max", i, u))
                        nc.vector.tensor_tensor(de[u][:, 0, :], m[u][:, 0:EC], m[u][:, 1:EC + 1], ALU.subtract
                                                ).then_inc(dve_did, 1)
                    for u in SLOTS:
                        dve.wait_ge(dve_did, DV.done("drop", i, u))
                        nc.vector.tensor_tensor(de[u][:, 0, :], de[u][:, 0, :], pen[u][:], ALU.add)
                        for s in range(2):
                            last = nc.vector.tensor_tensor(de[u][:, 1 + s, :], leaky[u][:, s, :],
                                                           m[u][:, 1:EC + 1], ALU.subtract)
                        last.then_inc(dve_did, 1)
                    for u in SLOTS:
                        dve.wait_ge(act_did, AC.done("exp", i, u))
                        nc.vector.tensor_tensor(start[u][:], start[u][:], ce[u][:, 2, :], ALU.mult
                                                ).then_inc(dve_did, 1)
                    for u in SLOTS:
                        dve.wait_ge(dve_did, DV.done("own", i, u))
                        nc.vector.tensor_tensor(top[u][:], start[u][:], ce[u][:, 1, :], ALU.add).then_inc(dve_did, 1)
                    for u in SLOTS:
                        dve.wait_ge(dve_did, DV.done("add_own", i, u))
                        dve.wait_ge(dve_did, DV.before("den", i, 1) if u == 0 else DV.done("den", i, 0))
                        nc.vector.tensor_tensor_scan(den[u][:], ce[u][:, 0, :], top[u][:],
                                                     den[1 - u][:, EC - 1:EC], ALU.mult, ALU.add
                                                     ).then_inc(dve_did, 1)
                    for u in SLOTS:
                        dve.wait_ge(dve_did, DV.done("den", i, u))
                        dve.wait_ge(pe_did, PE.before("spread3", i, u))
                        nc.vector.reciprocal(rden[u][:], den[u][:]).then_inc(dve_did, 1)
                    for h in heads:
                        for u in SLOTS:
                            dve.wait_ge(pe_did, PE.done(f"spread{h}", i, u))
                            nc.vector.tensor_tensor(part[u][:, h % 2, :], diff[u][:], B[u][:, 0:EC], ALU.mult
                                                    ).then_inc(dve_did, 1)
                        for u in SLOTS:
                            dve.wait_ge(dve_did, DV.done(f"part{h}", i, u))
                            dve.wait_ge(dve_did, DV.before(f"total{h}", i, 1) if u == 0
                                        else DV.done(f"total{h}", i, 0))
                            nc.vector.tensor_tensor_scan(total[u][:, h, :], C[u][:, 0:EC], part[u][:, h % 2, :],
                                                         total[1 - u][:, h, EC - 1:EC], ALU.mult, ALU.add
                                                         ).then_inc(dve_did, 1)
                        for u in SLOTS:
                            dve.wait_ge(dve_did, DV.done(f"total{h}", i, u))
                            if h < 2:
                                dve.wait_ge(pe_did, PE.before(f"rows{h + 2}", i, u))
                            else:
                                dve.wait_ge(pe_did, PE.done(f"rows{h - 2}", i, u))
                            nc.vector.tensor_tensor(share[u][:, h % 2, :], total[u][:, h, :], DD[u][:, 0:EC],
                                                    ALU.mult).then_inc(dve_did, 1)



def layer3_nodes(nc, sems, keep, t):
    with ExitStack() as ctx:
        p = NodePass(nc, sems, ctx, "n3", keep, t["x3"], t["agg_rows"], t["out"])
        w, two, wm = p.sb("w", [D, H3, D]), p.sb("two", [D, 2, D]), p.sb("wm", [D, D])
        bias = p.sb("bias", [128, D])
        xt = p.pair(p.sb, "xt", [D, NC_])
        more, both, res = (p.pair(p.sb, n, [128, 4, D]) for n in ("more", "both", "res"))
        A, B = p.pair(p.bank, "A"), p.pair(p.bank, "B")
        PE = Steps("turn", "own")
        AC = Steps("xt", "out_std")
        PO = Steps("more")
        DV = Steps("both", "res", *norm_steps("out"))
        pe_did, act_did, dve_did, pool_did = p.pe_did, p.act_did, p.dve_did, p.pool_did
        setup_did = p.sem("setup_did")
        with nc.Block() as block:
            @block.sync
            def _(sp):
                sp.dma_start(w[:], t["L3_W"].rearrange("i (h o) -> i h o", h=H3)).then_inc(p.weights, 16)
                sp.dma_start(bias[:], four(t["L3_bias"])).then_inc(p.weights, 16)

                def free(i, u):
                    sp.wait_ge(dve_did, DV.before("res", i, u))
                    settled(sp, p.passed)
                    sp.wait_ge(pe_did, PE.before("turn", i, u))
                    settled(sp, p.passed)
                    sp.wait_ge(pool_did, PO.before("more", i, u))
                    settled(sp, p.passed)

                p.sync_program(sp, free, lambda i, u: sp.wait_ge(dve_did, DV.done("out_apply", i, u)))

            @block.gpsimd
            def _(gp):
                gp.sem_inc(pool_did, PO.per_iteration)
                gp.wait_ge(p.weights, 32)
                with gp.Fori(0, N_ITERS) as i:
                    for u in SLOTS:
                        gp.wait_ge(p.loaded[u], i * p.per_load + p.per_load)
                        gp.wait_ge(dve_did, DV.before("both", i, u))
                        nc.gpsimd.tensor_tensor(more[u][:], p.sums[u][:, :, 0:D], each_tile(bias), ALU.add
                                                ).then_inc(pool_did, 1)

            @block.tensor
            def _(pe):
                pe.sem_inc(pe_did, PE.per_iteration)
                pe.wait_ge(setup_did, 3)
                with pe.Fori(0, N_ITERS) as i:
                    for u in SLOTS:
                        pe.wait_ge(p.loaded[u], i * p.per_load + p.per_load)
                        pe.wait_ge(act_did, AC.before("xt", i, u))
                        p.turn(A[u], u)
                    for u in SLOTS:
                        pe.wait_ge(act_did, AC.done("xt", i, u))
                        pe.wait_ge(dve_did, DV.before("both", i, u))
                        for j in range(4):
                            last = nc.tensor.matmul(B[u][:, j * D:(j + 1) * D], xt[u][:, j * D:(j + 1) * D], wm[:],
                                                    start=True, stop=True)
                        last.then_inc(pe_did, 1)

            @block.scalar
            def _(act):
                act.sem_inc(act_did, AC.per_iteration)
                with act.Fori(0, N_ITERS) as i:
                    for u in SLOTS:
                        act.wait_ge(pe_did, PE.done("turn", i, u))
                        nc.scalar.activation(xt[u][:], A[u][:], ACT.Copy).then_inc(act_did, 1)
                    p.norm_std(act, i, DV, "out")

            @block.vector
            def _(dve):
                dve.wait_ge(p.weights, 32)
                nc.vector.tensor_tensor(two[:], w[:, 0:2, :], w[:, 2:4, :], ALU.add).then_inc(setup_did, 1)
                dve.wait_ge(setup_did, 1)
                nc.vector.tensor_tensor(wm[:], two[:, 0, :], two[:, 1, :], ALU.add).then_inc(setup_did, 1)
                dve.wait_ge(setup_did, 2)
                nc.vector.tensor_scalar(wm[:], wm[:], 1.0 / H3, None, ALU.mult).then_inc(setup_did, 1)
                dve.sem_inc(dve_did, DV.per_iteration)
                with dve.Fori(0, N_ITERS) as i:
                    for u in SLOTS:
                        dve.wait_ge(pe_did, PE.done("own", i, u))
                        dve.wait_ge(pool_did, PO.done("more", i, u))
                        nc.vector.tensor_tensor(both[u][:], tiles(B[u]), more[u][:], ALU.add).then_inc(dve_did, 1)
                    for u in SLOTS:
                        dve.wait_ge(dve_did, DV.done("both", i, u))
                        nc.vector.scalar_tensor_tensor(out=flat(res[u]), in0=flat(both[u]), scalar=0.0,
                                                       in1=flat(p.rows[u]), op0=ALU.max, op1=ALU.add
                                                       ).then_inc(dve_did, 1)
                    p.norm_stats(dve, i, res, DV, AC, "out", "res")
                    p.norm_apply(dve, i, res, p.out, DV, "out",
                                 lambda i, u: dve.wait_ge(p.stored[u], i * 16 + 16))



def resident(nc, ctx):
    return {
        "gather_index": ctx.enter_context(nc.sbuf_tensor("gather_index", [ET, E // EC, 2 * TILES], I32)),
        "scatter_index": ctx.enter_context(nc.sbuf_tensor("scatter_index", [ET, E // EC, TILES], I32)),
        "ident": ctx.enter_context(nc.sbuf_tensor("ident", [128, 128], F32)),
    }


def scratch(nc):
    made = {n: nc.dram_tensor(n, [N, D], F32, kind="Internal").ap() for n in ("x1", "h1", "h2", "x2", "x3")}
    made["agg_rows"] = nc.dram_tensor("agg_rows", [N, ROW], F32, kind="Internal").ap()
    return made


def four_graph_layers(nc, t):
    with ExitStack() as sems, ExitStack() as ctx:
        keep = resident(nc, ctx)
        keep["small"] = t["ident"][0:16, 0:16]
        t = {**t, **scratch(nc)}
        setup_pass(nc, sems, keep, t)
        layer0_edges(nc, sems, keep, t)
        layer0_nodes(nc, sems, keep, t)
        states = ["x1", "h1", "h2", "x2"]
        for l in range(3):
            layer1_edges(nc, sems, keep, t, l, t[states[l]])
            layer1_nodes(nc, sems, keep, t, l, t[states[l]], t[states[l + 1]])
        layer2_edges(nc, sems, keep, t)
        layer2_nodes(nc, sems, keep, t)
        layer3_edges(nc, sems, keep, t)
        layer3_nodes(nc, sems, keep, t)


def laid_out(inputs):
    import numpy as np

    a = {n: np.asarray(v) for n, v in inputs.items()}
    dst = a["dst"]
    edge = np.full(1, -1, dst.dtype)
    tiles = lambda v: np.ascontiguousarray(v.reshape(E // ET, ET).T)
    chunks = lambda v: np.ascontiguousarray(v.reshape(E // EC, EC))
    of_head = (np.arange(D)[:, None] // (D // H0) == np.arange(H0)[None, :]).astype(np.float32)
    out = {
        "x": a["x"],
        "src_tiles": tiles(a["src"]), "dst_tiles": tiles(dst),
        "next_tiles": tiles(np.concatenate([dst[1:], edge])),
        "dst_rows": chunks(dst), "prev_rows": chunks(np.concatenate([edge, dst[:-1]])),
        "type_rows": chunks(a["edge_type_8"]), "edge_weight_rows": chunks(a["edge_weight"]),
        "ident": np.eye(128, dtype=np.float32),
        "head_mask": of_head / np.sqrt(np.float32(D // H0)),
        "head_spread": np.ascontiguousarray(of_head.T),
        "head_pick": np.ascontiguousarray(np.repeat(np.eye(H3, dtype=np.float32), D, axis=1)),
        "L0_Wg": np.ascontiguousarray(a["L0_gnn_Wg"].reshape(3, D).T),
        "L0_Ws_turned": np.ascontiguousarray(a["L0_gnn_Ws"].T),
        "L0_alpha": a["L0_gnn_alpha"].reshape(1, 1), "L0_bg": a["L0_gnn_bg"].reshape(1, 1),
        "L0_bs_row": a["L0_gnn_bs"].reshape(1, D),
        "L1_ew1": a["L1_gnn_ew1"], "L1_ew2": a["L1_gnn_ew2"],
        "L1_nw1": a["L1_gnn_nw1"], "L1_nw2": a["L1_gnn_nw2"],
        "L1_eb1": a["L1_gnn_eb1"].reshape(3, D, 1), "L1_eb2": a["L1_gnn_eb2"].reshape(3, D, 1),
        "L1_nb1": a["L1_gnn_nb1"].reshape(3, D, 1), "L1_nb2": a["L1_gnn_nb2"].reshape(3, 1, D),
        "L2_W": a["L2_gnn_W"], "L2_W0": a["L2_gnn_W0"],
        "L3_W": a["L3_gnn_W"], "L3_bias": a["L3_gnn_bias"].reshape(1, D),
        "L3_att_src": a["L3_gnn_att_src"].reshape(1, H3 * D),
        "L3_att_dst": a["L3_gnn_att_dst"].reshape(1, H3 * D),
    }
    for n in ("Wq", "Wk", "Wv", "Ws"):
        out[f"L0_{n}"] = a[f"L0_gnn_{n}"]
    for n in ("bq", "bk", "bv", "bs"):
        out[f"L0_{n}"] = a[f"L0_gnn_{n}"].reshape(D, 1)
    for layer in ("L0", "L1"):
        for n in ("gamma", "beta"):
            out[f"{layer}_{n}"] = a[f"{layer}_gnn_{n}"].reshape(1, D)
    return out


def kernel(**inputs):
    import numpy as _np
    import concourse.bacc as _bacc
    from concourse import mybir as _mybir
    from concourse.bass_utils import run_bass_kernel_spmd as _run

    nc = _bacc.Bacc("TRN2", target_bir_lowering=False, num_devices=1)
    arrays = {f"in_{n}": _np.ascontiguousarray(a) for n, a in laid_out(inputs).items()}
    t = {n[3:]: nc.dram_tensor(n, a.shape, _mybir.dt.from_np(a.dtype), kind="ExternalInput").ap()
         for n, a in arrays.items()}
    t["out"] = nc.dram_tensor("out", [N, D], F32, kind="ExternalOutput").ap()
    four_graph_layers(nc, t)
    r = _run(nc, [arrays], core_ids=[0])
    return r.results[0]["out"]
```

```python
from contextlib import ExitStack

import concourse.bass as bass
from concourse import mybir

ALU = mybir.AluOpType
ACT = mybir.ActivationFunctionType
F32 = mybir.dt.float32
I32 = mybir.dt.int32
BF16 = mybir.dt.bfloat16

D = 128
N = 50000
E = 25000
ET, TILES = 125, 4
EC = ET * TILES
E_ITERS = E // (2 * EC)
NC_ = 4 * D
N_ITERS = -(-N // (4 * NC_))
WALK = (N - N_ITERS * NC_) // 3
ROW = 132
H0, H3 = 4, 4
EPS = 1e-5
FAR = 1.0e30
SKIP = 65536
EDGE_SLOTS = (0, 1)
NODE_SLOTS = (0, 1, 2, 3)


class Steps:

    def __init__(self, *names, slots):
        self.order = []
        for name in names:
            step, _, slot = name.partition("/")
            self.order += [(step, int(slot))] if slot else [(step, u) for u in slots]
        self.per_iteration = len(self.order)

    def before(self, name, i, u):
        return i * self.per_iteration + (self.order.index((name, u)) + 1)

    def done(self, name, i, u):
        return i * self.per_iteration + (self.per_iteration + self.order.index((name, u)) + 1)


class Pass:

    slots = EDGE_SLOTS

    def __init__(self, nc, sems, ctx, tag):
        self.nc, self.sems, self.ctx, self.tag = nc, sems, ctx, tag

    def sb(self, name, shape, dt=F32):
        return self.ctx.enter_context(self.nc.sbuf_tensor(f"{self.tag}_{name}", shape, dt))

    def bank(self, name):
        return self.ctx.enter_context(self.nc.psum_tensor(f"{self.tag}_{name}", [128, 512], F32))

    def sem(self, name):
        return self.sems.enter_context(self.nc.semaphore(f"{self.tag}_{name}"))

    def pair(self, make, name, *args):
        return [make(f"{name}{u}", *args) for u in self.slots]


def settled(eng, passed):
    eng.sem_inc(passed, 1)


def as_rows(dram, i, u, width=D):
    start = u * WALK + i * NC_
    return dram[bass.ds(start, NC_), :].rearrange("(p j) d -> p j d", j=4)



def setup_pass(nc, sems, keep, t):
    with ExitStack() as ctx:
        p = Pass(nc, sems, ctx, "setup")
        gidx, sidx, ident = keep["gather_index"], keep["scatter_index"], keep["ident"]
        src = p.sb("src", [ET, E // ET], I32)
        dst = p.sb("dst", [ET, E // ET], I32)
        nxt = p.sb("nxt", [ET, E // ET], I32)
        same = p.sb("same", [ET, E // ET], I32)
        zeros = p.sb("zeros", [96, N * ROW // 96 // 10])
        loaded, zeroed, did, filled = (p.sem(s) for s in ("loaded", "zeroed", "did", "filled"))
        chunked = lambda a: a[:].rearrange("p (c j) -> p c j", j=TILES)
        with nc.Block() as block:
            @block.sync
            def _(sp):
                for tile, dram in ((src, t["src_tiles"]), (dst, t["dst_tiles"]), (nxt, t["next_tiles"]),
                                   (ident, t["ident"])):
                    sp.dma_start(tile[:], dram).then_inc(loaded, 16)
                sp.wait_ge(zeroed, 1)
                flat = t["agg_rows"].rearrange("n r -> (n r)").rearrange("(k p f) -> k p f", k=10, p=96)
                for k in range(10):
                    sp.dma_start(flat[k], zeros[:]).then_inc(filled, 16)
                sp.wait_ge(filled, 160)

            @block.vector
            def _(dve):
                nc.vector.memset(zeros[:], 0.0).then_inc(zeroed, 1)
                dve.wait_ge(loaded, 64)
                nc.vector.tensor_copy(gidx[:, :, 0:TILES], chunked(src))
                nc.vector.tensor_copy(gidx[:, :, TILES:2 * TILES], chunked(dst))
                nc.vector.tensor_tensor(same[:], dst[:], nxt[:], ALU.is_equal).then_inc(did, 1)
                dve.wait_ge(did, 1)
                nc.vector.scalar_tensor_tensor(out=sidx[:], in0=chunked(same), scalar=float(SKIP),
                                               in1=chunked(dst), op0=ALU.mult, op1=ALU.add).then_inc(did, 1)



class EdgePass(Pass):
    def __init__(self, nc, sems, ctx, tag, keep, table, agg, ends):
        super().__init__(nc, sems, ctx, tag)
        self.keep, self.table, self.agg, self.ends = keep, table, agg, ends
        self.end_rows = self.pair(self.sb, "rows_of_ends", [ET, 4 * ends, D])
        self.gi = self.pair(self.sb, "gi", [ET, 4 * ends], I32)
        self.si = self.pair(self.sb, "si", [ET, TILES], I32)
        self.out_rows = self.pair(self.sb, "out_rows", [ET, TILES, ROW])
        self.dst = self.pair(self.sb, "dst", [128, EC], I32)
        self.prev = self.pair(self.sb, "prev", [128, EC], I32)
        self.flag = self.pair(self.sb, "same_as_before", [128, EC])
        self.gathered = self.pair(self.sem, "gathered")
        self.scattered = self.pair(self.sem, "scattered")
        self.streamed = self.pair(self.sem, "streamed")
        self.weights = self.sem("weights")
        self.passed = keep["passed"]
        self.first = self.pair(self.sb, "first", [16, 16])
        self.pe_did, self.act_did, self.dve_did, self.pool_did = (
            self.sem(s) for s in ("pe_did", "act_did", "dve_did", "pool_did"))

    def pool_program(self, gp, PE, ACTS, ahead=1, E_=E_ITERS):
        nc = self.nc
        gidx, sidx = self.keep["gather_index"], self.keep["scatter_index"]
        k = 4 * self.ends
        def after_waits():
            settled(gp, self.passed)

        def gathers(i, u, copies, first=False):
            if not first:
                gp.wait_ge(self.pe_did, PE.before("turn", i, u))
                gp.wait_ge(self.gathered[u], 16 * k * i)
                after_waits()
            nc.gpsimd.tensor_copy(self.gi[u][:], gidx[:, bass.ds(2 * i + u, 1), 0:k].rearrange(
                "p a j -> p (a j)")).then_inc(self.pool_did, 1)
            gp.wait_ge(self.pool_did, copies + (u + 1))
            after_waits()
            for j in range(k):
                gp.indirect_dma_start(self.end_rows[u][:, j, :], None, self.table,
                                      bass.IndirectOffsetOnAxis(ap=self.gi[u][:, j:j + 1], axis=0)
                                      ).then_inc(self.gathered[u], 16)

        def scatters(i, u, copies):
            gp.wait_ge(self.scattered[u], i * (16 * TILES) + 16)
            gp.wait_ge(self.act_did, ACTS.done("rows", i, u))
            after_waits()
            nc.gpsimd.tensor_copy(self.si[u][:], sidx[:, bass.ds(2 * i + u, 1), :].rearrange(
                "p a j -> p (a j)")).then_inc(self.pool_did, 1)
            gp.wait_ge(self.pool_did, copies + (u + 1))
            after_waits()
            for j in range(TILES):
                gp.indirect_dma_start(self.agg, bass.IndirectOffsetOnAxis(ap=self.si[u][:, j:j + 1], axis=0),
                                      self.out_rows[u][:, j, :], None, bounds_check=N - 1,
                                      oob_is_err=False).then_inc(self.scattered[u], 16)

        for u in EDGE_SLOTS:
            gp.dma_start(self.first[u][:], self.keep["small"]).then_inc(self.scattered[u], 16)
            gathers(0, u, 0, first=True)
        for i in range(1, ahead):
            for u in EDGE_SLOTS:
                gathers(i, u, 2 * i)
        with gp.Fori(0, E_ - ahead) as i:
            for u in EDGE_SLOTS:
                gathers(i + ahead, u, i * 4 + 2 * ahead)
            for u in EDGE_SLOTS:
                scatters(i, u, i * 4 + (2 * ahead + 2))
        for i in range(E_ - ahead, E_):
            for u in EDGE_SLOTS:
                scatters(i, u, 2 * E_ + 2 * i)
        for u in EDGE_SLOTS:
            gp.wait_ge(self.scattered[u], 16 * TILES * E_ + 16)
        after_waits()

    def stream(self, sp, i, u, t, extra=()):
        at = 2 * i + u
        settled(sp, self.passed)
        sp.dma_start(self.dst[u][:], t["dst_rows"][bass.ds(at, 1), :].broadcast_to([128, EC])
                     ).then_inc(self.streamed[u], 16)
        sp.dma_start(self.prev[u][:], t["prev_rows"][bass.ds(at, 1), :].broadcast_to([128, EC])
                     ).then_inc(self.streamed[u], 16)
        for tile, rows, lanes in extra:
            sp.dma_start(tile, rows[bass.ds(at, 1), :].broadcast_to([lanes, EC])
                         ).then_inc(self.streamed[u], 16)

    def turn(self, pe, i, u, banks, PE):
        for end in range(self.ends):
            for j in range(TILES):
                last = self.nc.tensor.transpose(banks[end][:, j * ET:(j + 1) * ET],
                                                self.end_rows[u][:, end * TILES + j, :],
                                                self.keep["ident"][0:ET, 0:ET])
        last.then_inc(self.pe_did, 1)


def tile_of(a, j):
    return a[:, j * ET:(j + 1) * ET]



def layer0_edges(nc, sems, keep, t):
    with ExitStack() as ctx:
        p = EdgePass(nc, sems, ctx, "e0", keep, t["x"], t["agg_rows"], 2)
        ident = keep["ident"]
        wq, wk, wv = (p.sb(n, [D, D]) for n in ("wq", "wk", "wv"))
        bq, bk, bv = (p.sb(n, [D, 1]) for n in ("bq", "bk", "bv"))
        heads = p.sb("heads", [D, H0])
        spread = p.sb("spread", [H0, D])
        wg = p.sb("wg", [D, 3])
        gate_agg = p.sb("gate_agg", [D, 1])
        xs, xd, qs, pr, vb, wv_ = (p.pair(p.sb, n, [D, EC]) for n in ("xs", "xd", "qs", "pr", "vb", "wv_"))
        num, agg = p.pair(p.sb, "num", [D, EC]), p.pair(p.sb, "agg", [D, EC])
        pen = p.pair(p.sb, "pen", [H0, EC])
        m = p.pair(p.sb, "m", [H0, EC + 1])
        de, ce = p.pair(p.sb, "de", [H0, 2, EC]), p.pair(p.sb, "ce", [H0, 2, EC])
        den, rden = p.pair(p.sb, "den", [H0, EC]), p.pair(p.sb, "rden", [H0, EC])
        A, B, C, DD = (p.pair(p.bank, n) for n in "ABCD")
        PE = Steps("turn", "qkv", "logits", "spread_ce", "spread_den", "rows", slots=EDGE_SLOTS)
        AC = Steps("xs", "q", "v", "exp", "rows", slots=EDGE_SLOTS)
        DV = Steps("flag", "pen", "xd", "product", "carry/0", "max/0", "carry/1", "max/1", "drop", "differences", "den", "rden",
                   "weighted", "num", "agg", slots=EDGE_SLOTS)
        pe_did, act_did, dve_did, streamed = p.pe_did, p.act_did, p.dve_did, p.streamed
        WEIGHTS = 16 * 9
        with nc.Block() as block:
            @block.sync
            def _(sp):
                for tile, dram in ((wq, t["L0_Wq"]), (wk, t["L0_Wk"]), (wv, t["L0_Wv"]), (bq, t["L0_bq"]),
                                   (bk, t["L0_bk"]), (bv, t["L0_bv"]), (heads, t["head_mask"]),
                                   (spread, t["head_spread"]), (wg, t["L0_Wg"])):
                    sp.dma_start(tile[:], dram).then_inc(p.weights, 16)
                with sp.Fori(0, E_ITERS) as i:
                    for u in EDGE_SLOTS:
                        sp.wait_ge(dve_did, DV.before("flag", i, u))
                        p.stream(sp, i, u, t)

            @block.gpsimd
            def _(gp):
                p.pool_program(gp, PE, AC, ahead=2)

            @block.tensor
            def _(pe):
                pe.sem_inc(pe_did, PE.per_iteration)
                pe.wait_ge(p.weights, WEIGHTS)
                with pe.Fori(0, E_ITERS) as i:
                    for u in EDGE_SLOTS:
                        pe.wait_ge(p.gathered[u], i * 128 + 128)
                        pe.wait_ge(act_did, AC.before("rows", i, u))
                        p.turn(pe, i, u, (A[u], B[u]), PE)
                    for u in EDGE_SLOTS:
                        pe.wait_ge(act_did, AC.done("xs", i, u))
                        pe.wait_ge(dve_did, DV.done("xd", i, u))
                        nc.tensor.matmul(C[u][:, 0:EC], wq[:], xs[u][:], start=True, stop=True)
                        nc.tensor.matmul(DD[u][:, 0:EC], wk[:], xd[u][:], start=True, stop=True)
                        nc.tensor.matmul(A[u][:, 0:EC], wv[:], xs[u][:], start=True, stop=True).then_inc(pe_did, 1)
                    for u in EDGE_SLOTS:
                        pe.wait_ge(dve_did, DV.done("product", i, u))
                        nc.tensor.matmul(B[u][0:H0, 0:EC], heads[:], pr[u][:], start=True, stop=True
                                         ).then_inc(pe_did, 1)
                    for u in EDGE_SLOTS:
                        pe.wait_ge(act_did, AC.done("exp", i, u))
                        nc.tensor.matmul(C[u][:, 0:EC], spread[:], ce[u][:, 0, :], start=True, stop=True)
                        nc.tensor.matmul(DD[u][:, 0:EC], spread[:], ce[u][:, 1, :], start=True, stop=True
                                         ).then_inc(pe_did, 1)
                    for u in EDGE_SLOTS:
                        pe.wait_ge(dve_did, DV.done("rden", i, u))
                        nc.tensor.matmul(B[u][:, 0:EC], spread[:], rden[u][:], start=True, stop=True
                                         ).then_inc(pe_did, 1)
                    for u in EDGE_SLOTS:
                        pe.wait_ge(dve_did, DV.done("agg", i, u))
                        for j in range(TILES):
                            nc.tensor.matmul(A[u][0:ET, j * D:(j + 1) * D], tile_of(agg[u], j), ident[:],
                                             start=True, stop=True)
                        for j in range(TILES):
                            last = nc.tensor.matmul(B[u][0:ET, j:j + 1], tile_of(agg[u], j), gate_agg[:],
                                                    start=True, stop=True)
                        last.then_inc(pe_did, 1)

            @block.scalar
            def _(act):
                act.sem_inc(act_did, AC.per_iteration)
                act.wait_ge(p.weights, WEIGHTS)
                with act.Fori(0, E_ITERS) as i:
                    for u in EDGE_SLOTS:
                        act.wait_ge(pe_did, PE.done("turn", i, u))
                        nc.scalar.activation(xs[u][:], A[u][:, 0:EC], ACT.Copy).then_inc(act_did, 1)
                    for u in EDGE_SLOTS:
                        act.wait_ge(pe_did, PE.done("qkv", i, u))
                        act.wait_ge(dve_did, DV.before("product", i, u))
                        nc.scalar.activation(qs[u][:], C[u][:, 0:EC], ACT.Identity, bias=bq[:]).then_inc(act_did, 1)
                    for u in EDGE_SLOTS:
                        act.wait_ge(dve_did, DV.before("weighted", i, u))
                        nc.scalar.activation(vb[u][:], A[u][:, 0:EC], ACT.Identity, bias=bv[:]).then_inc(act_did, 1)
                    for u in EDGE_SLOTS:
                        act.wait_ge(dve_did, DV.done("differences", i, u))
                        act.wait_ge(pe_did, PE.before("spread_ce", i, u))
                        nc.scalar.activation(ce[u][:], de[u][:], ACT.Exp).then_inc(act_did, 1)
                    for u in EDGE_SLOTS:
                        act.wait_ge(pe_did, PE.done("rows", i, u))
                        act.wait_ge(p.scattered[u], i * 64 + 16)
                        nc.scalar.activation(p.out_rows[u][:, :, 0:D],
                                             A[u][0:ET, :].rearrange("p (j d) -> p j d", d=D), ACT.Copy)
                        nc.scalar.activation(p.out_rows[u][:, :, D:D + 1],
                                             B[u][0:ET, 0:TILES].rearrange("p (j a) -> p j a", a=1),
                                             ACT.Copy).then_inc(act_did, 1)

            @block.vector
            def _(dve):
                for u in EDGE_SLOTS:
                    nc.vector.memset(p.out_rows[u][:], 0.0)
                nc.vector.memset(m[1][:], 0.0)
                nc.vector.memset(den[1][:], 1.0)
                dve.wait_ge(p.weights, WEIGHTS)
                nc.vector.tensor_tensor(gate_agg[:], wg[:, 1:2], wg[:, 2:3], ALU.subtract)
                nc.vector.memset(num[1][:], 0.0).then_inc(dve_did, DV.per_iteration)
                with dve.Fori(0, E_ITERS) as i:
                    for u in EDGE_SLOTS:
                        dve.wait_ge(streamed[u], i * 32 + 32)
                        nc.vector.tensor_tensor(p.flag[u][:], p.dst[u][:], p.prev[u][:], ALU.is_equal
                                                ).then_inc(dve_did, 1)
                    for u in EDGE_SLOTS:
                        dve.wait_ge(dve_did, DV.done("flag", i, u))
                        nc.vector.tensor_scalar(pen[u][:], p.flag[u][0:H0, :], FAR, -FAR, ALU.mult, ALU.add
                                                ).then_inc(dve_did, 1)
                    for u in EDGE_SLOTS:
                        dve.wait_ge(pe_did, PE.done("turn", i, u))
                        nc.vector.tensor_copy(xd[u][:], B[u][:, 0:EC]).then_inc(dve_did, 1)
                    for u in EDGE_SLOTS:
                        dve.wait_ge(act_did, AC.done("q", i, u))
                        nc.vector.scalar_tensor_tensor(out=pr[u][:], in0=DD[u][:, 0:EC], scalar=bk[:],
                                                       in1=qs[u][:], op0=ALU.add, op1=ALU.mult
                                                       ).then_inc(dve_did, 1)
                    for u in EDGE_SLOTS:
                        dve.wait_ge(dve_did, DV.before("max", i, 1) if u == 0 else DV.done("max", i, 0))
                        nc.vector.tensor_copy(m[u][:, 0:1], m[1 - u][:, EC:EC + 1]).then_inc(dve_did, 1)
                        dve.wait_ge(pe_did, PE.done("logits", i, u))
                        dve.wait_ge(dve_did, DV.done("carry", i, u))
                        nc.vector.tensor_tensor_scan(m[u][:, 1:EC + 1], pen[u][:], B[u][0:H0, 0:EC], m[u][:, 0:1],
                                                     ALU.add, ALU.max).then_inc(dve_did, 1)
                    for u in EDGE_SLOTS:
                        dve.wait_ge(dve_did, DV.done("max", i, u))
                        nc.vector.tensor_tensor(de[u][:, 0, :], m[u][:, 0:EC], m[u][:, 1:EC + 1], ALU.subtract
                                                ).then_inc(dve_did, 1)
                    for u in EDGE_SLOTS:
                        dve.wait_ge(dve_did, DV.done("drop", i, u))
                        nc.vector.tensor_tensor(de[u][:, 0, :], de[u][:, 0, :], pen[u][:], ALU.add)
                        nc.vector.tensor_tensor(de[u][:, 1, :], B[u][0:H0, 0:EC], m[u][:, 1:EC + 1], ALU.subtract
                                                ).then_inc(dve_did, 1)
                    for u in EDGE_SLOTS:
                        dve.wait_ge(act_did, AC.done("exp", i, u))
                        dve.wait_ge(dve_did, DV.before("den", i, 1) if u == 0 else DV.done("den", i, 0))
                        nc.vector.tensor_tensor_scan(den[u][:], ce[u][:, 0, :], ce[u][:, 1, :],
                                                     den[1 - u][:, EC - 1:EC], ALU.mult, ALU.add
                                                     ).then_inc(dve_did, 1)
                    for u in EDGE_SLOTS:
                        dve.wait_ge(dve_did, DV.done("den", i, u))
                        dve.wait_ge(pe_did, PE.before("spread_den", i, u))
                        nc.vector.reciprocal(rden[u][:], den[u][:]).then_inc(dve_did, 1)
                    for u in EDGE_SLOTS:
                        dve.wait_ge(pe_did, PE.done("spread_ce", i, u))
                        dve.wait_ge(act_did, AC.done("v", i, u))
                        nc.vector.tensor_tensor(wv_[u][:], vb[u][:], DD[u][:, 0:EC], ALU.mult
                                                ).then_inc(dve_did, 1)
                    for u in EDGE_SLOTS:
                        dve.wait_ge(dve_did, DV.done("weighted", i, u))
                        dve.wait_ge(dve_did, DV.before("num", i, 1) if u == 0 else DV.done("num", i, 0))
                        nc.vector.tensor_tensor_scan(num[u][:], C[u][:, 0:EC], wv_[u][:], num[1 - u][:, EC - 1:EC],
                                                     ALU.mult, ALU.add).then_inc(dve_did, 1)
                    for u in EDGE_SLOTS:
                        dve.wait_ge(dve_did, DV.done("num", i, u))
                        dve.wait_ge(pe_did, PE.done("spread_den", i, u))
                        nc.vector.tensor_tensor(agg[u][:], num[u][:], B[u][:, 0:EC], ALU.mult).then_inc(dve_did, 1)



class NodePass(Pass):

    slots = NODE_SLOTS

    def __init__(self, nc, sems, ctx, tag, keep, dram_in, dram_agg, dram_out, dram_residual=None):
        super().__init__(nc, sems, ctx, tag)
        self.keep, self.dram_in, self.dram_agg, self.dram_out = keep, dram_in, dram_agg, dram_out
        self.dram_residual = dram_residual
        self.rows = self.pair(self.sb, "rows", [128, 4, D])
        self.sums = self.pair(self.sb, "sums", [128, 4, ROW])
        if dram_residual is not None:
            self.residual = self.pair(self.sb, "residual", [128, 4, D])
        self.out = self.pair(self.sb, "out", [128, 4, D])
        self.loaded = self.pair(self.sem, "loaded")
        self.stored = self.pair(self.sem, "stored")
        self.per_load = 16 * (2 if dram_residual is None else 3)
        self.weights = self.sem("weights")
        self.passed = keep["passed"]
        self.first = self.pair(self.sb, "first", [16, 16])
        self.pe_did, self.act_did, self.dve_did, self.pool_did = (
            self.sem(s) for s in ("pe_did", "act_did", "dve_did", "pool_did"))
        self.stats = self.pair(self.sb, "stats", [128, 4, 6])
        self.moments = self.pair(self.sb, "moments", [128, 4, 2])
        self.var = self.pair(self.sb, "var", [128, 4])
        self.std = self.pair(self.sb, "std", [128, 4])
        self.rstd = self.pair(self.sb, "rstd", [128, 4])

    def sync_program(self, sp, free, filled):
        def load(i, u, first=False):
            if not first:
                free(i, u)
            sp.dma_start(self.rows[u][:], as_rows(self.dram_in, i, u)).then_inc(self.loaded[u], 16)
            sp.dma_start(self.sums[u][:], as_rows(self.dram_agg, i, u)).then_inc(self.loaded[u], 16)
            if self.dram_residual is not None:
                sp.dma_start(self.residual[u][:], as_rows(self.dram_residual, i, u)
                             ).then_inc(self.loaded[u], 16)

        def store(i, u):
            filled(i, u)
            settled(sp, self.passed)
            sp.dma_start(as_rows(self.dram_out, i, u), self.out[u][:]).then_inc(self.stored[u], 16)

        for u in NODE_SLOTS:
            sp.dma_start(self.first[u][:], self.keep["small"]).then_inc(self.stored[u], 16)
            load(0, u, first=True)
        with sp.Fori(0, N_ITERS - 1) as i:
            for u in NODE_SLOTS:
                load(i + 1, u)
            for u in NODE_SLOTS:
                store(i, u)
        for u in NODE_SLOTS:
            store(N_ITERS - 1, u)
        for u in NODE_SLOTS:
            sp.wait_ge(self.stored[u], 16 * N_ITERS + 16)

    def turn(self, bank, u):
        for j in range(4):
            last = self.nc.tensor.transpose(bank[:, j * D:(j + 1) * D], self.rows[u][:, j, :],
                                            self.keep["ident"][:])
        last.then_inc(self.pe_did, 1)


    def norm_stats(self, dve, i, x, V, A, k, ready):
        nc = self.nc
        for u in NODE_SLOTS:
            ready(i, u)
            for j in range(4):
                last = nc.vector.bn_stats(self.stats[u][:, j, :], x[u][:, j, :])
            last.then_inc(self.dve_did, 1)
        for u in NODE_SLOTS:
            dve.wait_ge(self.dve_did, V.done(f"{k}_stats", i, u))
            settled(dve, self.passed)
            for j in range(4):
                last = nc.vector.bn_aggr(self.moments[u][:, j, :], self.stats[u][:, j, :])
            last.then_inc(self.dve_did, 1)
        for u in NODE_SLOTS:
            dve.wait_ge(self.dve_did, V.done(f"{k}_moments", i, u))
            nc.vector.tensor_scalar(self.var[u][:], self.moments[u][:, :, 1], EPS, None, ALU.add
                                    ).then_inc(self.dve_did, 1)
        for u in NODE_SLOTS:
            dve.wait_ge(self.act_did, A.done(f"{k}_std", i, u))
            nc.vector.reciprocal(self.rstd[u][:], self.std[u][:]).then_inc(self.dve_did, 1)

    def norm_std(self, act, i, V, k):
        for u in NODE_SLOTS:
            act.wait_ge(self.dve_did, V.done(f"{k}_var", i, u))
            self.nc.scalar.activation(self.std[u][:], self.var[u][:], ACT.Sqrt).then_inc(self.act_did, 1)

    def norm_apply(self, dve, i, x, y, V, k, wait=None):
        for u in NODE_SLOTS:
            dve.wait_ge(self.dve_did, V.done(f"{k}_rstd", i, u))
            if wait:
                wait(i, u)
            for j in range(4):
                last = self.nc.vector.tensor_scalar(y[u][:, j, :], x[u][:, j, :], self.moments[u][:, j, 0:1],
                                                    self.rstd[u][:, j:j + 1], ALU.subtract, ALU.mult)
            last.then_inc(self.dve_did, 1)


def norm_steps(k):
    return f"{k}_stats", f"{k}_moments", f"{k}_var", f"{k}_rstd", f"{k}_apply"


def four(row):
    return row.broadcast_to([128, D])


def each_tile(a):
    return a[:].rearrange("p (a d) -> p a d", a=1).broadcast_to([128, 4, D])


def flat(a):
    return a[:].rearrange("p j d -> p (j d)")


def tiles(bank):
    return bank[:].rearrange("p (j d) -> p j d", d=D)



def layer0_nodes(nc, sems, keep, t):
    with ExitStack() as ctx:
        p = NodePass(nc, sems, ctx, "n0", keep, t["x"], t["agg_rows"], t["x1"])
        ws, wst = p.sb("ws", [D, D]), p.sb("wst", [D, D])
        wg = p.sb("wg", [D, 3])
        bs_one, bs_col = p.sb("bs_one", [D, 1]), p.sb("bs_col", [D, 128])
        bs, gamma, beta = (p.sb(n, [128, D]) for n in ("bs", "gamma", "beta"))
        alpha, bg, rest = (p.sb(n, [128, 1]) for n in ("alpha", "bg", "rest"))
        gate_skip, gate_rows, off = p.sb("gate_skip", [D, 1]), p.sb("gate_rows", [D, 1]), p.sb("off", [128, 1])
        xt = p.pair(p.sb, "xt", [D, NC_])
        less, gap, mix, nrm, aff, pos, res = (p.pair(p.sb, n, [128, 4, D]) for n in (
            "less", "gap", "mix", "nrm", "aff", "pos", "res"))
        z, ez, ez1, g = (p.pair(p.sb, n, [128, 4]) for n in ("z", "ez", "ez1", "g"))
        A, B = p.pair(p.bank, "A"), p.pair(p.bank, "B")
        setup_did = p.sem("setup_did")
        PE = Steps("turn", "skip", slots=NODE_SLOTS)
        AC = Steps("xt", "exp", "in_std", "relu", "out_std", slots=NODE_SLOTS)
        DV = Steps("z", "gap", "ez1", "g", "mix", *norm_steps("in"), "leak", "res", *norm_steps("out"), slots=NODE_SLOTS)
        PO = Steps("less", "gamma", "beta", slots=NODE_SLOTS)
        pe_did, act_did, dve_did, pool_did = p.pe_did, p.act_did, p.dve_did, p.pool_did
        WEIGHTS = 16 * 9
        with nc.Block() as block:
            @block.sync
            def _(sp):
                for tile, dram in ((ws[:], t["L0_Ws"]), (wst[:], t["L0_Ws_turned"]), (wg[:], t["L0_Wg"]),
                                   (bs_one[:], t["L0_bs"]),
                                   (bs[:], four(t["L0_bs_row"])), (gamma[:], four(t["L0_gamma"])),
                                   (beta[:], four(t["L0_beta"])), (alpha[:], t["L0_alpha"].broadcast_to([128, 1])),
                                   (bg[:], t["L0_bg"].broadcast_to([128, 1]))):
                    sp.dma_start(tile, dram).then_inc(p.weights, 16)

                def free(i, u):
                    sp.wait_ge(dve_did, DV.before("leak", i, u))
                    settled(sp, p.passed)
                    sp.wait_ge(pe_did, PE.before("turn", i, u))
                    settled(sp, p.passed)
                    sp.wait_ge(pool_did, PO.before("less", i, u))
                    settled(sp, p.passed)

                p.sync_program(sp, free, lambda i, u: sp.wait_ge(dve_did, DV.done("out_apply", i, u)))

            @block.gpsimd
            def _(gp):
                gp.sem_inc(pool_did, PO.per_iteration)
                gp.wait_ge(p.weights, WEIGHTS)
                with gp.Fori(0, N_ITERS) as i:
                    for u in NODE_SLOTS:
                        gp.wait_ge(p.loaded[u], i * p.per_load + p.per_load)
                        gp.wait_ge(dve_did, DV.before("gap", i, u))
                        nc.gpsimd.tensor_tensor(less[u][:], p.sums[u][:, :, 0:D], each_tile(bs), ALU.subtract
                                                ).then_inc(pool_did, 1)
                    for u in NODE_SLOTS:
                        gp.wait_ge(dve_did, DV.done("in_apply", i, u))
                        gp.wait_ge(act_did, AC.before("relu", i, u))
                        nc.gpsimd.tensor_tensor(aff[u][:], nrm[u][:], each_tile(gamma), ALU.mult
                                                ).then_inc(pool_did, 1)
                    for u in NODE_SLOTS:
                        gp.wait_ge(pool_did, PO.done("gamma", i, u))
                        nc.gpsimd.tensor_tensor(aff[u][:], aff[u][:], each_tile(beta), ALU.add
                                                ).then_inc(pool_did, 1)

            @block.tensor
            def _(pe):
                pe.sem_inc(pe_did, PE.per_iteration)
                pe.wait_ge(p.weights, WEIGHTS)
                pe.wait_ge(setup_did, 2)
                nc.tensor.matmul(A[0][:, 8:9], wst[:], gate_skip[:], start=True, stop=True)
                nc.tensor.matmul(A[0][:, 9:10], bs_col[:], gate_skip[:], start=True, stop=True
                                 ).then_inc(setup_did, 1)
                pe.wait_ge(setup_did, 5)
                with pe.Fori(0, N_ITERS) as i:
                    for u in NODE_SLOTS:
                        pe.wait_ge(p.loaded[u], i * p.per_load + p.per_load)
                        pe.wait_ge(dve_did, DV.before("z", i, u))
                        p.turn(A[u], u)
                    for u in NODE_SLOTS:
                        pe.wait_ge(act_did, AC.done("xt", i, u))
                        pe.wait_ge(dve_did, DV.before("gap", i, u))
                        for j in range(4):
                            nc.tensor.matmul(B[u][:, j * D:(j + 1) * D], xt[u][:, j * D:(j + 1) * D], ws[:],
                                             start=True, stop=True)
                        for j in range(4):
                            last = nc.tensor.matmul(A[u][:, j:j + 1], xt[u][:, j * D:(j + 1) * D], gate_rows[:],
                                                    start=True, stop=True)
                        last.then_inc(pe_did, 1)

            @block.scalar
            def _(act):
                act.sem_inc(act_did, AC.per_iteration)
                act.wait_ge(setup_did, 5)
                with act.Fori(0, N_ITERS) as i:
                    for u in NODE_SLOTS:
                        act.wait_ge(pe_did, PE.done("turn", i, u))
                        nc.scalar.activation(xt[u][:], A[u][:], ACT.Copy).then_inc(act_did, 1)
                    for u in NODE_SLOTS:
                        act.wait_ge(dve_did, DV.done("z", i, u))
                        nc.scalar.activation(ez[u][:], z[u][:], ACT.Exp, bias=off[:], scale=-1.0
                                             ).then_inc(act_did, 1)
                    p.norm_std(act, i, DV, "in")
                    for u in NODE_SLOTS:
                        act.wait_ge(pool_did, PO.done("beta", i, u))
                        act.wait_ge(dve_did, DV.before("res", i, u))
                        nc.scalar.activation(pos[u][:], aff[u][:], ACT.Relu).then_inc(act_did, 1)
                    p.norm_std(act, i, DV, "out")

            @block.vector
            def _(dve):
                dve.wait_ge(p.weights, WEIGHTS)
                nc.vector.tensor_scalar(rest[:], alpha[:], -1.0, 1.0, ALU.mult, ALU.add).then_inc(setup_did, 1)
                nc.vector.tensor_copy(bs_col[:], bs_one[:].broadcast_to([D, 128]))
                nc.vector.tensor_tensor(gate_skip[:], wg[:, 0:1], wg[:, 2:3], ALU.add).then_inc(setup_did, 1)
                dve.wait_ge(setup_did, 3)
                nc.vector.tensor_copy(gate_rows[:], A[0][:, 8:9]).then_inc(setup_did, 1)
                nc.vector.scalar_tensor_tensor(out=off[:], in0=A[0][:, 9:10], scalar=-1.0, in1=bg[:],
                                               op0=ALU.mult, op1=ALU.subtract).then_inc(setup_did, 1)
                dve.sem_inc(dve_did, DV.per_iteration)
                with dve.Fori(0, N_ITERS) as i:
                    for u in NODE_SLOTS:
                        dve.wait_ge(p.loaded[u], i * p.per_load + p.per_load)
                        dve.wait_ge(pe_did, PE.done("skip", i, u))
                        dve.wait_ge(act_did, AC.before("exp", i, u))
                        nc.vector.tensor_tensor(z[u][:], A[u][:, 0:4], p.sums[u][:, :, D], ALU.add
                                                ).then_inc(dve_did, 1)
                    for u in NODE_SLOTS:
                        dve.wait_ge(pool_did, PO.done("less", i, u))
                        nc.vector.tensor_tensor(gap[u][:], tiles(B[u]), less[u][:], ALU.subtract
                                                ).then_inc(dve_did, 1)
                    for u in NODE_SLOTS:
                        dve.wait_ge(act_did, AC.done("exp", i, u))
                        nc.vector.tensor_scalar(ez1[u][:], ez[u][:], 1.0, None, ALU.add).then_inc(dve_did, 1)
                    for u in NODE_SLOTS:
                        dve.wait_ge(dve_did, DV.done("ez1", i, u))
                        nc.vector.reciprocal(g[u][:], ez1[u][:]).then_inc(dve_did, 1)
                    for u in NODE_SLOTS:
                        dve.wait_ge(dve_did, DV.done("g", i, u))
                        for j in range(4):
                            last = nc.vector.scalar_tensor_tensor(
                                out=mix[u][:, j, :], in0=gap[u][:, j, :], scalar=g[u][:, j:j + 1],
                                in1=p.sums[u][:, j, 0:D], op0=ALU.mult, op1=ALU.add)
                        last.then_inc(dve_did, 1)
                    p.norm_stats(dve, i, mix, DV, AC, "in",
                                 lambda i, u: dve.wait_ge(dve_did, DV.done("mix", i, u)))
                    p.norm_apply(dve, i, mix, nrm, DV, "in",
                                 lambda i, u: dve.wait_ge(pool_did, PO.before("gamma", i, u)))
                    for u in NODE_SLOTS:
                        dve.wait_ge(pool_did, PO.done("beta", i, u))
                        nc.vector.scalar_tensor_tensor(out=flat(res[u]), in0=flat(aff[u]), scalar=alpha[:],
                                                       in1=flat(p.rows[u]), op0=ALU.mult, op1=ALU.add
                                                       ).then_inc(dve_did, 1)
                    for u in NODE_SLOTS:
                        dve.wait_ge(act_did, AC.done("relu", i, u))
                        dve.wait_ge(dve_did, DV.done("leak", i, u))
                        nc.vector.scalar_tensor_tensor(out=flat(res[u]), in0=flat(pos[u]), scalar=rest[:],
                                                       in1=flat(res[u]), op0=ALU.mult, op1=ALU.add
                                                       ).then_inc(dve_did, 1)
                    p.norm_stats(dve, i, res, DV, AC, "out",
                                 lambda i, u: dve.wait_ge(dve_did, DV.done("res", i, u)))
                    p.norm_apply(dve, i, res, p.out, DV, "out",
                                 lambda i, u: dve.wait_ge(p.stored[u], i * 16 + 16))



def layer1_edges(nc, sems, keep, t, l, table):
    with ExitStack() as ctx:
        p = EdgePass(nc, sems, ctx, f"e1{l}", keep, table, t["agg_rows"], 2)
        w_dst, w_src, w2, w_agg = (p.sb(n, [D, D]) for n in ("w_dst", "w_src", "w2", "w_agg"))
        w_edge = p.sb("w_edge", [1, D])
        b1, b2 = p.sb("b1", [D, 1]), p.sb("b2", [D, 1])
        ones = p.sb("ones", [128, EC])
        weight = p.pair(p.sb, "weight", [1, EC])
        xs, xd, m1, m2, count, share, total, mean = (p.pair(p.sb, n, [D, EC]) for n in (
            "xs", "xd", "m1", "m2", "count", "share", "total", "mean"))
        A, B, C = (p.pair(p.bank, n) for n in "ABC")
        PE = Steps("turn", "m1", "m2", "rows", slots=EDGE_SLOTS)
        AC = Steps("xs", "m1", "m2", "rows", slots=EDGE_SLOTS)
        DV = Steps("flag", "xd", "count/0", "count/1", "share", "total/0", "total/1", "mean", slots=EDGE_SLOTS)
        pe_did, act_did, dve_did = p.pe_did, p.act_did, p.dve_did
        WEIGHTS = 16 * 7
        with nc.Block() as block:
            @block.sync
            def _(sp):
                for tile, dram in ((w_dst, t["L1_ew1"][l, 0:D, :]), (w_src, t["L1_ew1"][l, D:2 * D, :]),
                                   (w_edge, t["L1_ew1"][l, 2 * D:2 * D + 1, :]), (w2, t["L1_ew2"][l, :, :]),
                                   (w_agg, t["L1_nw1"][l, D:2 * D, :]), (b1, t["L1_eb1"][l, :, :]),
                                   (b2, t["L1_eb2"][l, :, :])):
                    sp.dma_start(tile[:], dram).then_inc(p.weights, 16)
                with sp.Fori(0, E_ITERS) as i:
                    for u in EDGE_SLOTS:
                        sp.wait_ge(pe_did, PE.before("m1", i, u))
                        settled(sp, p.passed)
                        sp.wait_ge(dve_did, DV.before("flag", i, u))
                        p.stream(sp, i, u, t, [(weight[u][:], t["edge_weight_rows"], 1)])

            @block.gpsimd
            def _(gp):
                p.pool_program(gp, PE, AC, ahead=2)

            @block.tensor
            def _(pe):
                pe.sem_inc(pe_did, PE.per_iteration)
                pe.wait_ge(p.weights, WEIGHTS)
                with pe.Fori(0, E_ITERS) as i:
                    for u in EDGE_SLOTS:
                        pe.wait_ge(p.gathered[u], i * 128 + 128)
                        pe.wait_ge(act_did, AC.before("rows", i, u))
                        p.turn(pe, i, u, (A[u], B[u]), PE)
                    for u in EDGE_SLOTS:
                        pe.wait_ge(p.streamed[u], i * 48 + 48)
                        pe.wait_ge(act_did, AC.done("xs", i, u))
                        pe.wait_ge(dve_did, DV.done("xd", i, u))
                        nc.tensor.matmul(C[u][:, 0:EC], w_edge[:], weight[u][:], start=True, stop=False)
                        nc.tensor.matmul(C[u][:, 0:EC], w_src[:], xs[u][:], start=False, stop=False)
                        nc.tensor.matmul(C[u][:, 0:EC], w_dst[:], xd[u][:], start=False, stop=True
                                         ).then_inc(pe_did, 1)
                    for u in EDGE_SLOTS:
                        pe.wait_ge(act_did, AC.done("m1", i, u))
                        nc.tensor.matmul(A[u][:, 0:EC], w2[:], m1[u][:], start=True, stop=True
                                         ).then_inc(pe_did, 1)
                    for u in EDGE_SLOTS:
                        pe.wait_ge(dve_did, DV.done("mean", i, u))
                        for j in range(TILES):
                            last = nc.tensor.matmul(B[u][0:ET, j * D:(j + 1) * D], tile_of(mean[u], j), w_agg[:],
                                                    start=True, stop=True)
                        last.then_inc(pe_did, 1)

            @block.scalar
            def _(act):
                act.sem_inc(act_did, AC.per_iteration)
                act.wait_ge(p.weights, WEIGHTS)
                with act.Fori(0, E_ITERS) as i:
                    for u in EDGE_SLOTS:
                        act.wait_ge(pe_did, PE.done("turn", i, u))
                        nc.scalar.activation(xs[u][:], A[u][:, 0:EC], ACT.Copy).then_inc(act_did, 1)
                    for u in EDGE_SLOTS:
                        act.wait_ge(pe_did, PE.done("m1", i, u))
                        nc.scalar.activation(m1[u][:], C[u][:, 0:EC], ACT.Relu, bias=b1[:]).then_inc(act_did, 1)
                    for u in EDGE_SLOTS:
                        act.wait_ge(pe_did, PE.done("m2", i, u))
                        act.wait_ge(dve_did, DV.before("total", i, u))
                        nc.scalar.activation(m2[u][:], A[u][:, 0:EC], ACT.Relu, bias=b2[:]).then_inc(act_did, 1)
                    for u in EDGE_SLOTS:
                        act.wait_ge(pe_did, PE.done("rows", i, u))
                        act.wait_ge(p.scattered[u], i * 64 + 16)
                        nc.scalar.activation(p.out_rows[u][:, :, 0:D], tiles(B[u])[0:ET], ACT.Copy
                                             ).then_inc(act_did, 1)

            @block.vector
            def _(dve):
                for u in EDGE_SLOTS:
                    nc.vector.memset(p.out_rows[u][:], 0.0)
                nc.vector.memset(ones[:], 1.0)
                nc.vector.memset(count[1][:], 0.0)
                nc.vector.memset(total[1][:], 0.0).then_inc(dve_did, DV.per_iteration)
                with dve.Fori(0, E_ITERS) as i:
                    for u in EDGE_SLOTS:
                        dve.wait_ge(p.streamed[u], i * 48 + 48)
                        dve.wait_ge(dve_did, DV.before("total", i, u))
                        nc.vector.tensor_tensor(p.flag[u][:], p.dst[u][:], p.prev[u][:], ALU.is_equal
                                                ).then_inc(dve_did, 1)
                    for u in EDGE_SLOTS:
                        dve.wait_ge(pe_did, PE.done("turn", i, u))
                        nc.vector.tensor_copy(xd[u][:], B[u][:, 0:EC]).then_inc(dve_did, 1)
                    for u in EDGE_SLOTS:
                        dve.wait_ge(dve_did, DV.before("count", i, 1) if u == 0 else DV.done("count", i, 0))
                        dve.wait_ge(dve_did, DV.done("flag", i, u))
                        nc.vector.tensor_tensor_scan(count[u][:], p.flag[u][:], ones[:], count[1 - u][:, EC - 1:EC],
                                                     ALU.mult, ALU.add).then_inc(dve_did, 1)
                    for u in EDGE_SLOTS:
                        dve.wait_ge(dve_did, DV.done("count", i, u))
                        nc.vector.reciprocal(share[u][:], count[u][:]).then_inc(dve_did, 1)
                    for u in EDGE_SLOTS:
                        dve.wait_ge(dve_did, DV.before("total", i, 1) if u == 0 else DV.done("total", i, 0))
                        dve.wait_ge(act_did, AC.done("m2", i, u))
                        nc.vector.tensor_tensor_scan(total[u][:], p.flag[u][:], m2[u][:], total[1 - u][:, EC - 1:EC],
                                                     ALU.mult, ALU.add).then_inc(dve_did, 1)
                    for u in EDGE_SLOTS:
                        dve.wait_ge(dve_did, DV.done("total", i, u))
                        dve.wait_ge(pe_did, PE.before("rows", i, u))
                        nc.vector.tensor_tensor(mean[u][:], total[u][:], share[u][:], ALU.mult
                                                ).then_inc(dve_did, 1)



def layer1_nodes(nc, sems, keep, t, l, source, target):
    final = l == 2
    with ExitStack() as ctx:
        p = NodePass(nc, sems, ctx, f"n1{l}", keep, source, t["agg_rows"], target, t["x1"] if final else None)
        ident = keep["ident"]
        w1, w2 = p.sb("w1", [D, D]), p.sb("w2", [D, D])
        b1 = p.sb("b1", [D, 1])
        b2, gamma, beta = (p.sb(n, [128, D]) for n in ("b2", "gamma", "beta"))
        xt, ht = p.pair(p.sb, "xt", [D, NC_]), p.pair(p.sb, "ht", [D, NC_])
        biased = p.pair(p.sb, "biased", [128, 4, D])
        A, B = p.pair(p.bank, "A"), p.pair(p.bank, "B")
        PE = Steps("turn", "hidden", "update", slots=NODE_SLOTS)
        AC = Steps("xt", "hidden", "update", *(("in_std", "out_std") if final else ()), slots=NODE_SLOTS)
        DV = Steps("biased", *((*norm_steps("in"), *norm_steps("out")) if final else ()), slots=NODE_SLOTS)
        PO = Steps("gamma", "beta", "res", slots=NODE_SLOTS)
        pe_did, act_did, dve_did, pool_did = p.pe_did, p.act_did, p.dve_did, p.pool_did
        if final:
            new, nrm, aff, res = (p.pair(p.sb, n, [128, 4, D]) for n in ("new", "nrm", "aff", "res"))
        else:
            new = p.out
        WEIGHTS = 16 * 6
        with nc.Block() as block:
            @block.sync
            def _(sp):
                for tile, dram in ((w1, t["L1_nw1"][l, 0:D, :]), (w2, t["L1_nw2"][l, :, :]),
                                   (b1, t["L1_nb1"][l, :, :]), (b2, four(t["L1_nb2"][l, :, :])),
                                   (gamma, four(t["L1_gamma"])), (beta, four(t["L1_beta"]))):
                    sp.dma_start(tile[:], dram).then_inc(p.weights, 16)

                def free(i, u):
                    sp.wait_ge(pe_did, PE.before("hidden", i, u))
                    settled(sp, p.passed)
                    if final:
                        sp.wait_ge(pool_did, PO.before("res", i, u))
                        settled(sp, p.passed)

                def filled(i, u):
                    if final:
                        sp.wait_ge(dve_did, DV.done("out_apply", i, u))
                    else:
                        sp.wait_ge(act_did, AC.done("update", i, u))

                p.sync_program(sp, free, filled)

            if final:
                @block.gpsimd
                def _(gp):
                    gp.sem_inc(pool_did, PO.per_iteration)
                    gp.wait_ge(p.weights, WEIGHTS)
                    with gp.Fori(0, N_ITERS) as i:
                        for u in NODE_SLOTS:
                            gp.wait_ge(dve_did, DV.done("in_apply", i, u))
                            nc.gpsimd.tensor_tensor(aff[u][:], nrm[u][:], each_tile(gamma), ALU.mult
                                                    ).then_inc(pool_did, 1)
                        for u in NODE_SLOTS:
                            gp.wait_ge(pool_did, PO.done("gamma", i, u))
                            nc.gpsimd.tensor_tensor(aff[u][:], aff[u][:], each_tile(beta), ALU.add
                                                    ).then_inc(pool_did, 1)
                        for u in NODE_SLOTS:
                            gp.wait_ge(pool_did, PO.done("beta", i, u))
                            gp.wait_ge(dve_did, DV.before("out_apply", i, u))
                            gp.wait_ge(p.loaded[u], i * p.per_load + p.per_load)
                            nc.gpsimd.tensor_tensor(res[u][:], aff[u][:], p.residual[u][:], ALU.add
                                                    ).then_inc(pool_did, 1)

            @block.tensor
            def _(pe):
                pe.sem_inc(pe_did, PE.per_iteration)
                pe.wait_ge(p.weights, WEIGHTS)
                with pe.Fori(0, N_ITERS) as i:
                    for u in NODE_SLOTS:
                        pe.wait_ge(p.loaded[u], i * p.per_load + p.per_load)
                        pe.wait_ge(dve_did, DV.before("biased", i, u))
                        p.turn(A[u], u)
                    for u in NODE_SLOTS:
                        pe.wait_ge(act_did, AC.done("xt", i, u))
                        nc.tensor.matmul(B[u][:], w1[:], xt[u][:], start=True, stop=False)
                        for j in range(4):
                            last = nc.tensor.matmul(B[u][:, j * D:(j + 1) * D], p.sums[u][:, j, 0:D], ident[:],
                                                    start=False, stop=(j == 3))
                        last.then_inc(pe_did, 1)
                    for u in NODE_SLOTS:
                        pe.wait_ge(act_did, AC.done("hidden", i, u))
                        for j in range(4):
                            last = nc.tensor.matmul(A[u][:, j * D:(j + 1) * D], ht[u][:, j * D:(j + 1) * D], w2[:],
                                                    start=True, stop=True)
                        last.then_inc(pe_did, 1)

            @block.scalar
            def _(act):
                act.sem_inc(act_did, AC.per_iteration)
                act.wait_ge(p.weights, WEIGHTS)
                with act.Fori(0, N_ITERS) as i:
                    for u in NODE_SLOTS:
                        act.wait_ge(pe_did, PE.done("turn", i, u))
                        nc.scalar.activation(xt[u][:], A[u][:], ACT.Copy).then_inc(act_did, 1)
                    for u in NODE_SLOTS:
                        act.wait_ge(pe_did, PE.done("hidden", i, u))
                        nc.scalar.activation(ht[u][:], B[u][:], ACT.Relu, bias=b1[:]).then_inc(act_did, 1)
                    for u in NODE_SLOTS:
                        act.wait_ge(dve_did, DV.done("biased", i, u))
                        if not final:
                            act.wait_ge(p.stored[u], i * 16 + 16)
                        nc.scalar.activation(new[u][:], biased[u][:], ACT.Relu).then_inc(act_did, 1)
                    if final:
                        p.norm_std(act, i, DV, "in")
                        p.norm_std(act, i, DV, "out")

            @block.vector
            def _(dve):
                dve.wait_ge(p.weights, WEIGHTS)
                dve.sem_inc(dve_did, DV.per_iteration)
                with dve.Fori(0, N_ITERS) as i:
                    for u in NODE_SLOTS:
                        dve.wait_ge(pe_did, PE.done("update", i, u))
                        dve.wait_ge(act_did, AC.before("update", i, u))
                        nc.vector.tensor_tensor(biased[u][:], tiles(A[u]), each_tile(b2), ALU.add
                                                ).then_inc(dve_did, 1)
                    if final:
                        p.norm_stats(dve, i, new, DV, AC, "in",
                                     lambda i, u: dve.wait_ge(act_did, AC.done("update", i, u)))
                        p.norm_apply(dve, i, new, nrm, DV, "in",
                                     lambda i, u: dve.wait_ge(pool_did, PO.before("gamma", i, u)))
                        p.norm_stats(dve, i, res, DV, AC, "out",
                                     lambda i, u: dve.wait_ge(pool_did, PO.done("res", i, u)))
                        p.norm_apply(dve, i, res, p.out, DV, "out",
                                     lambda i, u: dve.wait_ge(p.stored[u], i * 16 + 16))



def layer2_edges(nc, sems, keep, t):
    relations = t["L2_W"].shape[0]
    with ExitStack() as ctx:
        p = EdgePass(nc, sems, ctx, "e2", keep, t["x2"], t["agg_rows"], 1)
        ident = keep["ident"]
        w = p.sb("w", [D, relations, D])
        ones = p.sb("ones", [128, EC])
        kind = p.pair(p.sb, "kind", [128, EC], I32)
        xs, count, total = (p.pair(p.sb, n, [D, EC]) for n in ("xs", "count", "total"))
        of_kind = p.pair(p.sb, "of_kind", [D, relations, EC])
        A, B, C, DD = (p.pair(p.bank, n) for n in "ABCD")
        PE = Steps("turn", "messages", "rows", slots=EDGE_SLOTS)
        AC = Steps("xs", "rows", slots=EDGE_SLOTS)
        DV = Steps("flag", "of_kind", "count/0", "count/1", "total/0", "total/1", slots=EDGE_SLOTS)
        pe_did, act_did, dve_did = p.pe_did, p.act_did, p.dve_did
        with nc.Block() as block:
            @block.sync
            def _(sp):
                sp.dma_start(w[:], t["L2_W"].rearrange("r i o -> i r o")).then_inc(p.weights, 16)
                with sp.Fori(0, E_ITERS) as i:
                    for u in EDGE_SLOTS:
                        sp.wait_ge(dve_did, DV.before("of_kind", i, u))
                        p.stream(sp, i, u, t, [(kind[u][:], t["type_rows"], 128)])

            @block.gpsimd
            def _(gp):
                p.pool_program(gp, PE, AC, ahead=2)

            @block.tensor
            def _(pe):
                pe.sem_inc(pe_did, PE.per_iteration)
                pe.wait_ge(p.weights, 16)
                with pe.Fori(0, E_ITERS) as i:
                    for u in EDGE_SLOTS:
                        pe.wait_ge(p.gathered[u], i * 64 + 64)
                        pe.wait_ge(act_did, AC.before("xs", i, u))
                        p.turn(pe, i, u, (A[u],), PE)
                    for u in EDGE_SLOTS:
                        pe.wait_ge(dve_did, DV.done("of_kind", i, u))
                        pe.wait_ge(dve_did, DV.before("total", i, u))
                        for r in range(relations):
                            last = nc.tensor.matmul(B[u][:, 0:EC], w[:, r, :], of_kind[u][:, r, :],
                                                    start=(r == 0), stop=(r == relations - 1))
                        last.then_inc(pe_did, 1)
                    for u in EDGE_SLOTS:
                        pe.wait_ge(dve_did, DV.done("total", i, u))
                        pe.wait_ge(act_did, AC.before("rows", i, u))
                        for j in range(TILES):
                            nc.tensor.matmul(C[u][0:ET, j * D:(j + 1) * D], tile_of(total[u], j), ident[:],
                                             start=True, stop=True)
                        for j in range(TILES):
                            last = nc.tensor.matmul(DD[u][0:ET, j:j + 1], tile_of(count[u], j), ident[:, 0:1],
                                                    start=True, stop=True)
                        last.then_inc(pe_did, 1)

            @block.scalar
            def _(act):
                act.sem_inc(act_did, AC.per_iteration)
                with act.Fori(0, E_ITERS) as i:
                    for u in EDGE_SLOTS:
                        act.wait_ge(pe_did, PE.done("turn", i, u))
                        act.wait_ge(dve_did, DV.before("of_kind", i, u))
                        nc.scalar.activation(xs[u][:], A[u][:, 0:EC], ACT.Copy).then_inc(act_did, 1)
                    for u in EDGE_SLOTS:
                        act.wait_ge(pe_did, PE.done("rows", i, u))
                        act.wait_ge(p.scattered[u], i * 64 + 16)
                        nc.scalar.activation(p.out_rows[u][:, :, 0:D], tiles(C[u])[0:ET], ACT.Copy)
                        nc.scalar.activation(p.out_rows[u][:, :, D:D + 1],
                                             DD[u][0:ET, 0:TILES].rearrange("p (j a) -> p j a", a=1),
                                             ACT.Copy).then_inc(act_did, 1)

            @block.vector
            def _(dve):
                for u in EDGE_SLOTS:
                    nc.vector.memset(p.out_rows[u][:], 0.0)
                nc.vector.memset(ones[:], 1.0)
                nc.vector.memset(count[1][:], 0.0)
                nc.vector.memset(total[1][:], 0.0).then_inc(dve_did, DV.per_iteration)
                with dve.Fori(0, E_ITERS) as i:
                    for u in EDGE_SLOTS:
                        dve.wait_ge(p.streamed[u], i * 48 + 48)
                        dve.wait_ge(dve_did, DV.before("total", i, u))
                        nc.vector.tensor_tensor(p.flag[u][:], p.dst[u][:], p.prev[u][:], ALU.is_equal
                                                ).then_inc(dve_did, 1)
                    for u in EDGE_SLOTS:
                        dve.wait_ge(act_did, AC.done("xs", i, u))
                        dve.wait_ge(pe_did, PE.before("messages", i, u))
                        for r in range(relations):
                            last = nc.vector.scalar_tensor_tensor(
                                out=of_kind[u][:, r, :], in0=kind[u][:], scalar=float(r), in1=xs[u][:],
                                op0=ALU.is_equal, op1=ALU.mult)
                        last.then_inc(dve_did, 1)
                    for u in EDGE_SLOTS:
                        dve.wait_ge(dve_did, DV.before("count", i, 1) if u == 0 else DV.done("count", i, 0))
                        dve.wait_ge(dve_did, DV.done("flag", i, u))
                        dve.wait_ge(pe_did, PE.before("rows", i, u))
                        nc.vector.tensor_tensor_scan(count[u][:], p.flag[u][:], ones[:], count[1 - u][:, EC - 1:EC],
                                                     ALU.mult, ALU.add).then_inc(dve_did, 1)
                    for u in EDGE_SLOTS:
                        dve.wait_ge(dve_did, DV.before("total", i, 1) if u == 0 else DV.done("total", i, 0))
                        dve.wait_ge(pe_did, PE.done("messages", i, u))
                        nc.vector.tensor_tensor_scan(total[u][:], p.flag[u][:], B[u][:, 0:EC],
                                                     total[1 - u][:, EC - 1:EC], ALU.mult, ALU.add
                                                     ).then_inc(dve_did, 1)



def layer2_nodes(nc, sems, keep, t):
    with ExitStack() as ctx:
        p = NodePass(nc, sems, ctx, "n2", keep, t["x2"], t["agg_rows"], t["x3"])
        w0 = p.sb("w0", [D, D])
        xt = p.pair(p.sb, "xt", [D, NC_])
        both, res = p.pair(p.sb, "both", [128, 4, D]), p.pair(p.sb, "res", [128, 4, D])
        deg, share = p.pair(p.sb, "deg", [128, 4]), p.pair(p.sb, "share", [128, 4])
        A, B = p.pair(p.bank, "A"), p.pair(p.bank, "B")
        PE = Steps("turn", "own", slots=NODE_SLOTS)
        AC = Steps("xt", "out_std", slots=NODE_SLOTS)
        DV = Steps("deg", "share", "both", "res", *norm_steps("out"), slots=NODE_SLOTS)
        pe_did, act_did, dve_did = p.pe_did, p.act_did, p.dve_did
        with nc.Block() as block:
            @block.sync
            def _(sp):
                sp.dma_start(w0[:], t["L2_W0"]).then_inc(p.weights, 16)

                def free(i, u):
                    sp.wait_ge(dve_did, DV.before("res", i, u))
                    settled(sp, p.passed)
                    sp.wait_ge(pe_did, PE.before("turn", i, u))
                    settled(sp, p.passed)

                p.sync_program(sp, free, lambda i, u: sp.wait_ge(dve_did, DV.done("out_apply", i, u)))

            @block.tensor
            def _(pe):
                pe.sem_inc(pe_did, PE.per_iteration)
                pe.wait_ge(p.weights, 16)
                with pe.Fori(0, N_ITERS) as i:
                    for u in NODE_SLOTS:
                        pe.wait_ge(p.loaded[u], i * p.per_load + p.per_load)
                        pe.wait_ge(act_did, AC.before("xt", i, u))
                        p.turn(A[u], u)
                    for u in NODE_SLOTS:
                        pe.wait_ge(act_did, AC.done("xt", i, u))
                        pe.wait_ge(dve_did, DV.before("both", i, u))
                        for j in range(4):
                            last = nc.tensor.matmul(B[u][:, j * D:(j + 1) * D], xt[u][:, j * D:(j + 1) * D], w0[:],
                                                    start=True, stop=True)
                        last.then_inc(pe_did, 1)

            @block.scalar
            def _(act):
                act.sem_inc(act_did, AC.per_iteration)
                with act.Fori(0, N_ITERS) as i:
                    for u in NODE_SLOTS:
                        act.wait_ge(pe_did, PE.done("turn", i, u))
                        nc.scalar.activation(xt[u][:], A[u][:], ACT.Copy).then_inc(act_did, 1)
                    p.norm_std(act, i, DV, "out")

            @block.vector
            def _(dve):
                dve.sem_inc(dve_did, DV.per_iteration)
                with dve.Fori(0, N_ITERS) as i:
                    for u in NODE_SLOTS:
                        dve.wait_ge(p.loaded[u], i * p.per_load + p.per_load)
                        nc.vector.tensor_scalar(deg[u][:], p.sums[u][:, :, D], 1.0, None, ALU.max
                                                ).then_inc(dve_did, 1)
                    for u in NODE_SLOTS:
                        dve.wait_ge(dve_did, DV.done("deg", i, u))
                        nc.vector.reciprocal(share[u][:], deg[u][:]).then_inc(dve_did, 1)
                    for u in NODE_SLOTS:
                        dve.wait_ge(pe_did, PE.done("own", i, u))
                        nc.vector.tensor_tensor(both[u][:], tiles(B[u]), p.sums[u][:, :, 0:D], ALU.add
                                                ).then_inc(dve_did, 1)
                    for u in NODE_SLOTS:
                        dve.wait_ge(dve_did, DV.done("both", i, u))
                        for j in range(4):
                            last = nc.vector.scalar_tensor_tensor(
                                out=res[u][:, j, :], in0=both[u][:, j, :], scalar=share[u][:, j:j + 1],
                                in1=p.rows[u][:, j, :], op0=ALU.mult, op1=ALU.add)
                        last.then_inc(dve_did, 1)
                    p.norm_stats(dve, i, res, DV, AC, "out",
                                 lambda i, u: dve.wait_ge(dve_did, DV.done("res", i, u)))
                    p.norm_apply(dve, i, res, p.out, DV, "out",
                                 lambda i, u: dve.wait_ge(p.stored[u], i * 16 + 16))


class Stages:

    def __init__(self, *names):
        self.order, self.back = [], set()
        for name in names:
            half, _, step = name.partition(" ")
            step, _, slot = step.partition("/")
            self.order.append((step, int(slot or 0)))
            if half == "back":
                self.back.add((step, int(slot or 0)))
        self.per_iteration = len(self.order)

    def done(self, name, i, u=0):
        body = i + 1 if (name, u) in self.back else i
        return body * self.per_iteration + (self.per_iteration + self.order.index((name, u)) + 1)

    def before(self, name, i, u=0):
        body = i if (name, u) in self.back else i - 1
        return body * self.per_iteration + (self.per_iteration + self.order.index((name, u)) + 1)

    def runs(self, step, back, front):
        return (back if step in self.back else front) is not None

    def size(self, name, u, back, front):
        at = self.order.index((name, u))
        n = 1
        while n <= at and not self.runs(self.order[at - n], back, front):
            n += 1
        return n

    def left(self, back, front):
        n = 0
        while not self.runs(self.order[-1 - n], back, front):
            n += 1
        return n



def layer3_edges(nc, sems, keep, t):
    with ExitStack() as ctx:
        p = EdgePass(nc, sems, ctx, "e3", keep, t["x3"], t["agg_rows"], 2)
        lanes = 32 + H3
        low = 64
        at_slot = (slice(0, H3), slice(32, 32 + H3))
        w, att = p.sb("w", [D, H3, D]), p.sb("att", [D, 2, H3, D])
        weighed = p.sb("weighed", [D, 2, H3, D])
        to_logit = p.sb("to_logit", [D, 2, H3])
        own_logit = p.sb("own_logit", [D, H3])
        wq4 = p.sb("wq4", [D, H3, D])
        pick_f32 = p.sb("pick_f32", [low + lanes, 2 * H3, D])
        pick = p.sb("pick", [low + lanes, 2 * H3, D], BF16)
        xs, xd, diff = (p.pair(p.sb, n, [D, EC]) for n in ("xs", "xd", "diff"))
        part = p.pair(p.sb, "part", [D, EC])
        total = p.pair(p.sb, "total", [D, H3, EC])
        dst, prev = p.sb("lane_dst", [lanes, EC], I32), p.sb("lane_prev", [lanes, EC], I32)
        flag, pen, start = (p.sb(n, [lanes, EC]) for n in ("flag", "pen", "start"))
        raw, leaky = p.sb("raw", [lanes, 2, EC]), p.sb("leaky", [lanes, 2, EC])
        top = p.sb("top", [lanes, EC])
        m, den = p.sb("m", [lanes, EC + 1]), p.sb("den", [lanes, EC + 1])
        de, ce = p.sb("de", [lanes, 3, EC]), p.sb("ce", [lanes, 3, EC])
        rden, ratio = p.sb("rden", [lanes, EC]), p.sb("ratio", [lanes, EC])
        factors = p.sb("factors", [lanes, 2, EC])
        rest = p.sb("rest", [lanes, 2, EC])
        high_parts = p.sb("high_parts", [low + lanes, 2, EC], BF16)
        low_parts = p.sb("low_parts", [lanes, 2, EC], BF16)
        T = ctx.enter_context(nc.psum_tensor("e3_T", [128, 2, 512], F32))
        P = [[p.bank(f"P{k}{s}") for s in ("keep", "share")] for k in range(2)]
        R = p.pair(p.bank, "R")
        chains = [(h, u) for h in range(H3) for u in EDGE_SLOTS]
        PE = Stages("back spread0/0", "back spread0/1", "front turn/0",
                    "back spread1/0", "back rows0/0", "front turn/1",
                    "back spread1/1", "back rows0/1", "front logits",
                    "back spread2/0", "back rows1/0", "back spread2/1", "back rows1/1",
                    "back spread3/0", "back rows2/0", "back spread3/1", "back rows2/1",
                    "back rows3/0", "back rows3/1")
        AC = Stages("front xs/0", "front xd/0", "front xs/1", "front xd/1", "front raw", "front exp", "front high",
                    "front middle", "back rows/0", "back rows/1")
        DV = Stages("back part0/0", "back total0/0", "front flag", "back part0/1", "back total0/1", "front pen",
                    "back part1/0", "back total1/0", "back part1/1", "back total1/1", "front leaky",
                    "back part2/0", "back total2/0",
                    "front top", "front carry/0", "front max/0", "front carry/1", "front max/1", "front drop",
                    "front differences", "back part2/1", "back total2/1",
                    "front own", "front add_own", "front carry_den/0", "front den/0", "front carry_den/1",
                    "front den/1", "front rden", "front ratio", "front factors",
                    "back part3/0", "back total3/0", "front rest", "back part3/1", "back total3/1",
                    "front diff/0", "front diff/1", "front low")
        pe_did, act_did, dve_did = p.pe_did, p.act_did, p.dve_did
        setup_did = p.sem("setup_did")
        WEIGHTS = 16 * 4

        def bodies(eng, body):
            body(None, 0)
            with eng.Fori(0, E_ITERS - 1) as i:
                body(i, i + 1)
            body(E_ITERS - 1, None)

        with nc.Block() as block:
            @block.sync
            def _(sp):
                sp.dma_start(w[:], t["L3_W"].rearrange("i (h o) -> i h o", h=H3)).then_inc(p.weights, 16)
                sp.dma_start(att[:, 0, :, :].rearrange("p h o -> p (h o)"),
                             t["L3_att_src"].broadcast_to([D, H3 * D])).then_inc(p.weights, 16)
                sp.dma_start(att[:, 1, :, :].rearrange("p h o -> p (h o)"),
                             t["L3_att_dst"].broadcast_to([D, H3 * D])).then_inc(p.weights, 16)
                sp.dma_start(pick_f32[:].rearrange("k c o -> k (c o)"), t["head_pick"]).then_inc(p.weights, 16)
                with sp.Fori(0, E_ITERS) as i:
                    sp.wait_ge(dve_did, DV.before("flag", i))
                    settled(sp, p.passed)
                    for rows, tile in ((t["dst_rows"], dst), (t["prev_rows"], prev)):
                        sp.dma_start(tile[0:32, :], rows[bass.ds(2 * i, 1), :].broadcast_to([32, EC])
                                     ).then_inc(p.streamed[0], 16)
                        sp.dma_start(tile[32:lanes, :], rows[bass.ds(2 * i + 1, 1), :].broadcast_to([H3, EC])
                                     ).then_inc(p.streamed[0], 16)

            @block.gpsimd
            def _(gp):
                p.pool_program(gp, PE, AC, ahead=2)

            @block.tensor
            def _(pe):
                def body(back, front):
                    def spread(h, u):
                        c = chains.index((h, u))
                        if c < 2:
                            pe.wait_ge(dve_did, DV.done("low", back))
                        else:
                            before_h, before_u = chains[c - 2]
                            pe.wait_ge(dve_did, DV.done(f"total{before_h}", back, before_u))
                        lane = u * H3 + h
                        for s in range(2):
                            nc.tensor.matmul(P[c % 2][s][:, 0:EC], pick[:, lane, :], high_parts[:, s, :],
                                             start=True, stop=False)
                            last = nc.tensor.matmul(P[c % 2][s][:, 0:EC], pick[0:lanes, lane, :], low_parts[:, s, :],
                                                    start=False, stop=True)
                        last.then_inc(pe_did, PE.size(f"spread{h}", u, back, front))

                    def rows(h, u):
                        pe.wait_ge(dve_did, DV.done(f"total{h}", back, u))
                        if h == 0:
                            pe.wait_ge(act_did, AC.before("rows", back, u))
                        for j in range(TILES):
                            last = nc.tensor.matmul(R[u][0:ET, j * D:(j + 1) * D],
                                                    total[u][:, h, j * ET:(j + 1) * ET], wq4[:, h, :],
                                                    start=(h == 0 and j == 0), stop=(h == H3 - 1),
                                                    skip_group_check=True)
                        last.then_inc(pe_did, PE.size(f"rows{h}", u, back, front))

                    def turn(u):
                        pe.wait_ge(p.gathered[u], front * 128 + 128)
                        if u == 0:
                            pe.wait_ge(act_did, AC.before("raw", front))
                        else:
                            pe.wait_ge(act_did, AC.done("xd", front, 0))
                        for end in range(2):
                            for j in range(TILES):
                                last = nc.tensor.transpose(T[:, end, j * ET:(j + 1) * ET],
                                                           p.end_rows[u][:, end * TILES + j, :],
                                                           keep["ident"][0:ET, 0:ET])
                        last.then_inc(pe_did, PE.size("turn", u, back, front))

                    if back is not None:
                        spread(0, 0)
                        spread(0, 1)
                    if front is not None:
                        turn(0)
                    if back is not None:
                        spread(1, 0)
                        rows(0, 0)
                    if front is not None:
                        turn(1)
                    if back is not None:
                        spread(1, 1)
                        rows(0, 1)
                    if front is not None:
                        pe.wait_ge(act_did, AC.done("xd", front, 1))
                        for u in EDGE_SLOTS:
                            nc.tensor.matmul(T[at_slot[u], 0, 0:EC], to_logit[:, 0, :], xs[u][:],
                                             start=True, stop=False)
                            nc.tensor.matmul(T[at_slot[u], 0, 0:EC], to_logit[:, 1, :], xd[u][:],
                                             start=False, stop=True)
                            last = nc.tensor.matmul(T[at_slot[u], 1, 0:EC], own_logit[:], xd[u][:],
                                                    start=True, stop=True)
                        last.then_inc(pe_did, PE.size("logits", 0, back, front))
                    if back is not None:
                        for c in range(4, len(chains)):
                            spread(*chains[c])
                            rows(*chains[c - 2])
                        for c in range(len(chains) - 2, len(chains)):
                            rows(*chains[c])
                    else:
                        pe.wait_ge(pe_did, PE.done("logits", front))
                        pe.sem_inc(pe_did, PE.left(back, front))

                pe.sem_inc(pe_did, PE.per_iteration)
                pe.wait_ge(setup_did, 5)
                bodies(pe, body)

            @block.scalar
            def _(act):
                def body(back, front):
                    if front is not None:
                        for u in EDGE_SLOTS:
                            act.wait_ge(pe_did, PE.done("turn", front, u))
                            act.wait_ge(dve_did, DV.before("diff", front, u))
                            nc.scalar.activation(xs[u][:], T[:, 0, 0:EC], ACT.Copy
                                                 ).then_inc(act_did, AC.size("xs", u, back, front))
                            nc.scalar.activation(xd[u][:], T[:, 1, 0:EC], ACT.Copy
                                                 ).then_inc(act_did, AC.size("xd", u, back, front))
                        act.wait_ge(pe_did, PE.done("logits", front))
                        act.wait_ge(dve_did, DV.before("leaky", front))
                        nc.scalar.activation(raw[:], T[0:lanes, :, 0:EC], ACT.Copy
                                             ).then_inc(act_did, AC.size("raw", 0, back, front))
                        act.wait_ge(dve_did, DV.done("differences", front))
                        nc.scalar.activation(ce[:], de[:], ACT.Exp).then_inc(act_did, AC.size("exp", 0, back, front))
                        act.wait_ge(dve_did, DV.done("factors", front))
                        act.wait_ge(pe_did, PE.before("spread3", front, 1))
                        nc.scalar.activation(high_parts[0:lanes], factors[:], ACT.Copy
                                             ).then_inc(act_did, AC.size("high", 0, back, front))
                        act.wait_ge(dve_did, DV.done("rest", front))
                        nc.scalar.activation(high_parts[low:low + lanes], rest[:], ACT.Copy
                                             ).then_inc(act_did, AC.size("middle", 0, back, front))
                    if back is not None:
                        for u in EDGE_SLOTS:
                            act.wait_ge(pe_did, PE.done("rows3", back, u))
                            act.wait_ge(p.scattered[u], back * 64 + 16)
                            nc.scalar.activation(p.out_rows[u][:, :, 0:D], tiles(R[u])[0:ET], ACT.Copy
                                                 ).then_inc(act_did, AC.size("rows", u, back, front))
                    else:
                        act.wait_ge(act_did, AC.done("middle", front))
                        act.sem_inc(act_did, AC.left(back, front))

                act.sem_inc(act_did, AC.per_iteration)
                bodies(act, body)

            @block.vector
            def _(dve):
                def body(back, front):
                    def step(name, u=0):
                        return dve_did, DV.size(name, u, back, front)

                    def chain(h, u):
                        if back is None:
                            return
                        bank = P[chains.index((h, u)) % 2]
                        dve.wait_ge(pe_did, PE.done(f"spread{h}", back, u))
                        nc.vector.tensor_tensor(part[u][:], diff[u][:], bank[1][:, 0:EC], ALU.mult
                                                ).then_inc(*step(f"part{h}", u))
                        dve.wait_ge(dve_did, DV.done(f"part{h}", back, u))
                        dve.wait_ge(pe_did, PE.before(f"rows{h}", back, u))
                        dve.wait_ge(dve_did, DV.before(f"total{h}", back, 1) if u == 0
                                    else DV.done(f"total{h}", back, 0))
                        nc.vector.tensor_tensor_scan(total[u][:, h, :], bank[0][:, 0:EC], part[u][:],
                                                     total[1 - u][:, h, EC - 1:EC], ALU.mult, ALU.add
                                                     ).then_inc(*step(f"total{h}", u))

                    chain(0, 0)
                    if front is not None:
                        dve.wait_ge(p.streamed[0], front * 64 + 64)
                        nc.vector.tensor_tensor(flag[:], dst[:], prev[:], ALU.is_equal).then_inc(*step("flag"))
                    chain(0, 1)
                    if front is not None:
                        dve.wait_ge(dve_did, DV.done("flag", front))
                        nc.vector.tensor_scalar(pen[:], flag[:], FAR, -FAR, ALU.mult, ALU.add)
                        nc.vector.tensor_scalar(start[:], flag[:], -1.0, 1.0, ALU.mult, ALU.add
                                                ).then_inc(*step("pen"))
                    chain(1, 0)
                    chain(1, 1)
                    if front is not None:
                        dve.wait_ge(act_did, AC.done("raw", front))
                        nc.vector.scalar_tensor_tensor(out=leaky[:], in0=raw[:], scalar=0.2,
                                                       in1=raw[:], op0=ALU.mult, op1=ALU.max
                                                       ).then_inc(*step("leaky"))
                    chain(2, 0)
                    if front is not None:
                        dve.wait_ge(dve_did, DV.done("leaky", front))
                        nc.vector.tensor_tensor(top[:], leaky[:, 0, :], leaky[:, 1, :], ALU.max).then_inc(*step("top"))
                        for u in EDGE_SLOTS:
                            here, other = at_slot[u], at_slot[1 - u]
                            dve.wait_ge(dve_did, DV.done("top", front) if u == 0 else DV.done("max", front, 0))
                            nc.vector.tensor_copy(m[here, 0:1], m[other, EC:EC + 1]).then_inc(*step("carry", u))
                            dve.wait_ge(dve_did, DV.done("carry", front, u))
                            nc.vector.tensor_tensor_scan(m[here, 1:EC + 1], pen[here, :], top[here, :], m[here, 0:1],
                                                         ALU.add, ALU.max).then_inc(*step("max", u))
                        dve.wait_ge(dve_did, DV.done("max", front, 1))
                        nc.vector.tensor_tensor(de[:, 0, :], m[:, 0:EC], m[:, 1:EC + 1], ALU.subtract
                                                ).then_inc(*step("drop"))
                        dve.wait_ge(dve_did, DV.done("drop", front))
                        nc.vector.tensor_tensor(de[:, 0, :], de[:, 0, :], pen[:], ALU.add)
                        for s in range(2):
                            last = nc.vector.tensor_tensor(de[:, 1 + s, :], leaky[:, s, :], m[:, 1:EC + 1],
                                                           ALU.subtract)
                        last.then_inc(*step("differences"))
                    chain(2, 1)
                    if front is not None:
                        dve.wait_ge(act_did, AC.done("exp", front))
                        nc.vector.tensor_tensor(start[:], start[:], ce[:, 2, :], ALU.mult).then_inc(*step("own"))
                        dve.wait_ge(dve_did, DV.done("own", front))
                        nc.vector.tensor_tensor(top[:], start[:], ce[:, 1, :], ALU.add).then_inc(*step("add_own"))
                        for u in EDGE_SLOTS:
                            here, other = at_slot[u], at_slot[1 - u]
                            dve.wait_ge(dve_did, DV.done("add_own", front) if u == 0 else DV.done("den", front, 0))
                            nc.vector.tensor_copy(den[here, 0:1], den[other, EC:EC + 1]
                                                  ).then_inc(*step("carry_den", u))
                            dve.wait_ge(dve_did, DV.done("carry_den", front, u))
                            nc.vector.tensor_tensor_scan(den[here, 1:EC + 1], ce[here, 0, :], top[here, :],
                                                         den[here, 0:1], ALU.mult, ALU.add).then_inc(*step("den", u))
                        dve.wait_ge(dve_did, DV.done("den", front, 1))
                        nc.vector.reciprocal(rden[:], den[:, 1:EC + 1]).then_inc(*step("rden"))
                        dve.wait_ge(dve_did, DV.done("rden", front))
                        nc.vector.tensor_tensor(ratio[:], rden[:], den[:, 0:EC], ALU.mult).then_inc(*step("ratio"))
                        nc.vector.tensor_tensor(factors[:, 1, :], ce[:, 1, :], rden[:], ALU.mult)
                        dve.wait_ge(dve_did, DV.done("ratio", front))
                        nc.vector.tensor_tensor(factors[:, 0, :], ce[:, 0, :], ratio[:], ALU.mult
                                                ).then_inc(*step("factors"))
                    chain(3, 0)
                    if front is not None:
                        dve.wait_ge(act_did, AC.done("high", front))
                        nc.vector.tensor_tensor(rest[:], factors[:], high_parts[0:lanes], ALU.subtract
                                                ).then_inc(*step("rest"))
                    chain(3, 1)
                    if front is not None:
                        for u in EDGE_SLOTS:
                            dve.wait_ge(act_did, AC.done("xd", front, u))
                            nc.vector.tensor_tensor(diff[u][:], xs[u][:], xd[u][:], ALU.subtract
                                                    ).then_inc(*step("diff", u))
                        dve.wait_ge(act_did, AC.done("middle", front))
                        nc.vector.tensor_tensor(low_parts[:], rest[:], high_parts[low:low + lanes], ALU.subtract
                                                ).then_inc(*step("low"))

                for u in EDGE_SLOTS:
                    nc.vector.memset(p.out_rows[u][:], 0.0)
                nc.vector.memset(m[:], 0.0)
                nc.vector.memset(den[:], 1.0)
                nc.vector.memset(high_parts[:], 0.0)
                dve.wait_ge(p.weights, WEIGHTS)
                nc.vector.tensor_copy(pick[:], pick_f32[:]).then_inc(setup_did, 1)
                for s in range(2):
                    last = nc.vector.tensor_tensor(weighed[:, s, :, :], w[:], att[:, s, :, :], ALU.mult)
                last.then_inc(setup_did, 1)
                dve.wait_ge(setup_did, 2)
                nc.vector.tensor_reduce(to_logit[:].rearrange("p s h -> p (s h)"),
                                        weighed[:].rearrange("p s h o -> p (s h) o"), mybir.AxisListType.X, ALU.add
                                        ).then_inc(setup_did, 1)
                nc.vector.tensor_scalar(wq4[:], w[:], 1.0 / H3, None, ALU.mult).then_inc(setup_did, 1)
                dve.wait_ge(setup_did, 3)
                nc.vector.tensor_tensor(own_logit[:], to_logit[:, 0, :], to_logit[:, 1, :], ALU.add
                                        ).then_inc(setup_did, 1)
                nc.vector.memset(total[1][:], 0.0).then_inc(dve_did, DV.per_iteration)
                bodies(dve, body)



def layer3_nodes(nc, sems, keep, t):
    with ExitStack() as ctx:
        p = NodePass(nc, sems, ctx, "n3", keep, t["x3"], t["agg_rows"], t["out"])
        w, two, wm = p.sb("w", [D, H3, D]), p.sb("two", [D, 2, D]), p.sb("wm", [D, D])
        bias = p.sb("bias", [128, D])
        xt = p.pair(p.sb, "xt", [D, NC_])
        more, both, res = (p.pair(p.sb, n, [128, 4, D]) for n in ("more", "both", "res"))
        A, B = p.pair(p.bank, "A"), p.pair(p.bank, "B")
        PE = Steps("turn", "own", slots=NODE_SLOTS)
        AC = Steps("xt", "out_std", slots=NODE_SLOTS)
        PO = Steps("more", slots=NODE_SLOTS)
        DV = Steps("both", "res", *norm_steps("out"), slots=NODE_SLOTS)
        pe_did, act_did, dve_did, pool_did = p.pe_did, p.act_did, p.dve_did, p.pool_did
        setup_did = p.sem("setup_did")
        with nc.Block() as block:
            @block.sync
            def _(sp):
                sp.dma_start(w[:], t["L3_W"].rearrange("i (h o) -> i h o", h=H3)).then_inc(p.weights, 16)
                sp.dma_start(bias[:], four(t["L3_bias"])).then_inc(p.weights, 16)

                def free(i, u):
                    sp.wait_ge(dve_did, DV.before("res", i, u))
                    settled(sp, p.passed)
                    sp.wait_ge(pe_did, PE.before("turn", i, u))
                    settled(sp, p.passed)
                    sp.wait_ge(pool_did, PO.before("more", i, u))
                    settled(sp, p.passed)

                p.sync_program(sp, free, lambda i, u: sp.wait_ge(dve_did, DV.done("out_apply", i, u)))

            @block.gpsimd
            def _(gp):
                gp.sem_inc(pool_did, PO.per_iteration)
                gp.wait_ge(p.weights, 32)
                with gp.Fori(0, N_ITERS) as i:
                    for u in NODE_SLOTS:
                        gp.wait_ge(p.loaded[u], i * p.per_load + p.per_load)
                        gp.wait_ge(dve_did, DV.before("both", i, u))
                        nc.gpsimd.tensor_tensor(more[u][:], p.sums[u][:, :, 0:D], each_tile(bias), ALU.add
                                                ).then_inc(pool_did, 1)

            @block.tensor
            def _(pe):
                pe.sem_inc(pe_did, PE.per_iteration)
                pe.wait_ge(setup_did, 3)
                with pe.Fori(0, N_ITERS) as i:
                    for u in NODE_SLOTS:
                        pe.wait_ge(p.loaded[u], i * p.per_load + p.per_load)
                        pe.wait_ge(act_did, AC.before("xt", i, u))
                        p.turn(A[u], u)
                    for u in NODE_SLOTS:
                        pe.wait_ge(act_did, AC.done("xt", i, u))
                        pe.wait_ge(dve_did, DV.before("both", i, u))
                        for j in range(4):
                            last = nc.tensor.matmul(B[u][:, j * D:(j + 1) * D], xt[u][:, j * D:(j + 1) * D], wm[:],
                                                    start=True, stop=True)
                        last.then_inc(pe_did, 1)

            @block.scalar
            def _(act):
                act.sem_inc(act_did, AC.per_iteration)
                with act.Fori(0, N_ITERS) as i:
                    for u in NODE_SLOTS:
                        act.wait_ge(pe_did, PE.done("turn", i, u))
                        nc.scalar.activation(xt[u][:], A[u][:], ACT.Copy).then_inc(act_did, 1)
                    p.norm_std(act, i, DV, "out")

            @block.vector
            def _(dve):
                dve.wait_ge(p.weights, 32)
                nc.vector.tensor_tensor(two[:], w[:, 0:2, :], w[:, 2:4, :], ALU.add).then_inc(setup_did, 1)
                dve.wait_ge(setup_did, 1)
                nc.vector.tensor_tensor(wm[:], two[:, 0, :], two[:, 1, :], ALU.add).then_inc(setup_did, 1)
                dve.wait_ge(setup_did, 2)
                nc.vector.tensor_scalar(wm[:], wm[:], 1.0 / H3, None, ALU.mult).then_inc(setup_did, 1)
                dve.sem_inc(dve_did, DV.per_iteration)
                with dve.Fori(0, N_ITERS) as i:
                    for u in NODE_SLOTS:
                        dve.wait_ge(pe_did, PE.done("own", i, u))
                        dve.wait_ge(pool_did, PO.done("more", i, u))
                        nc.vector.tensor_tensor(both[u][:], tiles(B[u]), more[u][:], ALU.add).then_inc(dve_did, 1)
                    for u in NODE_SLOTS:
                        dve.wait_ge(dve_did, DV.done("both", i, u))
                        nc.vector.scalar_tensor_tensor(out=flat(res[u]), in0=flat(both[u]), scalar=0.0,
                                                       in1=flat(p.rows[u]), op0=ALU.max, op1=ALU.add
                                                       ).then_inc(dve_did, 1)
                    p.norm_stats(dve, i, res, DV, AC, "out",
                                 lambda i, u: dve.wait_ge(dve_did, DV.done("res", i, u)))
                    p.norm_apply(dve, i, res, p.out, DV, "out",
                                 lambda i, u: dve.wait_ge(p.stored[u], i * 16 + 16))



def resident(nc, ctx):
    return {
        "gather_index": ctx.enter_context(nc.sbuf_tensor("gather_index", [ET, E // EC, 2 * TILES], I32)),
        "scatter_index": ctx.enter_context(nc.sbuf_tensor("scatter_index", [ET, E // EC, TILES], I32)),
        "ident": ctx.enter_context(nc.sbuf_tensor("ident", [128, 128], F32)),
    }


def scratch(nc):
    made = {n: nc.dram_tensor(n, [N, D], F32, kind="Internal").ap() for n in ("x1", "h1", "h2", "x2", "x3")}
    made["agg_rows"] = nc.dram_tensor("agg_rows", [N, ROW], F32, kind="Internal").ap()
    return made


def four_graph_layers(nc, t):
    with ExitStack() as sems, ExitStack() as ctx:
        keep = resident(nc, ctx)
        keep["small"] = t["ident"][0:16, 0:16]
        keep["passed"] = sems.enter_context(nc.semaphore("passed"))
        t = {**t, **scratch(nc)}
        setup_pass(nc, sems, keep, t)
        layer0_edges(nc, sems, keep, t)
        layer0_nodes(nc, sems, keep, t)
        states = ["x1", "h1", "h2", "x2"]
        for l in range(3):
            layer1_edges(nc, sems, keep, t, l, t[states[l]])
            layer1_nodes(nc, sems, keep, t, l, t[states[l]], t[states[l + 1]])
        layer2_edges(nc, sems, keep, t)
        layer2_nodes(nc, sems, keep, t)
        layer3_edges(nc, sems, keep, t)
        layer3_nodes(nc, sems, keep, t)


def laid_out(inputs):
    import numpy as np

    a = {n: np.asarray(v) for n, v in inputs.items()}
    dst = a["dst"]
    edge = np.full(1, -1, dst.dtype)
    tiles = lambda v: np.ascontiguousarray(v.reshape(E // ET, ET).T)
    chunks = lambda v: np.ascontiguousarray(v.reshape(E // EC, EC))
    of_head = (np.arange(D)[:, None] // (D // H0) == np.arange(H0)[None, :]).astype(np.float32)
    head_pick = np.zeros((64 + 32 + H3, 2, H3, D), np.float32)
    for u in range(2):
        for h in range(H3):
            head_pick[[32 * u + h, 64 + 32 * u + h], u, h, :] = 1.0
    head_pick = head_pick.reshape(-1, 2 * H3 * D)
    out = {
        "x": a["x"],
        "src_tiles": tiles(a["src"]), "dst_tiles": tiles(dst),
        "next_tiles": tiles(np.concatenate([dst[1:], edge])),
        "dst_rows": chunks(dst), "prev_rows": chunks(np.concatenate([edge, dst[:-1]])),
        "type_rows": chunks(a["edge_type_8"]), "edge_weight_rows": chunks(a["edge_weight"]),
        "ident": np.eye(128, dtype=np.float32),
        "head_mask": of_head / np.sqrt(np.float32(D // H0)),
        "head_spread": np.ascontiguousarray(of_head.T),
        "head_pick": head_pick,
        "L0_Wg": np.ascontiguousarray(a["L0_gnn_Wg"].reshape(3, D).T),
        "L0_Ws_turned": np.ascontiguousarray(a["L0_gnn_Ws"].T),
        "L0_alpha": a["L0_gnn_alpha"].reshape(1, 1), "L0_bg": a["L0_gnn_bg"].reshape(1, 1),
        "L0_bs_row": a["L0_gnn_bs"].reshape(1, D),
        "L1_ew1": a["L1_gnn_ew1"], "L1_ew2": a["L1_gnn_ew2"],
        "L1_nw1": a["L1_gnn_nw1"], "L1_nw2": a["L1_gnn_nw2"],
        "L1_eb1": a["L1_gnn_eb1"].reshape(3, D, 1), "L1_eb2": a["L1_gnn_eb2"].reshape(3, D, 1),
        "L1_nb1": a["L1_gnn_nb1"].reshape(3, D, 1), "L1_nb2": a["L1_gnn_nb2"].reshape(3, 1, D),
        "L2_W": a["L2_gnn_W"], "L2_W0": a["L2_gnn_W0"],
        "L3_W": a["L3_gnn_W"], "L3_bias": a["L3_gnn_bias"].reshape(1, D),
        "L3_att_src": a["L3_gnn_att_src"].reshape(1, H3 * D),
        "L3_att_dst": a["L3_gnn_att_dst"].reshape(1, H3 * D),
    }
    for n in ("Wq", "Wk", "Wv", "Ws"):
        out[f"L0_{n}"] = a[f"L0_gnn_{n}"]
    for n in ("bq", "bk", "bv", "bs"):
        out[f"L0_{n}"] = a[f"L0_gnn_{n}"].reshape(D, 1)
    for layer in ("L0", "L1"):
        for n in ("gamma", "beta"):
            out[f"{layer}_{n}"] = a[f"{layer}_gnn_{n}"].reshape(1, D)
    return out


def kernel(**inputs):
    import numpy as _np
    import concourse.bacc as _bacc
    from concourse import mybir as _mybir
    from concourse.bass_utils import run_bass_kernel_spmd as _run

    nc = _bacc.Bacc("TRN2", target_bir_lowering=False, num_devices=1)
    arrays = {f"in_{n}": _np.ascontiguousarray(a) for n, a in laid_out(inputs).items()}
    t = {n[3:]: nc.dram_tensor(n, a.shape, _mybir.dt.from_np(a.dtype), kind="ExternalInput").ap()
         for n, a in arrays.items()}
    t["out"] = nc.dram_tensor("out", [N, D], F32, kind="ExternalOutput").ap()
    four_graph_layers(nc, t)
    r = _run(nc, [arrays], core_ids=[0])
    return r.results[0]["out"]
```

```python
from contextlib import ExitStack

import concourse.bass as bass
from concourse import mybir

ALU = mybir.AluOpType
ACT = mybir.ActivationFunctionType
F32 = mybir.dt.float32
I32 = mybir.dt.int32
BF16 = mybir.dt.bfloat16

D = 128
N = 50000
E = 25000
ET, TILES = 125, 4
EC = ET * TILES
E_ITERS = E // (2 * EC)
NC_ = 4 * D
N_ITERS = -(-N // (4 * NC_))
WALK = (N - N_ITERS * NC_) // 3
ROW = 132
H0, H3 = 4, 4
EPS = 1e-5
FAR = 1.0e30
FILLS = 10
SKIP = 65536
EDGE_SLOTS = (0, 1)
NODE_SLOTS = (0, 1, 2, 3)
EARLY, LATE = (0, 1), (2, 3)


class Steps:

    def __init__(self, *names, slots):
        self.order = []
        for name in names:
            step, _, slot = name.partition("/")
            self.order += [(step, int(slot))] if slot else [(step, u) for u in slots]
        self.per_iteration = len(self.order)

    def before(self, name, i, u):
        return i * self.per_iteration + (self.order.index((name, u)) + 1)

    def done(self, name, i, u):
        return i * self.per_iteration + (self.per_iteration + self.order.index((name, u)) + 1)


class Stages:

    def __init__(self, *names):
        self.order, self.back = [], set()
        for name in names:
            half, _, step = name.partition(" ")
            step, _, slot = step.partition("/")
            self.order.append((step, int(slot or 0)))
            if half == "back":
                self.back.add((step, int(slot or 0)))
        self.per_iteration = len(self.order)

    def done(self, name, i, u=0):
        body = i + 1 if (name, u) in self.back else i
        return body * self.per_iteration + (self.per_iteration + self.order.index((name, u)) + 1)

    def before(self, name, i, u=0):
        body = i if (name, u) in self.back else i - 1
        return body * self.per_iteration + (self.per_iteration + self.order.index((name, u)) + 1)

    def runs(self, step, back, front):
        return (back if step in self.back else front) is not None

    def size(self, name, u, back, front):
        at = self.order.index((name, u))
        n = 1
        while n <= at and not self.runs(self.order[at - n], back, front):
            n += 1
        return n

    def left(self, back, front):
        n = 0
        while not self.runs(self.order[-1 - n], back, front):
            n += 1
        return n

    def sizes(self, back, front):
        return lambda name, u=0: self.size(name, u, back, front)


def halves(*names):
    order = []
    for early, late, half_of_late in ((EARLY, LATE, "back"), (LATE, EARLY, "front")):
        for name in names:
            step, _, stage = name.partition(" ")
            half, slots = {"E": ("front", early), "L": (half_of_late, late), "P": ("back", early)}[stage]
            order += [f"{half} {step}/{u}" for u in slots]
    return order


def bodies(eng, iterations, body):
    body(None, 0)
    with eng.Fori(0, iterations - 1) as i:
        body(i, i + 1)
    body(iterations - 1, None)


class Iteration:

    def __init__(self, number, buffer, loads):
        self.number, self.buffer, self.loads = number, buffer, loads

    def __mul__(self, n):
        return self.number * n

    def __add__(self, n):
        return self.number + n

    def __sub__(self, n):
        return self.number - n


def buffered_bodies(eng, iterations, body):
    pairs = iterations // 2
    body(None, Iteration(0, 0, 1))
    with eng.Fori(0, pairs) as k:
        body(Iteration(2 * k, 0, k + 1), Iteration(2 * k + 1, 1, k + 1))
        body(Iteration(2 * k + 1, 1, k + 1), Iteration(2 * k + 2, 0, k + 2))
    body(Iteration(2 * pairs, 0, pairs + 1), None)


class Pass:

    slots = EDGE_SLOTS

    def __init__(self, nc, sems, ctx, tag):
        self.nc, self.sems, self.ctx, self.tag = nc, sems, ctx, tag

    def sb(self, name, shape, dt=F32):
        return self.ctx.enter_context(self.nc.sbuf_tensor(f"{self.tag}_{name}", shape, dt))

    def bank(self, name):
        return self.ctx.enter_context(self.nc.psum_tensor(f"{self.tag}_{name}", [128, 512], F32))

    def sem(self, name):
        return self.sems.enter_context(self.nc.semaphore(f"{self.tag}_{name}"))

    def pair(self, make, name, *args):
        return [make(f"{name}{u}", *args) for u in self.slots]


def settled(eng, passed):
    eng.sem_inc(passed, 1)


def as_rows(dram, i, u, width=D):
    start = u * WALK + i * NC_
    return dram[bass.ds(start, NC_), :].rearrange("(p j) d -> p j d", j=4)



def setup_pass(nc, sems, keep, t):
    with ExitStack() as ctx:
        p = Pass(nc, sems, ctx, "setup")
        gidx, sidx, ident = keep["gather_index"], keep["scatter_index"], keep["ident"]
        src = p.sb("src", [ET, E // ET], I32)
        dst = p.sb("dst", [ET, E // ET], I32)
        nxt = p.sb("nxt", [ET, E // ET], I32)
        same = p.sb("same", [ET, E // ET], I32)
        zeros, filled = keep["zeros"], keep["filled"]
        loaded, zeroed, did = (p.sem(s) for s in ("loaded", "zeroed", "did"))
        chunked = lambda a: a[:].rearrange("p (c j) -> p c j", j=TILES)
        with nc.Block() as block:
            @block.sync
            def _(sp):
                for tile, dram in ((src, t["src_tiles"]), (dst, t["dst_tiles"]), (nxt, t["next_tiles"]),
                                   (ident, t["ident"])):
                    sp.dma_start(tile[:], dram).then_inc(loaded, 16)
                sp.wait_ge(zeroed, 1)
                table = t["agg_rows"].rearrange("n r -> (n r)").rearrange("(k p f) -> k p f", k=FILLS, p=96)
                for k in range(FILLS):
                    sp.dma_start(table[k], zeros[:]).then_inc(filled, 16)

            @block.vector
            def _(dve):
                nc.vector.memset(zeros[:], 0.0).then_inc(zeroed, 1)
                dve.wait_ge(loaded, 64)
                nc.vector.tensor_copy(gidx[:, :, 0:TILES], chunked(src))
                nc.vector.tensor_copy(gidx[:, :, TILES:2 * TILES], chunked(dst))
                nc.vector.tensor_tensor(same[:], dst[:], nxt[:], ALU.is_equal).then_inc(did, 1)
                dve.wait_ge(did, 1)
                nc.vector.scalar_tensor_tensor(out=sidx[:], in0=chunked(same), scalar=float(SKIP),
                                               in1=chunked(dst), op0=ALU.mult, op1=ALU.add).then_inc(did, 1)



class EdgePass(Pass):
    def __init__(self, nc, sems, ctx, tag, keep, table, agg, ends):
        super().__init__(nc, sems, ctx, tag)
        self.keep, self.table, self.agg, self.ends = keep, table, agg, ends
        self.end_rows = self.pair(self.sb, "rows_of_ends", [ET, 4 * ends, D])
        self.gi = self.pair(self.sb, "gi", [ET, 4 * ends], I32)
        self.si = self.pair(self.sb, "si", [ET, TILES], I32)
        self.out_rows = self.pair(self.sb, "out_rows", [ET, TILES, ROW])
        self.dst = self.pair(self.sb, "dst", [128, EC], I32)
        self.prev = self.pair(self.sb, "prev", [128, EC], I32)
        self.flag = self.pair(self.sb, "same_as_before", [128, EC])
        self.gathered = self.pair(self.sem, "gathered")
        self.scattered = self.pair(self.sem, "scattered")
        self.streamed = self.pair(self.sem, "streamed")
        self.weights = self.sem("weights")
        self.passed = keep["passed"]
        self.first = self.pair(self.sb, "first", [16, 16])
        self.pe_did, self.act_did, self.dve_did, self.pool_did = (
            self.sem(s) for s in ("pe_did", "act_did", "dve_did", "pool_did"))

    def pool_program(self, gp, PE, ACTS, ahead=1, E_=E_ITERS):
        nc = self.nc
        gidx, sidx = self.keep["gather_index"], self.keep["scatter_index"]
        k = 4 * self.ends
        def after_waits():
            settled(gp, self.passed)

        def gathers(i, u, copies, first=False):
            if not first:
                gp.wait_ge(self.pe_did, PE.before("turn", i, u))
                gp.wait_ge(self.gathered[u], 16 * k * i)
                after_waits()
            nc.gpsimd.tensor_copy(self.gi[u][:], gidx[:, bass.ds(2 * i + u, 1), 0:k].rearrange(
                "p a j -> p (a j)")).then_inc(self.pool_did, 1)
            gp.wait_ge(self.pool_did, copies + (u + 1))
            after_waits()
            for j in range(k):
                gp.indirect_dma_start(self.end_rows[u][:, j, :], None, self.table,
                                      bass.IndirectOffsetOnAxis(ap=self.gi[u][:, j:j + 1], axis=0)
                                      ).then_inc(self.gathered[u], 16)

        def scatters(i, u, copies):
            gp.wait_ge(self.scattered[u], i * (16 * TILES) + 16)
            gp.wait_ge(self.act_did, ACTS.done("rows", i, u))
            after_waits()
            nc.gpsimd.tensor_copy(self.si[u][:], sidx[:, bass.ds(2 * i + u, 1), :].rearrange(
                "p a j -> p (a j)")).then_inc(self.pool_did, 1)
            gp.wait_ge(self.pool_did, copies + (u + 1))
            after_waits()
            for j in range(TILES):
                gp.indirect_dma_start(self.agg, bass.IndirectOffsetOnAxis(ap=self.si[u][:, j:j + 1], axis=0),
                                      self.out_rows[u][:, j, :], None, bounds_check=N - 1,
                                      oob_is_err=False).then_inc(self.scattered[u], 16)

        for u in EDGE_SLOTS:
            gp.dma_start(self.first[u][:], self.keep["small"]).then_inc(self.scattered[u], 16)
            gathers(0, u, 0, first=True)
        for i in range(1, ahead):
            for u in EDGE_SLOTS:
                gathers(i, u, 2 * i)
        gp.wait_ge(self.keep["filled"], 16 * FILLS)
        with gp.Fori(0, E_ - ahead) as i:
            for u in EDGE_SLOTS:
                gathers(i + ahead, u, i * 4 + 2 * ahead)
            for u in EDGE_SLOTS:
                scatters(i, u, i * 4 + (2 * ahead + 2))
        for i in range(E_ - ahead, E_):
            for u in EDGE_SLOTS:
                scatters(i, u, 2 * E_ + 2 * i)
        for u in EDGE_SLOTS:
            gp.wait_ge(self.scattered[u], 16 * TILES * E_ + 16)
        after_waits()

    def stream(self, sp, i, u, t, extra=()):
        at = 2 * i + u
        settled(sp, self.passed)
        sp.dma_start(self.dst[u][:], t["dst_rows"][bass.ds(at, 1), :].broadcast_to([128, EC])
                     ).then_inc(self.streamed[u], 16)
        sp.dma_start(self.prev[u][:], t["prev_rows"][bass.ds(at, 1), :].broadcast_to([128, EC])
                     ).then_inc(self.streamed[u], 16)
        for tile, rows, lanes in extra:
            sp.dma_start(tile, rows[bass.ds(at, 1), :].broadcast_to([lanes, EC])
                         ).then_inc(self.streamed[u], 16)

    def turn(self, pe, i, u, banks, PE):
        for end in range(self.ends):
            for j in range(TILES):
                last = self.nc.tensor.transpose(banks[end][:, j * ET:(j + 1) * ET],
                                                self.end_rows[u][:, end * TILES + j, :],
                                                self.keep["ident"][0:ET, 0:ET])
        last.then_inc(self.pe_did, 1)


def tile_of(a, j):
    return a[:, j * ET:(j + 1) * ET]



def layer0_edges(nc, sems, keep, t):
    with ExitStack() as ctx:
        p = EdgePass(nc, sems, ctx, "e0", keep, t["x"], t["agg_rows"], 2)
        ident = keep["ident"]
        lanes = 32 + H0
        low = 64
        at_slot = (slice(0, H0), slice(32, lanes))
        wq, wk, wv = (p.sb(n, [D, D]) for n in ("wq", "wk", "wv"))
        bq, bk, bv = (p.sb(n, [D, 1]) for n in ("bq", "bk", "bv"))
        heads = p.sb("heads", [D, 32])
        spread_f32 = p.sb("spread_f32", [low + lanes, 2, D])
        spread = p.sb("spread", [low + lanes, 2, D], BF16)
        wg, ident_gate = p.sb("wg", [D, 3]), p.sb("ident_gate", [D, D + 1])
        xs, xd, qs, pr, vb, part, total = (p.pair(p.sb, n, [D, EC]) for n in (
            "xs", "xd", "qs", "pr", "vb", "part", "total"))
        dst, prev = p.sb("lane_dst", [lanes, EC], I32), p.sb("lane_prev", [lanes, EC], I32)
        flag, pen = p.sb("flag", [lanes, EC]), p.sb("pen", [lanes, EC])
        m, den = p.sb("m", [lanes, EC + 1]), p.sb("den", [lanes, EC + 1])
        de, ce = p.sb("de", [lanes, 2, EC]), p.sb("ce", [lanes, 2, EC])
        rden, ratio = p.sb("rden", [lanes, EC]), p.sb("ratio", [lanes, EC])
        factors, rest = p.sb("factors", [lanes, 2, EC]), p.sb("rest", [lanes, 2, EC])
        high_parts = p.sb("high_parts", [low + lanes, 2, EC], BF16)
        low_parts = p.sb("low_parts", [lanes, 2, EC], BF16)
        T = ctx.enter_context(nc.psum_tensor("e0_T", [128, 2, 512], F32))
        Q, K, V, R = (p.bank(n) for n in ("Q", "K", "V", "R"))
        P = [p.bank(n) for n in ("P_keep", "P_share")]
        PE = Stages("back v/0", "back v/1", "front turn/0", "front qk/0", "front turn/1", "front qk/1",
                    "front logits/0", "back spread/0", "front logits/1", "back spread/1", "back rows/0",
                    "back rows/1")
        AC = Stages("back v/0", "back v/1", "back exp", "front xs/0", "front xd/0", "front q/0", "front xs/1",
                    "front xd/1", "back high", "back middle", "front q/1", "back rows/0", "back rows/1")
        DV = Stages("back flag", "back pen", "back carry/0", "back max/0", "back carry/1", "back max/1",
                    "back drop", "back differences", "back carry_den/0", "back den/0", "back carry_den/1",
                    "back den/1", "back rden", "front product/0", "back ratio", "back factors", "back rest",
                    "back low", "front product/1", "back part/0", "back total/0", "back part/1", "back total/1")
        pe_did, act_did, dve_did = p.pe_did, p.act_did, p.dve_did
        WEIGHTS = 16 * 9
        with nc.Block() as block:
            @block.sync
            def _(sp):
                for tile, dram in ((wq[:], t["L0_Wq"]), (wk[:], t["L0_Wk"]), (wv[:], t["L0_Wv"]), (bq[:], t["L0_bq"]),
                                   (bk[:], t["L0_bk"]), (bv[:], t["L0_bv"]), (heads[:], t["head_mask"]),
                                   (spread_f32[:].rearrange("k u d -> k (u d)"), t["head_spread"]),
                                   (wg[:], t["L0_Wg"])):
                    sp.dma_start(tile, dram).then_inc(p.weights, 16)
                with sp.Fori(0, E_ITERS) as i:
                    sp.wait_ge(dve_did, DV.before("flag", i))
                    settled(sp, p.passed)
                    for rows, tile in ((t["dst_rows"], dst), (t["prev_rows"], prev)):
                        sp.dma_start(tile[0:32, :], rows[bass.ds(2 * i, 1), :].broadcast_to([32, EC])
                                     ).then_inc(p.streamed[0], 16)
                        sp.dma_start(tile[32:lanes, :], rows[bass.ds(2 * i + 1, 1), :].broadcast_to([H0, EC])
                                     ).then_inc(p.streamed[0], 16)

            @block.gpsimd
            def _(gp):
                p.pool_program(gp, PE, AC, ahead=2)

            @block.tensor
            def _(pe):
                def body(back, front):
                    size = PE.sizes(back, front)

                    def spread_factors(u):
                        if back is None:
                            return
                        if u == 0:
                            pe.wait_ge(dve_did, DV.done("low", back))
                        else:
                            pe.wait_ge(dve_did, DV.done("total", back, 0))
                        for s in range(2):
                            nc.tensor.matmul(P[s][:, 0:EC], spread[:, u, :], high_parts[:, s, :],
                                             start=True, stop=False)
                            last = nc.tensor.matmul(P[s][:, 0:EC], spread[0:lanes, u, :], low_parts[:, s, :],
                                                    start=False, stop=True)
                        last.then_inc(pe_did, size("spread", u))

                    def turn(u):
                        if front is None:
                            return
                        pe.wait_ge(p.gathered[u], front * 128 + 128)
                        if u == 0:
                            if back is not None:
                                pe.wait_ge(dve_did, DV.done("differences", back))
                        else:
                            pe.wait_ge(act_did, AC.done("xd", front, 0))
                        for end in range(2):
                            for j in range(TILES):
                                last = nc.tensor.transpose(T[:, end, j * ET:(j + 1) * ET],
                                                           p.end_rows[u][:, end * TILES + j, :],
                                                           ident[0:ET, 0:ET])
                        last.then_inc(pe_did, size("turn", u))

                    def qk(u):
                        if front is None:
                            return
                        pe.wait_ge(act_did, AC.done("xd", front, u))
                        if u == 0:
                            pe.wait_ge(dve_did, DV.before("product", front, 1))
                            if back is not None:
                                settled(pe, p.passed)
                                pe.wait_ge(act_did, AC.before("rows", back, 1))
                        else:
                            pe.wait_ge(dve_did, DV.done("product", front, 0))
                        nc.tensor.matmul(Q[:, 0:EC], wq[:], xs[u][:], start=True, stop=True)
                        nc.tensor.matmul(K[:, 0:EC], wk[:], xd[u][:], start=True, stop=True
                                         ).then_inc(pe_did, size("qk", u))

                    def logits(u):
                        if front is None:
                            return
                        pe.wait_ge(dve_did, DV.done("product", front, u))
                        here = (slice(0, 32), at_slot[1])[u]
                        nc.tensor.matmul(T[here, 0, 0:EC], heads[:, 0:here.stop - here.start], pr[u][:],
                                         start=True, stop=True).then_inc(pe_did, size("logits", u))

                    def v(u):
                        if back is None:
                            return
                        pe.wait_ge(act_did, AC.before("v", back, 1) if u == 0 else AC.done("v", back, 0))
                        nc.tensor.matmul(V[:, 0:EC], wv[:], xs[u][:], start=True, stop=True
                                         ).then_inc(pe_did, size("v", u))

                    def rows(u):
                        if back is None:
                            return
                        pe.wait_ge(dve_did, DV.done("total", back, u))
                        pe.wait_ge(act_did, AC.before("rows", back, 1) if u == 0 else AC.done("rows", back, 0))
                        if front is not None:
                            settled(pe, p.passed)
                            pe.wait_ge(act_did, AC.done("q", front, 1))
                        for j in range(TILES):
                            bank, at = (R, j * (D + 1)) if j < 3 else (Q, 0)
                            last = nc.tensor.matmul(bank[0:ET, at:at + D + 1], tile_of(total[u], j), ident_gate[:],
                                                    start=True, stop=True)
                        last.then_inc(pe_did, size("rows", u))

                    v(0)
                    v(1)
                    turn(0)
                    qk(0)
                    turn(1)
                    qk(1)
                    logits(0)
                    spread_factors(0)
                    logits(1)
                    spread_factors(1)
                    rows(0)
                    rows(1)
                    if back is None:
                        pe.wait_ge(pe_did, PE.done("logits", front, 1))
                        pe.sem_inc(pe_did, PE.left(back, front))

                pe.sem_inc(pe_did, PE.per_iteration)
                pe.wait_ge(p.weights, WEIGHTS)
                pe.wait_ge(dve_did, DV.per_iteration)
                bodies(pe, E_ITERS, body)

            @block.scalar
            def _(act):
                def body(back, front):
                    size = AC.sizes(back, front)

                    def ends(u):
                        if front is None:
                            return
                        act.wait_ge(pe_did, PE.done("turn", front, u))
                        nc.scalar.activation(xs[u][:], T[:, 0, 0:EC], ACT.Copy).then_inc(act_did, size("xs", u))
                        nc.scalar.activation(xd[u][:], T[:, 1, 0:EC], ACT.Copy).then_inc(act_did, size("xd", u))

                    def q(u):
                        if front is None:
                            return
                        act.wait_ge(pe_did, PE.done("qk", front, u))
                        act.wait_ge(dve_did, DV.before("product", front, u))
                        nc.scalar.activation(qs[u][:], Q[:, 0:EC], ACT.Identity, bias=bq[:]
                                             ).then_inc(act_did, size("q", u))

                    def v(u):
                        if back is None:
                            return
                        act.wait_ge(pe_did, PE.done("v", back, u))
                        act.wait_ge(dve_did, DV.before("part", back, u))
                        nc.scalar.activation(vb[u][:], V[:, 0:EC], ACT.Identity, bias=bv[:]
                                             ).then_inc(act_did, size("v", u))

                    def rows(u):
                        if back is None:
                            return
                        act.wait_ge(pe_did, PE.done("rows", back, u))
                        act.wait_ge(p.scattered[u], back * 64 + 16)
                        nc.scalar.activation(p.out_rows[u][:, 0:3, 0:D + 1], R[0:ET, 0:3 * (D + 1)].rearrange(
                            "p (j d) -> p j d", j=3), ACT.Copy)
                        nc.scalar.activation(p.out_rows[u][:, 3, 0:D + 1], Q[0:ET, 0:D + 1], ACT.Copy
                                             ).then_inc(act_did, size("rows", u))

                    v(0)
                    v(1)
                    if back is not None:
                        act.wait_ge(dve_did, DV.done("differences", back))
                        nc.scalar.activation(ce[:], de[:], ACT.Exp).then_inc(act_did, size("exp"))
                    ends(0)
                    q(0)
                    ends(1)
                    if back is not None:
                        act.wait_ge(dve_did, DV.done("factors", back))
                        act.wait_ge(pe_did, PE.before("spread", back, 1))
                        nc.scalar.activation(high_parts[0:lanes], factors[:], ACT.Copy
                                             ).then_inc(act_did, size("high"))
                        act.wait_ge(dve_did, DV.done("rest", back))
                        nc.scalar.activation(high_parts[low:low + lanes], rest[:], ACT.Copy
                                             ).then_inc(act_did, size("middle"))
                    q(1)
                    rows(0)
                    rows(1)
                    if back is None:
                        act.wait_ge(act_did, AC.done("q", front, 1))
                        act.sem_inc(act_did, AC.left(back, front))

                act.sem_inc(act_did, AC.per_iteration)
                act.wait_ge(p.weights, WEIGHTS)
                bodies(act, E_ITERS, body)

            @block.vector
            def _(dve):
                def body(back, front):
                    size = DV.sizes(back, front)

                    def summed(u):
                        if back is None:
                            return
                        dve.wait_ge(pe_did, PE.done("spread", back, u))
                        dve.wait_ge(act_did, AC.done("v", back, u))
                        nc.vector.tensor_tensor(part[u][:], vb[u][:], P[1][:, 0:EC], ALU.mult
                                                ).then_inc(dve_did, size("part", u))
                        dve.wait_ge(dve_did, DV.done("part", back, u))
                        dve.wait_ge(pe_did, PE.before("rows", back, u))
                        nc.vector.tensor_tensor_scan(total[u][:], P[0][:, 0:EC], part[u][:],
                                                     total[1 - u][:, EC - 1:EC], ALU.mult, ALU.add
                                                     ).then_inc(dve_did, size("total", u))

                    def product(u):
                        if front is None:
                            return
                        dve.wait_ge(act_did, AC.done("q", front, u))
                        dve.wait_ge(pe_did, PE.before("logits", front, u))
                        nc.vector.scalar_tensor_tensor(out=pr[u][:], in0=K[:, 0:EC], scalar=bk[:], in1=qs[u][:],
                                                       op0=ALU.add, op1=ALU.mult).then_inc(dve_did, size("product", u))

                    if back is not None:
                        dve.wait_ge(p.streamed[0], back * 64 + 64)
                        nc.vector.tensor_tensor(flag[:], dst[:], prev[:], ALU.is_equal).then_inc(dve_did, size("flag"))
                        dve.wait_ge(dve_did, DV.done("flag", back))
                        nc.vector.tensor_scalar(pen[:], flag[:], FAR, -FAR, ALU.mult, ALU.add
                                                ).then_inc(dve_did, size("pen"))
                        dve.wait_ge(pe_did, PE.done("logits", back, 1))
                        for u in EDGE_SLOTS:
                            here, other = at_slot[u], at_slot[1 - u]
                            dve.wait_ge(dve_did, DV.before("max", back, 1) if u == 0 else DV.done("max", back, 0))
                            nc.vector.tensor_copy(m[here, 0:1], m[other, EC:EC + 1]).then_inc(dve_did, size("carry", u))
                            dve.wait_ge(dve_did, DV.done("carry", back, u))
                            nc.vector.tensor_tensor_scan(m[here, 1:EC + 1], pen[here, :], T[here, 0, 0:EC], m[here, 0:1],
                                                         ALU.add, ALU.max).then_inc(dve_did, size("max", u))
                        dve.wait_ge(dve_did, DV.done("max", back, 1))
                        nc.vector.tensor_tensor(de[:, 0, :], m[:, 0:EC], m[:, 1:EC + 1], ALU.subtract
                                                ).then_inc(dve_did, size("drop"))
                        dve.wait_ge(dve_did, DV.done("drop", back))
                        nc.vector.tensor_tensor(de[:, 0, :], de[:, 0, :], pen[:], ALU.add)
                        nc.vector.tensor_tensor(de[:, 1, :], T[0:lanes, 0, 0:EC], m[:, 1:EC + 1], ALU.subtract
                                                ).then_inc(dve_did, size("differences"))
                        dve.wait_ge(act_did, AC.done("exp", back))
                        for u in EDGE_SLOTS:
                            here, other = at_slot[u], at_slot[1 - u]
                            dve.wait_ge(dve_did, DV.before("den", back, 1) if u == 0 else DV.done("den", back, 0))
                            nc.vector.tensor_copy(den[here, 0:1], den[other, EC:EC + 1]
                                                  ).then_inc(dve_did, size("carry_den", u))
                            dve.wait_ge(dve_did, DV.done("carry_den", back, u))
                            nc.vector.tensor_tensor_scan(den[here, 1:EC + 1], ce[here, 0, :], ce[here, 1, :],
                                                         den[here, 0:1], ALU.mult, ALU.add).then_inc(dve_did, size("den", u))
                        dve.wait_ge(dve_did, DV.done("den", back, 1))
                        nc.vector.reciprocal(rden[:], den[:, 1:EC + 1]).then_inc(dve_did, size("rden"))
                    product(0)
                    if back is not None:
                        dve.wait_ge(dve_did, DV.done("rden", back))
                        nc.vector.tensor_tensor(ratio[:], rden[:], den[:, 0:EC], ALU.mult).then_inc(dve_did, size("ratio"))
                        nc.vector.tensor_tensor(factors[:, 1, :], ce[:, 1, :], rden[:], ALU.mult)
                        dve.wait_ge(dve_did, DV.done("ratio", back))
                        nc.vector.tensor_tensor(factors[:, 0, :], ce[:, 0, :], ratio[:], ALU.mult
                                                ).then_inc(dve_did, size("factors"))
                        dve.wait_ge(act_did, AC.done("high", back))
                        nc.vector.tensor_tensor(rest[:], factors[:], high_parts[0:lanes], ALU.subtract
                                                ).then_inc(dve_did, size("rest"))
                        dve.wait_ge(act_did, AC.done("middle", back))
                        nc.vector.tensor_tensor(low_parts[:], rest[:], high_parts[low:low + lanes], ALU.subtract
                                                ).then_inc(dve_did, size("low"))
                    product(1)
                    summed(0)
                    summed(1)
                    if back is None:
                        dve.wait_ge(dve_did, DV.done("product", front, 1))
                        dve.sem_inc(dve_did, DV.left(back, front))

                for u in EDGE_SLOTS:
                    nc.vector.memset(p.out_rows[u][:], 0.0)
                nc.vector.memset(m[:], 0.0)
                nc.vector.memset(den[:], 1.0)
                nc.vector.memset(high_parts[:], 0.0)
                dve.wait_ge(p.weights, WEIGHTS)
                nc.vector.tensor_copy(spread[:], spread_f32[:])
                nc.vector.tensor_copy(ident_gate[:, 0:D], ident[:])
                nc.vector.tensor_tensor(ident_gate[:, D:D + 1], wg[:, 1:2], wg[:, 2:3], ALU.subtract)
                nc.vector.memset(total[1][:], 0.0).then_inc(dve_did, DV.per_iteration)
                bodies(dve, E_ITERS, body)



class NodePass(Pass):

    slots = NODE_SLOTS

    def __init__(self, nc, sems, ctx, tag, keep, dram_in, dram_agg, dram_out, dram_residual=None, buffers=2):
        super().__init__(nc, sems, ctx, tag)
        self.keep, self.dram_in, self.dram_agg, self.dram_out = keep, dram_in, dram_agg, dram_out
        self.dram_residual = dram_residual
        self.rows, self.sums, self.loaded = ([self.pair(make, f"{name}{b}_", *shape) for b in range(buffers)]
                                             for make, name, shape in ((self.sb, "rows", ([128, 4, D],)),
                                                                       (self.sb, "sums", ([128, 4, ROW],)),
                                                                       (self.sem, "loaded", ())))
        if dram_residual is not None:
            self.residual = self.pair(self.sb, "residual", [128, 4, D])
            self.residual_loaded = self.pair(self.sem, "residual_loaded")
        self.out = self.pair(self.sb, "out", [128, 4, D])
        self.stored = keep["stored"]
        self.stored_before = keep["stored_before"].pop()
        keep["stored_before"].append(self.stored_before + 16 * N_ITERS + 16)
        self.per_load = 16 * 2
        self.weights = self.sem("weights")
        self.passed = keep["passed"]
        self.first = self.pair(self.sb, "first", [16, 16])
        self.pe_did, self.act_did, self.dve_did, self.pool_did = (
            self.sem(s) for s in ("pe_did", "act_did", "dve_did", "pool_did"))
        self.stats = self.pair(self.sb, "stats", [128, 4, 6])
        self.moments = self.pair(self.sb, "moments", [128, 4, 2])
        self.shift = self.pair(self.sb, "shift", [128, 4])
        self.eps, self.dummy = self.sb("eps", [128, 1]), self.sb("dummy", [128, 1])
        self.std = self.pair(self.sb, "std", [128, 4])
        self.rstd = self.pair(self.sb, "rstd", [128, 4])

    def stores(self, i):
        return i * 16 + (self.stored_before + 16)

    def load(self, sp, i, slots, buffer=0):
        for u in slots:
            sp.dma_start(self.rows[buffer][u][:], as_rows(self.dram_in, i, u)).then_inc(self.loaded[buffer][u], 16)
            sp.dma_start(self.sums[buffer][u][:], as_rows(self.dram_agg, i, u)).then_inc(self.loaded[buffer][u], 16)

    def load_residual(self, sp, i, slots, free=None):
        for u in slots if self.dram_residual is not None else ():
            if free:
                free(i, u)
            sp.dma_start(self.residual[u][:], as_rows(self.dram_residual, i, u)
                         ).then_inc(self.residual_loaded[u], 16)

    def store(self, sp, i, slots, filled):
        for u in slots:
            filled(i, u)
            settled(sp, self.passed)
            sp.dma_start(as_rows(self.dram_out, i, u), self.out[u][:]).then_inc(self.stored[u], 16)

    def first_loads(self, sp):
        for u in NODE_SLOTS:
            sp.dma_start(self.first[u][:], self.keep["small"]).then_inc(self.stored[u], 16)
            for buffer in range(len(self.rows)):
                self.load(sp, buffer, (u,), buffer)
            self.load_residual(sp, 0, (u,))

    def all_stored(self, sp):
        for u in NODE_SLOTS:
            sp.wait_ge(self.stored[u], self.stores(N_ITERS))

    def sync_program(self, sp, free, filled):
        self.first_loads(sp)
        with sp.Fori(0, N_ITERS - 1) as i:
            for u in NODE_SLOTS:
                free(i + 1, u)
                self.load(sp, i + 1, (u,))
            self.store(sp, i, NODE_SLOTS, filled)
        self.store(sp, N_ITERS - 1, NODE_SLOTS, filled)
        self.all_stored(sp)

    def sync_halves(self, sp, free, filled, residual_free=None, early_stored="front"):
        def load(front, slots):
            for u in slots:
                free(front + 1, u)
                self.load(sp, front + 2, (u,), front.buffer)

        def body(back, front, loads=True):
            if front is not None and loads:
                load(front, EARLY)
            if back is not None:
                if front is not None:
                    self.load_residual(sp, front, LATE, residual_free)
                self.store(sp, back, LATE if early_stored == "front" else EARLY, filled)
            if front is not None:
                if loads:
                    load(front, LATE)
                if loads or front.number != N_ITERS - 1:
                    self.load_residual(sp, front + 1, EARLY, residual_free)
                if early_stored == "front":
                    self.store(sp, front, EARLY, filled)
            if back is not None and early_stored == "back":
                self.store(sp, back, LATE, filled)

        pairs = N_ITERS // 2
        self.first_loads(sp)
        body(None, Iteration(0, 0, 1))
        with sp.Fori(0, pairs - 1) as k:
            body(Iteration(2 * k, 0, k + 1), Iteration(2 * k + 1, 1, k + 1))
            body(Iteration(2 * k + 1, 1, k + 1), Iteration(2 * k + 2, 0, k + 2))
        body(Iteration(N_ITERS - 3, 0, pairs), Iteration(N_ITERS - 2, 1, pairs), loads=False)
        body(Iteration(N_ITERS - 2, 1, pairs), Iteration(N_ITERS - 1, 0, pairs + 1), loads=False)
        body(Iteration(N_ITERS - 1, 0, pairs + 1), None)
        self.all_stored(sp)

    def turn(self, bank, a, size=1):
        for j in range(4):
            last = self.nc.tensor.transpose(bank[:, j * D:(j + 1) * D], a[:, j, :],
                                            self.keep["ident"][:])
        last.then_inc(self.pe_did, size)

    def sqrt_table(self, act):
        self.nc.scalar.activation(self.dummy[:], self.eps[:], ACT.Sqrt)


    def norm_stats(self, dve, i, slots, x, k, size, ready):
        for u in slots if i is not None else ():
            ready(i, u)
            for j in range(4):
                last = self.nc.vector.bn_stats(self.stats[u][:, j, :], x[u][:, j, :])
            last.then_inc(self.dve_did, size(f"{k}_stats", u))

    def norm_moments(self, dve, i, slots, V, k, size):
        for u in slots if i is not None else ():
            dve.wait_ge(self.dve_did, V.done(f"{k}_stats", i, u))
            settled(dve, self.passed)
            for j in range(4):
                last = self.nc.vector.bn_aggr(self.moments[u][:, j, :], self.stats[u][:, j, :])
            last.then_inc(self.dve_did, size(f"{k}_moments", u))

    def norm_std(self, act, i, slots, V, k, size):
        for u in slots if i is not None else ():
            act.wait_ge(self.dve_did, V.done(f"{k}_moments", i, u))
            self.nc.scalar.activation(self.std[u][:], self.moments[u][:, :, 1], ACT.Sqrt, bias=self.eps[:]
                                      ).then_inc(self.act_did, size(f"{k}_std", u))

    def norm_rstd(self, dve, i, slots, A, k, size):
        for u in slots if i is not None else ():
            dve.wait_ge(self.act_did, A.done(f"{k}_std", i, u))
            self.nc.vector.reciprocal(self.rstd[u][:], self.std[u][:]).then_inc(self.dve_did, size(f"{k}_rstd", u))

    def norm_apply_dve(self, dve, i, slots, x, y, V, k, size, free):
        for u in slots if i is not None else ():
            dve.wait_ge(self.dve_did, V.done(f"{k}_rstd", i, u))
            free(i, u)
            for j in range(4):
                last = self.nc.vector.tensor_scalar(y[u][:, j, :], x[u][:, j, :], self.moments[u][:, j, 0:1],
                                                    self.rstd[u][:, j:j + 1], ALU.subtract, ALU.mult)
            last.then_inc(self.dve_did, size(f"{k}_apply", u))

    def norm_shift(self, dve, i, slots, V, k, size):
        for u in slots if i is not None else ():
            dve.wait_ge(self.dve_did, V.done(f"{k}_rstd", i, u))
            self.nc.vector.scalar_tensor_tensor(out=self.shift[u][:], in0=self.moments[u][:, :, 0], scalar=-1.0,
                                                in1=self.rstd[u][:], op0=ALU.mult, op1=ALU.mult
                                                ).then_inc(self.dve_did, size(f"{k}_shift", u))

    def norm_apply_act(self, act, i, slots, x, y, V, k, size, free):
        for u in slots if i is not None else ():
            act.wait_ge(self.dve_did, V.done(f"{k}_shift", i, u))
            free(i, u)
            for j in range(4):
                last = self.nc.scalar.activation(y[u][:, j, :], x[u][:, j, :], ACT.Identity,
                                                 bias=self.shift[u][:, j:j + 1], scale=self.rstd[u][:, j:j + 1])
            last.then_inc(self.act_did, size(f"{k}_apply", u))


def four(row):
    return row.broadcast_to([128, D])


def each_tile(a):
    return a[:].rearrange("p (a d) -> p a d", a=1).broadcast_to([128, 4, D])


def flat(a):
    return a[:].rearrange("p j d -> p (j d)")


def tiles(bank):
    return bank[:].rearrange("p (j d) -> p j d", d=D)



def layer0_nodes(nc, sems, keep, t):
    with ExitStack() as ctx:
        p = NodePass(nc, sems, ctx, "n0", keep, t["x"], t["agg_rows"], t["x1"])
        ws, wst = p.sb("ws", [D, D + 1]), p.sb("wst", [D, D])
        wg = p.sb("wg", [D, 3])
        bs_one, bs_col = p.sb("bs_one", [D, 1]), p.sb("bs_col", [D, 128])
        bs = p.sb("bs", [128, D])
        gamma, beta = p.sb("gamma", [D, 1]), p.sb("beta", [D, 1])
        alpha, bg, rest = (p.sb(n, [128, 1]) for n in ("alpha", "bg", "rest"))
        slope_gamma, slope_beta = p.sb("slope_gamma", [D, 1]), p.sb("slope_beta", [D, 1])
        gate_skip, off = p.sb("gate_skip", [D, 1]), p.sb("off", [128, 1])
        less, gap, mix, nrm, res = (p.pair(p.sb, n, [128, 4, D]) for n in ("less", "gap", "mix", "nrm", "res"))
        xt, aff, pos = (p.pair(p.sb, n, [D, NC_]) for n in ("xt", "aff", "pos"))
        leaky = p.pair(p.sb, "leaky", [D, 4, 128])
        z, ez, ez1, g = (p.pair(p.sb, n, [128, 4]) for n in ("z", "ez", "ez1", "g"))
        A, B = p.pair(p.bank, "A"), p.pair(p.bank, "B")
        setup_did = p.sem("setup_did")
        PE = Stages(*halves("turn E", "skip E", "turn_normed L", "turn_back L"))
        AC = Stages(*halves("xt E", "in_apply L", "exp E", "affine L", "out_std L", "in_std E"))
        DV = Stages(*halves("z E", "gap E", "ez1 E", "g E", "mix E", "leaky L", "res L", "out_stats L",
                            "out_moments L", "in_stats E", "in_moments E", "out_rstd L", "out_apply L", "in_rstd E",
                            "in_shift E"))
        PO = Stages(*halves("less E"))
        pe_did, act_did, dve_did, pool_did = p.pe_did, p.act_did, p.dve_did, p.pool_did
        WEIGHTS = 16 * 9
        with nc.Block() as block:
            @block.sync
            def _(sp):
                for tile, dram in ((ws[:, 0:D], t["L0_Ws"]), (wst[:], t["L0_Ws_turned"]), (wg[:], t["L0_Wg"]),
                                   (bs_one[:], t["L0_bs"]),
                                   (bs[:], four(t["L0_bs_row"])),
                                   (gamma[:], t["L0_gamma"]), (beta[:], t["L0_beta"]),
                                   (alpha[:], t["L0_alpha"].broadcast_to([128, 1])),
                                   (bg[:], t["L0_bg"].broadcast_to([128, 1]))):
                    sp.dma_start(tile, dram).then_inc(p.weights, 16)

                def free(i, u):
                    sp.wait_ge(dve_did, DV.before("res", i, u))
                    settled(sp, p.passed)
                    sp.wait_ge(pe_did, PE.before("turn", i, u))
                    settled(sp, p.passed)
                    sp.wait_ge(pool_did, PO.before("less", i, u))
                    settled(sp, p.passed)

                p.sync_halves(sp, free, lambda i, u: sp.wait_ge(dve_did, DV.done("out_apply", i, u)))

            @block.gpsimd
            def _(gp):
                def less_bias(i, slots, size):
                    for u in slots if i is not None else ():
                        gp.wait_ge(p.loaded[i.buffer][u], i.loads * p.per_load)
                        gp.wait_ge(dve_did, DV.before("gap", i, u))
                        nc.gpsimd.tensor_tensor(less[u][:], p.sums[i.buffer][u][:, :, 0:D], each_tile(bs), ALU.subtract
                                                ).then_inc(pool_did, size("less", u))

                def body(back, front):
                    size = PO.sizes(back, front)
                    less_bias(front, EARLY, size)
                    less_bias(front, LATE, size)

                gp.sem_inc(pool_did, PO.per_iteration)
                gp.wait_ge(p.weights, WEIGHTS)
                buffered_bodies(gp, N_ITERS, body)

            @block.tensor
            def _(pe):
                def turn(i, slots, size):
                    for u in slots if i is not None else ():
                        pe.wait_ge(p.loaded[i.buffer][u], i.loads * p.per_load)
                        pe.wait_ge(act_did, AC.before("affine", i, u))
                        p.turn(A[u], p.rows[i.buffer][u], size("turn", u))

                def skip(i, slots, size):
                    for u in slots if i is not None else ():
                        pe.wait_ge(act_did, AC.done("xt", i, u))
                        pe.wait_ge(dve_did, DV.before("res", i, u))
                        for j in range(4):
                            bank, at = (B[u], j * (D + 1)) if j < 3 else (A[u], 0)
                            last = nc.tensor.matmul(bank[:, at:at + D + 1], xt[u][:, j * D:(j + 1) * D], ws[:],
                                                    start=True, stop=True)
                        last.then_inc(pe_did, size("skip", u))

                def turn_normed(i, slots, size):
                    for u in slots if i is not None else ():
                        pe.wait_ge(act_did, AC.done("in_apply", i, u))
                        p.turn(A[u], nrm[u], size("turn_normed", u))

                def turn_back(i, slots, size):
                    for u in slots if i is not None else ():
                        pe.wait_ge(dve_did, DV.done("leaky", i, u))
                        p.turn(B[u], leaky[u], size("turn_back", u))

                def half(i_early, early, i_late, late, size):
                    turn(i_early, early, size)
                    skip(i_early, early, size)
                    turn_normed(i_late, late, size)
                    turn_back(i_late, late, size)

                def body(back, front):
                    size = PE.sizes(back, front)
                    half(front, EARLY, back, LATE, size)
                    half(front, LATE, front, EARLY, size)

                pe.sem_inc(pe_did, PE.per_iteration)
                pe.wait_ge(p.weights, WEIGHTS)
                pe.wait_ge(setup_did, 2)
                nc.tensor.matmul(A[0][:, 8:9], wst[:], gate_skip[:], start=True, stop=True)
                nc.tensor.matmul(A[0][:, 9:10], bs_col[:], gate_skip[:], start=True, stop=True
                                 ).then_inc(setup_did, 1)
                pe.wait_ge(setup_did, 5)
                buffered_bodies(pe, N_ITERS, body)

            @block.scalar
            def _(act):
                def copy_xt(i, slots, size):
                    for u in slots if i is not None else ():
                        act.wait_ge(pe_did, PE.done("turn", i, u))
                        nc.scalar.activation(xt[u][:], A[u][:], ACT.Copy).then_inc(act_did, size("xt", u))

                def exp(i, slots, size):
                    for u in slots if i is not None else ():
                        act.wait_ge(dve_did, DV.done("z", i, u))
                        nc.scalar.activation(ez[u][:], z[u][:], ACT.Exp, bias=off[:], scale=-1.0
                                             ).then_inc(act_did, size("exp", u))

                def affine(i, slots, size):
                    for u in slots if i is not None else ():
                        act.wait_ge(pe_did, PE.done("turn_normed", i, u))
                        act.wait_ge(dve_did, DV.before("leaky", i, u))
                        nc.scalar.activation(aff[u][:], A[u][:], ACT.Identity, bias=slope_beta[:],
                                             scale=slope_gamma[:])
                        nc.scalar.activation(pos[u][:], A[u][:], ACT.Relu, bias=beta[:], scale=gamma[:]
                                             ).then_inc(act_did, size("affine", u))

                def in_apply(i, slots, size):
                    p.norm_apply_act(act, i, slots, mix, nrm, DV, "in", size,
                                     lambda i, u: act.wait_ge(pe_did, PE.before("turn_normed", i, u)))

                def half(i_early, early, i_late, late, size):
                    copy_xt(i_early, early, size)
                    in_apply(i_late, late, size)
                    exp(i_early, early, size)
                    affine(i_late, late, size)
                    p.norm_std(act, i_late, late, DV, "out", size)
                    p.norm_std(act, i_early, early, DV, "in", size)

                def body(back, front):
                    size = AC.sizes(back, front)
                    half(front, EARLY, back, LATE, size)
                    half(front, LATE, front, EARLY, size)

                act.sem_inc(act_did, AC.per_iteration)
                act.wait_ge(setup_did, 5)
                act.wait_ge(dve_did, DV.per_iteration)
                buffered_bodies(act, N_ITERS, body)

            @block.vector
            def _(dve):
                def skipped(bank):
                    return bank[:, 0:3 * (D + 1)].rearrange("p (j d) -> p j d", j=3)

                def leaky_relu(i, slots, size):
                    for u in slots if i is not None else ():
                        dve.wait_ge(act_did, AC.done("affine", i, u))
                        dve.wait_ge(pe_did, PE.before("turn_back", i, u))
                        nc.vector.scalar_tensor_tensor(out=leaky[u][:].rearrange("p j d -> p (j d)"), in0=pos[u][:],
                                                       scalar=rest[:], in1=aff[u][:], op0=ALU.mult, op1=ALU.add
                                                       ).then_inc(dve_did, size("leaky", u))

                def add_residual(i, slots, size):
                    for u in slots if i is not None else ():
                        dve.wait_ge(pe_did, PE.done("turn_back", i, u))
                        nc.vector.tensor_tensor(res[u][:], tiles(B[u]), p.rows[i.buffer][u][:], ALU.add
                                                ).then_inc(dve_did, size("res", u))

                def mixed(i, slots, size):
                    for u in slots if i is not None else ():
                        dve.wait_ge(p.loaded[i.buffer][u], i.loads * p.per_load)
                        dve.wait_ge(pe_did, PE.done("skip", i, u))
                        dve.wait_ge(act_did, AC.before("exp", i, u))
                        nc.vector.tensor_tensor(z[u][:, 0:3], skipped(B[u])[:, :, D], p.sums[i.buffer][u][:, 0:3, D], ALU.add)
                        nc.vector.tensor_tensor(z[u][:, 3:4], A[u][:, D:D + 1], p.sums[i.buffer][u][:, 3, D:D + 1], ALU.add
                                                ).then_inc(dve_did, size("z", u))
                    for u in slots if i is not None else ():
                        dve.wait_ge(pool_did, PO.done("less", i, u))
                        nc.vector.tensor_tensor(gap[u][:, 0:3, :], skipped(B[u])[:, :, 0:D], less[u][:, 0:3, :],
                                                ALU.subtract)
                        nc.vector.tensor_tensor(gap[u][:, 3, :], A[u][:, 0:D], less[u][:, 3, :], ALU.subtract
                                                ).then_inc(dve_did, size("gap", u))
                    for u in slots if i is not None else ():
                        dve.wait_ge(act_did, AC.done("exp", i, u))
                        nc.vector.tensor_scalar(ez1[u][:], ez[u][:], 1.0, None, ALU.add
                                                ).then_inc(dve_did, size("ez1", u))
                    for u in slots if i is not None else ():
                        dve.wait_ge(dve_did, DV.done("ez1", i, u))
                        nc.vector.reciprocal(g[u][:], ez1[u][:]).then_inc(dve_did, size("g", u))
                    for u in slots if i is not None else ():
                        dve.wait_ge(dve_did, DV.done("g", i, u))
                        dve.wait_ge(act_did, AC.before("in_apply", i, u))
                        for j in range(4):
                            last = nc.vector.scalar_tensor_tensor(
                                out=mix[u][:, j, :], in0=gap[u][:, j, :], scalar=g[u][:, j:j + 1],
                                in1=p.sums[i.buffer][u][:, j, 0:D], op0=ALU.mult, op1=ALU.add)
                        last.then_inc(dve_did, size("mix", u))

                def half(i_early, early, i_late, late, size):
                    mixed(i_early, early, size)
                    leaky_relu(i_late, late, size)
                    add_residual(i_late, late, size)
                    p.norm_stats(dve, i_late, late, res, "out", size,
                                 lambda i, u: dve.wait_ge(dve_did, DV.done("res", i, u)))
                    p.norm_moments(dve, i_late, late, DV, "out", size)
                    p.norm_stats(dve, i_early, early, mix, "in", size,
                                 lambda i, u: dve.wait_ge(dve_did, DV.done("mix", i, u)))
                    p.norm_moments(dve, i_early, early, DV, "in", size)
                    p.norm_rstd(dve, i_late, late, AC, "out", size)
                    p.norm_apply_dve(dve, i_late, late, res, p.out, DV, "out", size,
                                     lambda i, u: dve.wait_ge(p.stored[u], p.stores(i)))
                    p.norm_rstd(dve, i_early, early, AC, "in", size)
                    p.norm_shift(dve, i_early, early, DV, "in", size)

                def body(back, front):
                    size = DV.sizes(back, front)
                    half(front, EARLY, back, LATE, size)
                    half(front, LATE, front, EARLY, size)

                dve.wait_ge(p.weights, WEIGHTS)
                nc.vector.tensor_scalar(rest[:], alpha[:], -1.0, 1.0, ALU.mult, ALU.add).then_inc(setup_did, 1)
                nc.vector.tensor_copy(bs_col[:], bs_one[:].broadcast_to([D, 128]))
                nc.vector.tensor_tensor(slope_gamma[:], gamma[:], alpha[:], ALU.mult)
                nc.vector.tensor_tensor(slope_beta[:], beta[:], alpha[:], ALU.mult)
                nc.vector.tensor_tensor(gate_skip[:], wg[:, 0:1], wg[:, 2:3], ALU.add).then_inc(setup_did, 1)
                dve.wait_ge(setup_did, 3)
                nc.vector.tensor_copy(ws[:, D:D + 1], A[0][:, 8:9]).then_inc(setup_did, 1)
                nc.vector.scalar_tensor_tensor(out=off[:], in0=A[0][:, 9:10], scalar=-1.0, in1=bg[:],
                                               op0=ALU.mult, op1=ALU.subtract).then_inc(setup_did, 1)
                nc.vector.memset(p.eps[:], EPS).then_inc(dve_did, DV.per_iteration)
                buffered_bodies(dve, N_ITERS, body)



def layer1_edges(nc, sems, keep, t, l, table):
    with ExitStack() as ctx:
        p = EdgePass(nc, sems, ctx, f"e1{l}", keep, table, t["agg_rows"], 2)
        w_dst, w_src, w2, w_agg = (p.sb(n, [D, D]) for n in ("w_dst", "w_src", "w2", "w_agg"))
        w_edge = p.sb("w_edge", [1, D])
        b1, b2 = p.sb("b1", [D, 1]), p.sb("b2", [D, 1])
        ones = p.sb("ones", [128, EC])
        weight = p.pair(p.sb, "weight", [1, EC])
        xs, xd, m1, m2, count, share, total, mean = (p.pair(p.sb, n, [D, EC]) for n in (
            "xs", "xd", "m1", "m2", "count", "share", "total", "mean"))
        A, B, C = (p.pair(p.bank, n) for n in "ABC")
        PE = Steps("turn", "m1", "m2", "rows", slots=EDGE_SLOTS)
        AC = Steps("xs", "m1", "m2", "rows", slots=EDGE_SLOTS)
        DV = Steps("flag", "xd", "count/0", "count/1", "share", "total/0", "total/1", "mean", slots=EDGE_SLOTS)
        pe_did, act_did, dve_did = p.pe_did, p.act_did, p.dve_did
        WEIGHTS = 16 * 7
        with nc.Block() as block:
            @block.sync
            def _(sp):
                for tile, dram in ((w_dst, t["L1_ew1"][l, 0:D, :]), (w_src, t["L1_ew1"][l, D:2 * D, :]),
                                   (w_edge, t["L1_ew1"][l, 2 * D:2 * D + 1, :]), (w2, t["L1_ew2"][l, :, :]),
                                   (w_agg, t["L1_nw1"][l, D:2 * D, :]), (b1, t["L1_eb1"][l, :, :]),
                                   (b2, t["L1_eb2"][l, :, :])):
                    sp.dma_start(tile[:], dram).then_inc(p.weights, 16)
                with sp.Fori(0, E_ITERS) as i:
                    for u in EDGE_SLOTS:
                        sp.wait_ge(pe_did, PE.before("m1", i, u))
                        settled(sp, p.passed)
                        sp.wait_ge(dve_did, DV.before("flag", i, u))
                        p.stream(sp, i, u, t, [(weight[u][:], t["edge_weight_rows"], 1)])

            @block.gpsimd
            def _(gp):
                p.pool_program(gp, PE, AC, ahead=2)

            @block.tensor
            def _(pe):
                pe.sem_inc(pe_did, PE.per_iteration)
                pe.wait_ge(p.weights, WEIGHTS)
                with pe.Fori(0, E_ITERS) as i:
                    for u in EDGE_SLOTS:
                        pe.wait_ge(p.gathered[u], i * 128 + 128)
                        pe.wait_ge(act_did, AC.before("rows", i, u))
                        p.turn(pe, i, u, (A[u], B[u]), PE)
                    for u in EDGE_SLOTS:
                        pe.wait_ge(p.streamed[u], i * 48 + 48)
                        pe.wait_ge(act_did, AC.done("xs", i, u))
                        pe.wait_ge(dve_did, DV.done("xd", i, u))
                        nc.tensor.matmul(C[u][:, 0:EC], w_edge[:], weight[u][:], start=True, stop=False)
                        nc.tensor.matmul(C[u][:, 0:EC], w_src[:], xs[u][:], start=False, stop=False)
                        nc.tensor.matmul(C[u][:, 0:EC], w_dst[:], xd[u][:], start=False, stop=True
                                         ).then_inc(pe_did, 1)
                    for u in EDGE_SLOTS:
                        pe.wait_ge(act_did, AC.done("m1", i, u))
                        nc.tensor.matmul(A[u][:, 0:EC], w2[:], m1[u][:], start=True, stop=True
                                         ).then_inc(pe_did, 1)
                    for u in EDGE_SLOTS:
                        pe.wait_ge(dve_did, DV.done("mean", i, u))
                        for j in range(TILES):
                            last = nc.tensor.matmul(B[u][0:ET, j * D:(j + 1) * D], tile_of(mean[u], j), w_agg[:],
                                                    start=True, stop=True)
                        last.then_inc(pe_did, 1)

            @block.scalar
            def _(act):
                act.sem_inc(act_did, AC.per_iteration)
                act.wait_ge(p.weights, WEIGHTS)
                with act.Fori(0, E_ITERS) as i:
                    for u in EDGE_SLOTS:
                        act.wait_ge(pe_did, PE.done("turn", i, u))
                        nc.scalar.activation(xs[u][:], A[u][:, 0:EC], ACT.Copy).then_inc(act_did, 1)
                    for u in EDGE_SLOTS:
                        act.wait_ge(pe_did, PE.done("m1", i, u))
                        nc.scalar.activation(m1[u][:], C[u][:, 0:EC], ACT.Relu, bias=b1[:]).then_inc(act_did, 1)
                    for u in EDGE_SLOTS:
                        act.wait_ge(pe_did, PE.done("m2", i, u))
                        act.wait_ge(dve_did, DV.before("total", i, u))
                        nc.scalar.activation(m2[u][:], A[u][:, 0:EC], ACT.Relu, bias=b2[:]).then_inc(act_did, 1)
                    for u in EDGE_SLOTS:
                        act.wait_ge(pe_did, PE.done("rows", i, u))
                        act.wait_ge(p.scattered[u], i * 64 + 16)
                        nc.scalar.activation(p.out_rows[u][:, :, 0:D], tiles(B[u])[0:ET], ACT.Copy
                                             ).then_inc(act_did, 1)

            @block.vector
            def _(dve):
                for u in EDGE_SLOTS:
                    nc.vector.memset(p.out_rows[u][:], 0.0)
                nc.vector.memset(ones[:], 1.0)
                nc.vector.memset(count[1][:], 0.0)
                nc.vector.memset(total[1][:], 0.0).then_inc(dve_did, DV.per_iteration)
                with dve.Fori(0, E_ITERS) as i:
                    for u in EDGE_SLOTS:
                        dve.wait_ge(p.streamed[u], i * 48 + 48)
                        dve.wait_ge(dve_did, DV.before("total", i, u))
                        nc.vector.tensor_tensor(p.flag[u][:], p.dst[u][:], p.prev[u][:], ALU.is_equal
                                                ).then_inc(dve_did, 1)
                    for u in EDGE_SLOTS:
                        dve.wait_ge(pe_did, PE.done("turn", i, u))
                        nc.vector.tensor_copy(xd[u][:], B[u][:, 0:EC]).then_inc(dve_did, 1)
                    for u in EDGE_SLOTS:
                        dve.wait_ge(dve_did, DV.before("count", i, 1) if u == 0 else DV.done("count", i, 0))
                        dve.wait_ge(dve_did, DV.done("flag", i, u))
                        nc.vector.tensor_tensor_scan(count[u][:], p.flag[u][:], ones[:], count[1 - u][:, EC - 1:EC],
                                                     ALU.mult, ALU.add).then_inc(dve_did, 1)
                    for u in EDGE_SLOTS:
                        dve.wait_ge(dve_did, DV.done("count", i, u))
                        nc.vector.reciprocal(share[u][:], count[u][:]).then_inc(dve_did, 1)
                    for u in EDGE_SLOTS:
                        dve.wait_ge(dve_did, DV.before("total", i, 1) if u == 0 else DV.done("total", i, 0))
                        dve.wait_ge(act_did, AC.done("m2", i, u))
                        nc.vector.tensor_tensor_scan(total[u][:], p.flag[u][:], m2[u][:], total[1 - u][:, EC - 1:EC],
                                                     ALU.mult, ALU.add).then_inc(dve_did, 1)
                    for u in EDGE_SLOTS:
                        dve.wait_ge(dve_did, DV.done("total", i, u))
                        dve.wait_ge(pe_did, PE.before("rows", i, u))
                        nc.vector.tensor_tensor(mean[u][:], total[u][:], share[u][:], ALU.mult
                                                ).then_inc(dve_did, 1)



def layer1_nodes(nc, sems, keep, t, l, source, target):
    with ExitStack() as ctx:
        p = NodePass(nc, sems, ctx, f"n1{l}", keep, source, t["agg_rows"], target, buffers=1)
        ident = keep["ident"]
        w1, w2 = p.sb("w1", [D, D]), p.sb("w2", [D, D])
        b1 = p.sb("b1", [D, 1])
        b2 = p.sb("b2", [128, D])
        xt, ht = p.pair(p.sb, "xt", [D, NC_]), p.pair(p.sb, "ht", [D, NC_])
        biased = p.pair(p.sb, "biased", [128, 4, D])
        A, B = p.pair(p.bank, "A"), p.pair(p.bank, "B")
        PE = Steps("turn", "hidden", "update", slots=NODE_SLOTS)
        AC = Steps("xt", "hidden", "update", slots=NODE_SLOTS)
        DV = Steps("biased", slots=NODE_SLOTS)
        pe_did, act_did, dve_did = p.pe_did, p.act_did, p.dve_did
        WEIGHTS = 16 * 4
        with nc.Block() as block:
            @block.sync
            def _(sp):
                for tile, dram in ((w1, t["L1_nw1"][l, 0:D, :]), (w2, t["L1_nw2"][l, :, :]),
                                   (b1, t["L1_nb1"][l, :, :]), (b2, four(t["L1_nb2"][l, :, :]))):
                    sp.dma_start(tile[:], dram).then_inc(p.weights, 16)

                def free(i, u):
                    sp.wait_ge(pe_did, PE.before("hidden", i, u))
                    settled(sp, p.passed)

                p.sync_program(sp, free, lambda i, u: sp.wait_ge(act_did, AC.done("update", i, u)))

            @block.tensor
            def _(pe):
                pe.sem_inc(pe_did, PE.per_iteration)
                pe.wait_ge(p.weights, WEIGHTS)
                with pe.Fori(0, N_ITERS) as i:
                    for u in NODE_SLOTS:
                        pe.wait_ge(p.loaded[0][u], i * p.per_load + p.per_load)
                        pe.wait_ge(dve_did, DV.before("biased", i, u))
                        p.turn(A[u], p.rows[0][u])
                    for u in NODE_SLOTS:
                        pe.wait_ge(act_did, AC.done("xt", i, u))
                        nc.tensor.matmul(B[u][:], w1[:], xt[u][:], start=True, stop=False)
                        for j in range(4):
                            last = nc.tensor.matmul(B[u][:, j * D:(j + 1) * D], p.sums[0][u][:, j, 0:D], ident[:],
                                                    start=False, stop=(j == 3))
                        last.then_inc(pe_did, 1)
                    for u in NODE_SLOTS:
                        pe.wait_ge(act_did, AC.done("hidden", i, u))
                        for j in range(4):
                            last = nc.tensor.matmul(A[u][:, j * D:(j + 1) * D], ht[u][:, j * D:(j + 1) * D], w2[:],
                                                    start=True, stop=True)
                        last.then_inc(pe_did, 1)

            @block.scalar
            def _(act):
                act.sem_inc(act_did, AC.per_iteration)
                act.wait_ge(p.weights, WEIGHTS)
                with act.Fori(0, N_ITERS) as i:
                    for u in NODE_SLOTS:
                        act.wait_ge(pe_did, PE.done("turn", i, u))
                        nc.scalar.activation(xt[u][:], A[u][:], ACT.Copy).then_inc(act_did, 1)
                    for u in NODE_SLOTS:
                        act.wait_ge(pe_did, PE.done("hidden", i, u))
                        nc.scalar.activation(ht[u][:], B[u][:], ACT.Relu, bias=b1[:]).then_inc(act_did, 1)
                    for u in NODE_SLOTS:
                        act.wait_ge(dve_did, DV.done("biased", i, u))
                        act.wait_ge(p.stored[u], p.stores(i))
                        nc.scalar.activation(p.out[u][:], biased[u][:], ACT.Relu).then_inc(act_did, 1)

            @block.vector
            def _(dve):
                dve.wait_ge(p.weights, WEIGHTS)
                dve.sem_inc(dve_did, DV.per_iteration)
                with dve.Fori(0, N_ITERS) as i:
                    for u in NODE_SLOTS:
                        dve.wait_ge(pe_did, PE.done("update", i, u))
                        dve.wait_ge(act_did, AC.before("update", i, u))
                        nc.vector.tensor_tensor(biased[u][:], tiles(A[u]), each_tile(b2), ALU.add
                                                ).then_inc(dve_did, 1)



def layer1_last_nodes(nc, sems, keep, t, l, source, target):
    with ExitStack() as ctx:
        p = NodePass(nc, sems, ctx, f"n1{l}", keep, source, t["agg_rows"], target, t["x1"])
        ident = keep["ident"]
        w1, w2 = p.sb("w1", [D, D]), p.sb("w2", [D, D])
        b1, gamma, beta = (p.sb(n, [D, 1]) for n in ("b1", "gamma", "beta"))
        ones, b2_rows = p.sb("ones", [1, 128]), p.sb("b2_rows", [1, 4 * D])
        xt, ht = p.pair(p.sb, "xt", [D, NC_]), p.pair(p.sb, "ht", [D, NC_])
        new, nrm, res = (p.pair(p.sb, n, [128, 4, D]) for n in ("new", "nrm", "res"))
        aff = p.pair(p.sb, "aff", [D, 4, 128])
        A, B = p.pair(p.bank, "A"), p.pair(p.bank, "B")
        PE = Stages(*halves("turn E", "hidden E", "turn_normed L", "turn_back L", "update E"))
        AC = Stages(*halves("xt E", "in_apply L", "hidden E", "affine L", "update E", "out_std L", "in_std E"))
        DV = Stages(*halves("res L", "out_stats L", "out_moments L", "in_stats E", "in_moments E", "out_rstd L",
                            "out_apply L", "in_rstd E", "in_shift E"))
        pe_did, act_did, dve_did = p.pe_did, p.act_did, p.dve_did
        WEIGHTS = 16 * 6
        with nc.Block() as block:
            @block.sync
            def _(sp):
                for tile, dram in ((w1, t["L1_nw1"][l, 0:D, :]), (w2, t["L1_nw2"][l, :, :]),
                                   (b1, t["L1_nb1"][l, :, :]), (b2_rows, t["L1_nb2_rows"][l:l + 1, :]),
                                   (gamma, t["L1_gamma"]), (beta, t["L1_beta"])):
                    sp.dma_start(tile[:], dram).then_inc(p.weights, 16)

                def free(i, u):
                    sp.wait_ge(pe_did, PE.before("hidden", i, u))
                    settled(sp, p.passed)

                def residual_free(i, u):
                    sp.wait_ge(dve_did, DV.before("res", i, u))
                    settled(sp, p.passed)

                p.sync_halves(sp, free, lambda i, u: sp.wait_ge(dve_did, DV.done("out_apply", i, u)),
                              residual_free)

            @block.tensor
            def _(pe):
                def turn(i, slots, size):
                    for u in slots if i is not None else ():
                        pe.wait_ge(p.loaded[i.buffer][u], i.loads * p.per_load)
                        pe.wait_ge(act_did, AC.before("affine", i, u))
                        p.turn(A[u], p.rows[i.buffer][u], size("turn", u))

                def hidden(i, slots, size):
                    for u in slots if i is not None else ():
                        pe.wait_ge(act_did, AC.done("xt", i, u))
                        pe.wait_ge(dve_did, DV.before("res", i, u))
                        nc.tensor.matmul(B[u][:], w1[:], xt[u][:], start=True, stop=False)
                        for j in range(4):
                            last = nc.tensor.matmul(B[u][:, j * D:(j + 1) * D], p.sums[i.buffer][u][:, j, 0:D], ident[:],
                                                    start=False, stop=(j == 3))
                        last.then_inc(pe_did, size("hidden", u))

                def update(i, slots, size):
                    for u in slots if i is not None else ():
                        pe.wait_ge(act_did, AC.done("hidden", i, u))
                        nc.tensor.matmul(A[u][:], ones[:], b2_rows[:], start=True, stop=False)
                        for j in range(4):
                            last = nc.tensor.matmul(A[u][:, j * D:(j + 1) * D], ht[u][:, j * D:(j + 1) * D], w2[:],
                                                    start=False, stop=(j == 3))
                        last.then_inc(pe_did, size("update", u))

                def turn_normed(i, slots, size):
                    for u in slots if i is not None else ():
                        pe.wait_ge(act_did, AC.done("in_apply", i, u))
                        p.turn(A[u], nrm[u], size("turn_normed", u))

                def turn_back(i, slots, size):
                    for u in slots if i is not None else ():
                        pe.wait_ge(act_did, AC.done("affine", i, u))
                        p.turn(B[u], aff[u], size("turn_back", u))

                def half(i_early, early, i_late, late, size):
                    turn(i_early, early, size)
                    hidden(i_early, early, size)
                    turn_normed(i_late, late, size)
                    turn_back(i_late, late, size)
                    update(i_early, early, size)

                def body(back, front):
                    size = PE.sizes(back, front)
                    half(front, EARLY, back, LATE, size)
                    half(front, LATE, front, EARLY, size)

                pe.sem_inc(pe_did, PE.per_iteration)
                pe.wait_ge(p.weights, WEIGHTS)
                pe.wait_ge(dve_did, DV.per_iteration)
                buffered_bodies(pe, N_ITERS, body)

            @block.scalar
            def _(act):
                def copy_xt(i, slots, size):
                    for u in slots if i is not None else ():
                        act.wait_ge(pe_did, PE.done("turn", i, u))
                        nc.scalar.activation(xt[u][:], A[u][:], ACT.Copy).then_inc(act_did, size("xt", u))

                def hidden(i, slots, size):
                    for u in slots if i is not None else ():
                        act.wait_ge(pe_did, PE.done("hidden", i, u))
                        nc.scalar.activation(ht[u][:], B[u][:], ACT.Relu, bias=b1[:]
                                             ).then_inc(act_did, size("hidden", u))

                def update(i, slots, size):
                    for u in slots if i is not None else ():
                        act.wait_ge(pe_did, PE.done("update", i, u))
                        nc.scalar.activation(new[u][:], tiles(A[u]), ACT.Relu).then_inc(act_did, size("update", u))

                def affine(i, slots, size):
                    for u in slots if i is not None else ():
                        act.wait_ge(pe_did, PE.done("turn_normed", i, u))
                        nc.scalar.activation(aff[u][:].rearrange("p j d -> p (j d)"), A[u][:], ACT.Identity,
                                             bias=beta[:], scale=gamma[:]).then_inc(act_did, size("affine", u))

                def half(i_early, early, i_late, late, size):
                    copy_xt(i_early, early, size)
                    p.norm_apply_act(act, i_late, late, new, nrm, DV, "in", size,
                                     lambda i, u: act.wait_ge(pe_did, PE.before("turn_normed", i, u)))
                    hidden(i_early, early, size)
                    affine(i_late, late, size)
                    update(i_early, early, size)
                    p.norm_std(act, i_late, late, DV, "out", size)
                    p.norm_std(act, i_early, early, DV, "in", size)

                def body(back, front):
                    size = AC.sizes(back, front)
                    p.sqrt_table(act)
                    half(front, EARLY, back, LATE, size)
                    half(front, LATE, front, EARLY, size)

                act.sem_inc(act_did, AC.per_iteration)
                act.wait_ge(p.weights, WEIGHTS)
                act.wait_ge(dve_did, DV.per_iteration)
                buffered_bodies(act, N_ITERS, body)

            @block.vector
            def _(dve):
                def add_residual(i, slots, size):
                    for u in slots if i is not None else ():
                        dve.wait_ge(pe_did, PE.done("turn_back", i, u))
                        dve.wait_ge(p.residual_loaded[u], i * 16 + 16)
                        nc.vector.tensor_tensor(res[u][:], tiles(B[u]), p.residual[u][:], ALU.add
                                                ).then_inc(dve_did, size("res", u))

                def half(i_early, early, i_late, late, size):
                    add_residual(i_late, late, size)
                    p.norm_stats(dve, i_late, late, res, "out", size,
                                 lambda i, u: dve.wait_ge(dve_did, DV.done("res", i, u)))
                    p.norm_moments(dve, i_late, late, DV, "out", size)
                    p.norm_stats(dve, i_early, early, new, "in", size,
                                 lambda i, u: dve.wait_ge(act_did, AC.done("update", i, u)))
                    p.norm_moments(dve, i_early, early, DV, "in", size)
                    p.norm_rstd(dve, i_late, late, AC, "out", size)
                    p.norm_apply_dve(dve, i_late, late, res, p.out, DV, "out", size,
                                     lambda i, u: dve.wait_ge(p.stored[u], p.stores(i)))
                    p.norm_rstd(dve, i_early, early, AC, "in", size)
                    p.norm_shift(dve, i_early, early, DV, "in", size)

                def body(back, front):
                    size = DV.sizes(back, front)
                    half(front, EARLY, back, LATE, size)
                    half(front, LATE, front, EARLY, size)

                dve.wait_ge(p.weights, WEIGHTS)
                nc.vector.memset(ones[:], 1.0)
                nc.vector.memset(p.eps[:], EPS).then_inc(dve_did, DV.per_iteration)
                buffered_bodies(dve, N_ITERS, body)



def layer2_edges(nc, sems, keep, t):
    relations = t["L2_W"].shape[0]
    with ExitStack() as ctx:
        p = EdgePass(nc, sems, ctx, "e2", keep, t["x2"], t["agg_rows"], 1)
        ident = keep["ident"]
        w = p.sb("w", [D, relations, D])
        ones = p.sb("ones", [128, EC])
        kind = p.pair(p.sb, "kind", [128, EC], I32)
        xs, count, total = (p.pair(p.sb, n, [D, EC]) for n in ("xs", "count", "total"))
        of_kind = p.pair(p.sb, "of_kind", [D, relations, EC])
        A, B, C, DD = (p.pair(p.bank, n) for n in "ABCD")
        PE = Steps("turn", "messages", "rows", slots=EDGE_SLOTS)
        AC = Steps("xs", "rows", slots=EDGE_SLOTS)
        DV = Steps("flag", *(f"of_kind{r}/{u}" for u in EDGE_SLOTS for r in range(relations)), "count/0", "count/1", "total/0", "total/1", slots=EDGE_SLOTS)
        pe_did, act_did, dve_did = p.pe_did, p.act_did, p.dve_did
        with nc.Block() as block:
            @block.sync
            def _(sp):
                sp.dma_start(w[:], t["L2_W"].rearrange("r i o -> i r o")).then_inc(p.weights, 16)
                with sp.Fori(0, E_ITERS) as i:
                    for u in EDGE_SLOTS:
                        sp.wait_ge(dve_did, DV.before(f"of_kind{relations - 1}", i, u))
                        p.stream(sp, i, u, t, [(kind[u][:], t["type_rows"], 128)])

            @block.gpsimd
            def _(gp):
                p.pool_program(gp, PE, AC, ahead=2)

            @block.tensor
            def _(pe):
                pe.sem_inc(pe_did, PE.per_iteration)
                pe.wait_ge(p.weights, 16)
                with pe.Fori(0, E_ITERS) as i:
                    for u in EDGE_SLOTS:
                        pe.wait_ge(p.gathered[u], i * 64 + 64)
                        pe.wait_ge(act_did, AC.before("xs", i, u))
                        p.turn(pe, i, u, (A[u],), PE)
                    for u in EDGE_SLOTS:
                        for r in range(relations):
                            pe.wait_ge(dve_did, DV.done(f"of_kind{r}", i, u))
                            last = nc.tensor.matmul(B[u][:, 0:EC], w[:, r, :], of_kind[u][:, r, :],
                                                    start=(r == 0), stop=(r == relations - 1))
                        last.then_inc(pe_did, 1)
                    for u in EDGE_SLOTS:
                        pe.wait_ge(dve_did, DV.done("total", i, u))
                        pe.wait_ge(act_did, AC.before("rows", i, u))
                        for j in range(TILES):
                            nc.tensor.matmul(C[u][0:ET, j * D:(j + 1) * D], tile_of(total[u], j), ident[:],
                                             start=True, stop=True)
                        for j in range(TILES):
                            last = nc.tensor.matmul(DD[u][0:ET, j:j + 1], tile_of(count[u], j), ident[:, 0:1],
                                                    start=True, stop=True)
                        last.then_inc(pe_did, 1)

            @block.scalar
            def _(act):
                act.sem_inc(act_did, AC.per_iteration)
                with act.Fori(0, E_ITERS) as i:
                    for u in EDGE_SLOTS:
                        act.wait_ge(pe_did, PE.done("turn", i, u))
                        act.wait_ge(dve_did, DV.before(f"of_kind{relations - 1}", i, u))
                        nc.scalar.activation(xs[u][:], A[u][:, 0:EC], ACT.Copy).then_inc(act_did, 1)
                    for u in EDGE_SLOTS:
                        act.wait_ge(pe_did, PE.done("rows", i, u))
                        act.wait_ge(p.scattered[u], i * 64 + 16)
                        nc.scalar.activation(p.out_rows[u][:, :, 0:D], tiles(C[u])[0:ET], ACT.Copy)
                        nc.scalar.activation(p.out_rows[u][:, :, D:D + 1],
                                             DD[u][0:ET, 0:TILES].rearrange("p (j a) -> p j a", a=1),
                                             ACT.Copy).then_inc(act_did, 1)

            @block.vector
            def _(dve):
                for u in EDGE_SLOTS:
                    nc.vector.memset(p.out_rows[u][:], 0.0)
                nc.vector.memset(ones[:], 1.0)
                nc.vector.memset(count[1][:], 0.0)
                nc.vector.memset(total[1][:], 0.0).then_inc(dve_did, DV.per_iteration)
                with dve.Fori(0, E_ITERS) as i:
                    for u in EDGE_SLOTS:
                        dve.wait_ge(p.streamed[u], i * 48 + 48)
                        dve.wait_ge(dve_did, DV.before("total", i, u))
                        nc.vector.tensor_tensor(p.flag[u][:], p.dst[u][:], p.prev[u][:], ALU.is_equal
                                                ).then_inc(dve_did, 1)
                    for u in EDGE_SLOTS:
                        dve.wait_ge(act_did, AC.done("xs", i, u))
                        dve.wait_ge(pe_did, PE.before("messages", i, u))
                        for r in range(relations):
                            nc.vector.scalar_tensor_tensor(
                                out=of_kind[u][:, r, :], in0=kind[u][:], scalar=float(r), in1=xs[u][:],
                                op0=ALU.is_equal, op1=ALU.mult).then_inc(dve_did, 1)
                    for u in EDGE_SLOTS:
                        dve.wait_ge(dve_did, DV.before("count", i, 1) if u == 0 else DV.done("count", i, 0))
                        dve.wait_ge(dve_did, DV.done("flag", i, u))
                        dve.wait_ge(pe_did, PE.before("rows", i, u))
                        nc.vector.tensor_tensor_scan(count[u][:], p.flag[u][:], ones[:], count[1 - u][:, EC - 1:EC],
                                                     ALU.mult, ALU.add).then_inc(dve_did, 1)
                    for u in EDGE_SLOTS:
                        dve.wait_ge(dve_did, DV.before("total", i, 1) if u == 0 else DV.done("total", i, 0))
                        dve.wait_ge(pe_did, PE.done("messages", i, u))
                        nc.vector.tensor_tensor_scan(total[u][:], p.flag[u][:], B[u][:, 0:EC],
                                                     total[1 - u][:, EC - 1:EC], ALU.mult, ALU.add
                                                     ).then_inc(dve_did, 1)



def layer2_nodes(nc, sems, keep, t):
    with ExitStack() as ctx:
        p = NodePass(nc, sems, ctx, "n2", keep, t["x2"], t["agg_rows"], t["x3"])
        w0 = p.sb("w0", [D, D])
        deg, share = p.pair(p.sb, "deg", [128, 4]), p.pair(p.sb, "share", [128, 4])
        xt = p.pair(p.sb, "xt", [D, NC_])
        both, res = p.pair(p.sb, "both", [128, 4, D]), p.pair(p.sb, "res", [128, 4, D])
        A, B = p.pair(p.bank, "A"), p.pair(p.bank, "B")
        PE = Stages(*halves("turn E", "own E"))
        AC = Stages(*halves("xt E", "out_apply P", "out_std L"))
        DV = Stages(*halves("deg E", "share E", "out_stats L", "out_moments L", "both E", "out_rstd L", "out_shift L", "res E"))
        pe_did, act_did, dve_did = p.pe_did, p.act_did, p.dve_did
        with nc.Block() as block:
            @block.sync
            def _(sp):
                sp.dma_start(w0[:], t["L2_W0"]).then_inc(p.weights, 16)

                def free(i, u):
                    sp.wait_ge(dve_did, DV.before("res", i, u))
                    settled(sp, p.passed)
                    sp.wait_ge(pe_did, PE.before("turn", i, u))
                    settled(sp, p.passed)

                p.sync_halves(sp, free, lambda i, u: sp.wait_ge(act_did, AC.done("out_apply", i, u)),
                              early_stored="back")

            @block.tensor
            def _(pe):
                def half(i, slots, size):
                    for u in slots if i is not None else ():
                        pe.wait_ge(p.loaded[i.buffer][u], i.loads * p.per_load)
                        pe.wait_ge(act_did, AC.before("xt", i, u))
                        p.turn(A[u], p.rows[i.buffer][u], size("turn", u))
                    for u in slots if i is not None else ():
                        pe.wait_ge(act_did, AC.done("xt", i, u))
                        pe.wait_ge(dve_did, DV.before("both", i, u))
                        for j in range(4):
                            last = nc.tensor.matmul(B[u][:, j * D:(j + 1) * D], xt[u][:, j * D:(j + 1) * D], w0[:],
                                                    start=True, stop=True)
                        last.then_inc(pe_did, size("own", u))

                def body(back, front):
                    size = PE.sizes(back, front)
                    half(front, EARLY, size)
                    half(front, LATE, size)

                pe.sem_inc(pe_did, PE.per_iteration)
                pe.wait_ge(p.weights, 16)
                buffered_bodies(pe, N_ITERS, body)

            @block.scalar
            def _(act):
                def half(i_early, early, i_late, late, i_post, size):
                    for u in early if i_early is not None else ():
                        act.wait_ge(pe_did, PE.done("turn", i_early, u))
                        nc.scalar.activation(xt[u][:], A[u][:], ACT.Copy).then_inc(act_did, size("xt", u))
                    p.norm_apply_act(act, i_post, early, res, p.out, DV, "out", size,
                                     lambda i, u: act.wait_ge(p.stored[u], p.stores(i)))
                    p.norm_std(act, i_late, late, DV, "out", size)

                def body(back, front):
                    size = AC.sizes(back, front)
                    p.sqrt_table(act)
                    half(front, EARLY, back, LATE, back, size)
                    half(front, LATE, front, EARLY, back, size)

                act.sem_inc(act_did, AC.per_iteration)
                act.wait_ge(dve_did, DV.per_iteration)
                buffered_bodies(act, N_ITERS, body)

            @block.vector
            def _(dve):
                def half(i_early, early, i_late, late, size):
                    for u in early if i_early is not None else ():
                        dve.wait_ge(p.loaded[i_early.buffer][u], i_early.loads * p.per_load)
                        nc.vector.tensor_scalar(deg[u][:], p.sums[i_early.buffer][u][:, :, D], 1.0, None, ALU.max
                                                ).then_inc(dve_did, size("deg", u))
                    for u in early if i_early is not None else ():
                        dve.wait_ge(dve_did, DV.done("deg", i_early, u))
                        nc.vector.reciprocal(share[u][:], deg[u][:]).then_inc(dve_did, size("share", u))
                    p.norm_stats(dve, i_late, late, res, "out", size,
                                 lambda i, u: dve.wait_ge(dve_did, DV.done("res", i, u)))
                    p.norm_moments(dve, i_late, late, DV, "out", size)
                    for u in early if i_early is not None else ():
                        dve.wait_ge(pe_did, PE.done("own", i_early, u))
                        nc.vector.tensor_tensor(both[u][:], tiles(B[u]), p.sums[i_early.buffer][u][:, :, 0:D], ALU.add
                                                ).then_inc(dve_did, size("both", u))
                    p.norm_rstd(dve, i_late, late, AC, "out", size)
                    p.norm_shift(dve, i_late, late, DV, "out", size)
                    for u in early if i_early is not None else ():
                        dve.wait_ge(dve_did, DV.done("both", i_early, u))
                        dve.wait_ge(act_did, AC.before("out_apply", i_early, u))
                        for j in range(4):
                            last = nc.vector.scalar_tensor_tensor(
                                out=res[u][:, j, :], in0=both[u][:, j, :], scalar=share[u][:, j:j + 1],
                                in1=p.rows[i_early.buffer][u][:, j, :], op0=ALU.mult, op1=ALU.add)
                        last.then_inc(dve_did, size("res", u))

                def body(back, front):
                    size = DV.sizes(back, front)
                    half(front, EARLY, back, LATE, size)
                    half(front, LATE, front, EARLY, size)

                nc.vector.memset(p.eps[:], EPS).then_inc(dve_did, DV.per_iteration)
                buffered_bodies(dve, N_ITERS, body)



def layer3_edges(nc, sems, keep, t):
    with ExitStack() as ctx:
        p = EdgePass(nc, sems, ctx, "e3", keep, t["x3"], t["agg_rows"], 2)
        lanes = 32 + H3
        low = 64
        at_slot = (slice(0, H3), slice(32, 32 + H3))
        w, att = p.sb("w", [D, H3, D]), p.sb("att", [D, 2, H3, D])
        weighed = p.sb("weighed", [D, 2, H3, D])
        to_logit = p.sb("to_logit", [D, 2, H3])
        own_logit = p.sb("own_logit", [D, H3])
        wq4 = p.sb("wq4", [D, H3, D])
        pick_f32 = p.sb("pick_f32", [low + lanes, 2 * H3, D])
        pick = p.sb("pick", [low + lanes, 2 * H3, D], BF16)
        xs, xd, diff = (p.pair(p.sb, n, [D, EC]) for n in ("xs", "xd", "diff"))
        part = p.pair(p.sb, "part", [D, EC])
        total = p.pair(p.sb, "total", [D, H3, EC])
        dst, prev = p.sb("lane_dst", [lanes, EC], I32), p.sb("lane_prev", [lanes, EC], I32)
        flag, pen, start = (p.sb(n, [lanes, EC]) for n in ("flag", "pen", "start"))
        raw, leaky = p.sb("raw", [lanes, 2, EC]), p.sb("leaky", [lanes, 2, EC])
        top = p.sb("top", [lanes, EC])
        m, den = p.sb("m", [lanes, EC + 1]), p.sb("den", [lanes, EC + 1])
        de, ce = p.sb("de", [lanes, 3, EC]), p.sb("ce", [lanes, 3, EC])
        rden, ratio = p.sb("rden", [lanes, EC]), p.sb("ratio", [lanes, EC])
        factors = p.sb("factors", [lanes, 2, EC])
        rest = p.sb("rest", [lanes, 2, EC])
        high_parts = p.sb("high_parts", [low + lanes, 2, EC], BF16)
        low_parts = p.sb("low_parts", [lanes, 2, EC], BF16)
        T = ctx.enter_context(nc.psum_tensor("e3_T", [128, 2, 512], F32))
        P = [[p.bank(f"P{k}{s}") for s in ("keep", "share")] for k in range(2)]
        R = p.pair(p.bank, "R")
        chains = [(h, u) for h in range(H3) for u in EDGE_SLOTS]
        PE = Stages("back spread0/0", "back spread0/1", "front turn/0",
                    "back spread1/0", "back rows0/0", "front turn/1",
                    "back spread1/1", "back rows0/1", "front logits",
                    "back spread2/0", "back rows1/0", "back spread2/1", "back rows1/1",
                    "back spread3/0", "back rows2/0", "back spread3/1", "back rows2/1",
                    "back rows3/0", "back rows3/1")
        AC = Stages("front xs/0", "front xd/0", "front xs/1", "front xd/1", "front raw", "front exp", "front high",
                    "front middle", "back rows/0", "back rows/1")
        DV = Stages("back part0/0", "back total0/0", "front flag", "back part0/1", "back total0/1", "front pen",
                    "back part1/0", "back total1/0", "back part1/1", "back total1/1", "front leaky",
                    "back part2/0", "back total2/0",
                    "front top", "front carry/0", "front max/0", "front carry/1", "front max/1", "front drop",
                    "front differences", "back part2/1", "back total2/1",
                    "front own", "front add_own", "front carry_den/0", "front den/0", "front carry_den/1",
                    "front den/1", "front rden", "front ratio", "front factors",
                    "back part3/0", "back total3/0", "front rest", "back part3/1", "back total3/1",
                    "front diff/0", "front diff/1", "front low")
        pe_did, act_did, dve_did = p.pe_did, p.act_did, p.dve_did
        setup_did = p.sem("setup_did")
        WEIGHTS = 16 * 4

        with nc.Block() as block:
            @block.sync
            def _(sp):
                sp.dma_start(w[:], t["L3_W"].rearrange("i (h o) -> i h o", h=H3)).then_inc(p.weights, 16)
                sp.dma_start(att[:, 0, :, :].rearrange("p h o -> p (h o)"),
                             t["L3_att_src"].broadcast_to([D, H3 * D])).then_inc(p.weights, 16)
                sp.dma_start(att[:, 1, :, :].rearrange("p h o -> p (h o)"),
                             t["L3_att_dst"].broadcast_to([D, H3 * D])).then_inc(p.weights, 16)
                sp.dma_start(pick_f32[:].rearrange("k c o -> k (c o)"), t["head_pick"]).then_inc(p.weights, 16)
                with sp.Fori(0, E_ITERS) as i:
                    sp.wait_ge(dve_did, DV.before("flag", i))
                    settled(sp, p.passed)
                    for rows, tile in ((t["dst_rows"], dst), (t["prev_rows"], prev)):
                        sp.dma_start(tile[0:32, :], rows[bass.ds(2 * i, 1), :].broadcast_to([32, EC])
                                     ).then_inc(p.streamed[0], 16)
                        sp.dma_start(tile[32:lanes, :], rows[bass.ds(2 * i + 1, 1), :].broadcast_to([H3, EC])
                                     ).then_inc(p.streamed[0], 16)

            @block.gpsimd
            def _(gp):
                p.pool_program(gp, PE, AC, ahead=2)

            @block.tensor
            def _(pe):
                def body(back, front):
                    def spread(h, u):
                        c = chains.index((h, u))
                        if c < 2:
                            pe.wait_ge(dve_did, DV.done("low", back))
                        else:
                            before_h, before_u = chains[c - 2]
                            pe.wait_ge(dve_did, DV.done(f"total{before_h}", back, before_u))
                        lane = u * H3 + h
                        for s in range(2):
                            nc.tensor.matmul(P[c % 2][s][:, 0:EC], pick[:, lane, :], high_parts[:, s, :],
                                             start=True, stop=False)
                            last = nc.tensor.matmul(P[c % 2][s][:, 0:EC], pick[0:lanes, lane, :], low_parts[:, s, :],
                                                    start=False, stop=True)
                        last.then_inc(pe_did, PE.size(f"spread{h}", u, back, front))

                    def rows(h, u):
                        pe.wait_ge(dve_did, DV.done(f"total{h}", back, u))
                        if h == 0:
                            pe.wait_ge(act_did, AC.before("rows", back, u))
                        for j in range(TILES):
                            last = nc.tensor.matmul(R[u][0:ET, j * D:(j + 1) * D],
                                                    total[u][:, h, j * ET:(j + 1) * ET], wq4[:, h, :],
                                                    start=(h == 0 and j == 0), stop=(h == H3 - 1),
                                                    skip_group_check=True)
                        last.then_inc(pe_did, PE.size(f"rows{h}", u, back, front))

                    def turn(u):
                        pe.wait_ge(p.gathered[u], front * 128 + 128)
                        if u == 0:
                            pe.wait_ge(act_did, AC.before("raw", front))
                        else:
                            pe.wait_ge(act_did, AC.done("xd", front, 0))
                        for end in range(2):
                            for j in range(TILES):
                                last = nc.tensor.transpose(T[:, end, j * ET:(j + 1) * ET],
                                                           p.end_rows[u][:, end * TILES + j, :],
                                                           keep["ident"][0:ET, 0:ET])
                        last.then_inc(pe_did, PE.size("turn", u, back, front))

                    if back is not None:
                        spread(0, 0)
                        spread(0, 1)
                    if front is not None:
                        turn(0)
                    if back is not None:
                        spread(1, 0)
                        rows(0, 0)
                    if front is not None:
                        turn(1)
                    if back is not None:
                        spread(1, 1)
                        rows(0, 1)
                    if front is not None:
                        pe.wait_ge(act_did, AC.done("xd", front, 1))
                        for u in EDGE_SLOTS:
                            nc.tensor.matmul(T[at_slot[u], 0, 0:EC], to_logit[:, 0, :], xs[u][:],
                                             start=True, stop=False)
                            nc.tensor.matmul(T[at_slot[u], 0, 0:EC], to_logit[:, 1, :], xd[u][:],
                                             start=False, stop=True)
                            last = nc.tensor.matmul(T[at_slot[u], 1, 0:EC], own_logit[:], xd[u][:],
                                                    start=True, stop=True)
                        last.then_inc(pe_did, PE.size("logits", 0, back, front))
                    if back is not None:
                        for c in range(4, len(chains)):
                            spread(*chains[c])
                            rows(*chains[c - 2])
                        for c in range(len(chains) - 2, len(chains)):
                            rows(*chains[c])
                    else:
                        pe.wait_ge(pe_did, PE.done("logits", front))
                        pe.sem_inc(pe_did, PE.left(back, front))

                pe.sem_inc(pe_did, PE.per_iteration)
                pe.wait_ge(setup_did, 5)
                bodies(pe, E_ITERS, body)

            @block.scalar
            def _(act):
                def body(back, front):
                    if front is not None:
                        for u in EDGE_SLOTS:
                            act.wait_ge(pe_did, PE.done("turn", front, u))
                            act.wait_ge(dve_did, DV.before("diff", front, u))
                            nc.scalar.activation(xs[u][:], T[:, 0, 0:EC], ACT.Copy
                                                 ).then_inc(act_did, AC.size("xs", u, back, front))
                            nc.scalar.activation(xd[u][:], T[:, 1, 0:EC], ACT.Copy
                                                 ).then_inc(act_did, AC.size("xd", u, back, front))
                        act.wait_ge(pe_did, PE.done("logits", front))
                        act.wait_ge(dve_did, DV.before("leaky", front))
                        nc.scalar.activation(raw[:], T[0:lanes, :, 0:EC], ACT.Copy
                                             ).then_inc(act_did, AC.size("raw", 0, back, front))
                        act.wait_ge(dve_did, DV.done("differences", front))
                        nc.scalar.activation(ce[:], de[:], ACT.Exp).then_inc(act_did, AC.size("exp", 0, back, front))
                        act.wait_ge(dve_did, DV.done("factors", front))
                        act.wait_ge(pe_did, PE.before("spread3", front, 1))
                        nc.scalar.activation(high_parts[0:lanes], factors[:], ACT.Copy
                                             ).then_inc(act_did, AC.size("high", 0, back, front))
                        act.wait_ge(dve_did, DV.done("rest", front))
                        nc.scalar.activation(high_parts[low:low + lanes], rest[:], ACT.Copy
                                             ).then_inc(act_did, AC.size("middle", 0, back, front))
                    if back is not None:
                        for u in EDGE_SLOTS:
                            act.wait_ge(pe_did, PE.done("rows3", back, u))
                            act.wait_ge(p.scattered[u], back * 64 + 16)
                            nc.scalar.activation(p.out_rows[u][:, :, 0:D], tiles(R[u])[0:ET], ACT.Copy
                                                 ).then_inc(act_did, AC.size("rows", u, back, front))
                    else:
                        act.wait_ge(act_did, AC.done("middle", front))
                        act.sem_inc(act_did, AC.left(back, front))

                act.sem_inc(act_did, AC.per_iteration)
                bodies(act, E_ITERS, body)

            @block.vector
            def _(dve):
                def body(back, front):
                    def step(name, u=0):
                        return dve_did, DV.size(name, u, back, front)

                    def chain(h, u):
                        if back is None:
                            return
                        bank = P[chains.index((h, u)) % 2]
                        dve.wait_ge(pe_did, PE.done(f"spread{h}", back, u))
                        nc.vector.tensor_tensor(part[u][:], diff[u][:], bank[1][:, 0:EC], ALU.mult
                                                ).then_inc(*step(f"part{h}", u))
                        dve.wait_ge(dve_did, DV.done(f"part{h}", back, u))
                        dve.wait_ge(pe_did, PE.before(f"rows{h}", back, u))
                        dve.wait_ge(dve_did, DV.before(f"total{h}", back, 1) if u == 0
                                    else DV.done(f"total{h}", back, 0))
                        nc.vector.tensor_tensor_scan(total[u][:, h, :], bank[0][:, 0:EC], part[u][:],
                                                     total[1 - u][:, h, EC - 1:EC], ALU.mult, ALU.add
                                                     ).then_inc(*step(f"total{h}", u))

                    chain(0, 0)
                    if front is not None:
                        dve.wait_ge(p.streamed[0], front * 64 + 64)
                        nc.vector.tensor_tensor(flag[:], dst[:], prev[:], ALU.is_equal).then_inc(*step("flag"))
                    chain(0, 1)
                    if front is not None:
                        dve.wait_ge(dve_did, DV.done("flag", front))
                        nc.vector.tensor_scalar(pen[:], flag[:], FAR, -FAR, ALU.mult, ALU.add)
                        nc.vector.tensor_scalar(start[:], flag[:], -1.0, 1.0, ALU.mult, ALU.add
                                                ).then_inc(*step("pen"))
                    chain(1, 0)
                    chain(1, 1)
                    if front is not None:
                        dve.wait_ge(act_did, AC.done("raw", front))
                        nc.vector.scalar_tensor_tensor(out=leaky[:], in0=raw[:], scalar=0.2,
                                                       in1=raw[:], op0=ALU.mult, op1=ALU.max
                                                       ).then_inc(*step("leaky"))
                    chain(2, 0)
                    if front is not None:
                        dve.wait_ge(dve_did, DV.done("leaky", front))
                        nc.vector.tensor_tensor(top[:], leaky[:, 0, :], leaky[:, 1, :], ALU.max).then_inc(*step("top"))
                        for u in EDGE_SLOTS:
                            here, other = at_slot[u], at_slot[1 - u]
                            dve.wait_ge(dve_did, DV.done("top", front) if u == 0 else DV.done("max", front, 0))
                            nc.vector.tensor_copy(m[here, 0:1], m[other, EC:EC + 1]).then_inc(*step("carry", u))
                            dve.wait_ge(dve_did, DV.done("carry", front, u))
                            nc.vector.tensor_tensor_scan(m[here, 1:EC + 1], pen[here, :], top[here, :], m[here, 0:1],
                                                         ALU.add, ALU.max).then_inc(*step("max", u))
                        dve.wait_ge(dve_did, DV.done("max", front, 1))
                        nc.vector.tensor_tensor(de[:, 0, :], m[:, 0:EC], m[:, 1:EC + 1], ALU.subtract
                                                ).then_inc(*step("drop"))
                        dve.wait_ge(dve_did, DV.done("drop", front))
                        nc.vector.tensor_tensor(de[:, 0, :], de[:, 0, :], pen[:], ALU.add)
                        for s in range(2):
                            last = nc.vector.tensor_tensor(de[:, 1 + s, :], leaky[:, s, :], m[:, 1:EC + 1],
                                                           ALU.subtract)
                        last.then_inc(*step("differences"))
                    chain(2, 1)
                    if front is not None:
                        dve.wait_ge(act_did, AC.done("exp", front))
                        nc.vector.tensor_tensor(start[:], start[:], ce[:, 2, :], ALU.mult).then_inc(*step("own"))
                        dve.wait_ge(dve_did, DV.done("own", front))
                        nc.vector.tensor_tensor(top[:], start[:], ce[:, 1, :], ALU.add).then_inc(*step("add_own"))
                        for u in EDGE_SLOTS:
                            here, other = at_slot[u], at_slot[1 - u]
                            dve.wait_ge(dve_did, DV.done("add_own", front) if u == 0 else DV.done("den", front, 0))
                            nc.vector.tensor_copy(den[here, 0:1], den[other, EC:EC + 1]
                                                  ).then_inc(*step("carry_den", u))
                            dve.wait_ge(dve_did, DV.done("carry_den", front, u))
                            nc.vector.tensor_tensor_scan(den[here, 1:EC + 1], ce[here, 0, :], top[here, :],
                                                         den[here, 0:1], ALU.mult, ALU.add).then_inc(*step("den", u))
                        dve.wait_ge(dve_did, DV.done("den", front, 1))
                        nc.vector.reciprocal(rden[:], den[:, 1:EC + 1]).then_inc(*step("rden"))
                        dve.wait_ge(dve_did, DV.done("rden", front))
                        nc.vector.tensor_tensor(ratio[:], rden[:], den[:, 0:EC], ALU.mult).then_inc(*step("ratio"))
                        nc.vector.tensor_tensor(factors[:, 1, :], ce[:, 1, :], rden[:], ALU.mult)
                        dve.wait_ge(dve_did, DV.done("ratio", front))
                        nc.vector.tensor_tensor(factors[:, 0, :], ce[:, 0, :], ratio[:], ALU.mult
                                                ).then_inc(*step("factors"))
                    chain(3, 0)
                    if front is not None:
                        dve.wait_ge(act_did, AC.done("high", front))
                        nc.vector.tensor_tensor(rest[:], factors[:], high_parts[0:lanes], ALU.subtract
                                                ).then_inc(*step("rest"))
                    chain(3, 1)
                    if front is not None:
                        for u in EDGE_SLOTS:
                            dve.wait_ge(act_did, AC.done("xd", front, u))
                            nc.vector.tensor_tensor(diff[u][:], xs[u][:], xd[u][:], ALU.subtract
                                                    ).then_inc(*step("diff", u))
                        dve.wait_ge(act_did, AC.done("middle", front))
                        nc.vector.tensor_tensor(low_parts[:], rest[:], high_parts[low:low + lanes], ALU.subtract
                                                ).then_inc(*step("low"))

                for u in EDGE_SLOTS:
                    nc.vector.memset(p.out_rows[u][:], 0.0)
                nc.vector.memset(m[:], 0.0)
                nc.vector.memset(den[:], 1.0)
                nc.vector.memset(high_parts[:], 0.0)
                dve.wait_ge(p.weights, WEIGHTS)
                nc.vector.tensor_copy(pick[:], pick_f32[:]).then_inc(setup_did, 1)
                for s in range(2):
                    last = nc.vector.tensor_tensor(weighed[:, s, :, :], w[:], att[:, s, :, :], ALU.mult)
                last.then_inc(setup_did, 1)
                dve.wait_ge(setup_did, 2)
                nc.vector.tensor_reduce(to_logit[:].rearrange("p s h -> p (s h)"),
                                        weighed[:].rearrange("p s h o -> p (s h) o"), mybir.AxisListType.X, ALU.add
                                        ).then_inc(setup_did, 1)
                nc.vector.tensor_scalar(wq4[:], w[:], 1.0 / H3, None, ALU.mult).then_inc(setup_did, 1)
                dve.wait_ge(setup_did, 3)
                nc.vector.tensor_tensor(own_logit[:], to_logit[:, 0, :], to_logit[:, 1, :], ALU.add
                                        ).then_inc(setup_did, 1)
                nc.vector.memset(total[1][:], 0.0).then_inc(dve_did, DV.per_iteration)
                bodies(dve, E_ITERS, body)



def layer3_nodes(nc, sems, keep, t):
    with ExitStack() as ctx:
        p = NodePass(nc, sems, ctx, "n3", keep, t["x3"], t["agg_rows"], t["out"])
        w, two, wm = p.sb("w", [D, H3, D]), p.sb("two", [D, 2, D]), p.sb("wm", [D, D])
        bias = p.sb("bias", [128, D])
        more = p.pair(p.sb, "more", [128, 4, D])
        PO = Stages(*halves("more E"))
        pool_did = p.pool_did
        setup_did = p.sem("setup_did")
        xt = p.pair(p.sb, "xt", [D, NC_])
        both, res = p.pair(p.sb, "both", [128, 4, D]), p.pair(p.sb, "res", [128, 4, D])
        A, B = p.pair(p.bank, "A"), p.pair(p.bank, "B")
        PE = Stages(*halves("turn E", "own E"))
        AC = Stages(*halves("xt E", "out_apply P", "out_std L"))
        DV = Stages(*halves("out_stats L", "out_moments L", "both E", "out_rstd L", "out_shift L", "res E"))
        pe_did, act_did, dve_did = p.pe_did, p.act_did, p.dve_did
        with nc.Block() as block:
            @block.sync
            def _(sp):
                sp.dma_start(w[:], t["L3_W"].rearrange("i (h o) -> i h o", h=H3)).then_inc(p.weights, 16)
                sp.dma_start(bias[:], four(t["L3_bias"])).then_inc(p.weights, 16)

                def free(i, u):
                    sp.wait_ge(dve_did, DV.before("res", i, u))
                    settled(sp, p.passed)
                    sp.wait_ge(pe_did, PE.before("turn", i, u))
                    settled(sp, p.passed)
                    sp.wait_ge(pool_did, PO.before("more", i, u))
                    settled(sp, p.passed)

                p.sync_halves(sp, free, lambda i, u: sp.wait_ge(act_did, AC.done("out_apply", i, u)),
                              early_stored="back")

            @block.gpsimd
            def _(gp):
                def add_bias(i, slots, size):
                    for u in slots if i is not None else ():
                        gp.wait_ge(p.loaded[i.buffer][u], i.loads * p.per_load)
                        gp.wait_ge(dve_did, DV.before("both", i, u))
                        nc.gpsimd.tensor_tensor(more[u][:], p.sums[i.buffer][u][:, :, 0:D], each_tile(bias), ALU.add
                                                ).then_inc(pool_did, size("more", u))

                def body(back, front):
                    size = PO.sizes(back, front)
                    add_bias(front, EARLY, size)
                    add_bias(front, LATE, size)

                gp.sem_inc(pool_did, PO.per_iteration)
                gp.wait_ge(p.weights, 32)
                buffered_bodies(gp, N_ITERS, body)

            @block.tensor
            def _(pe):
                def half(i, slots, size):
                    for u in slots if i is not None else ():
                        pe.wait_ge(p.loaded[i.buffer][u], i.loads * p.per_load)
                        pe.wait_ge(act_did, AC.before("xt", i, u))
                        p.turn(A[u], p.rows[i.buffer][u], size("turn", u))
                    for u in slots if i is not None else ():
                        pe.wait_ge(act_did, AC.done("xt", i, u))
                        pe.wait_ge(dve_did, DV.before("both", i, u))
                        for j in range(4):
                            last = nc.tensor.matmul(B[u][:, j * D:(j + 1) * D], xt[u][:, j * D:(j + 1) * D], wm[:],
                                                    start=True, stop=True)
                        last.then_inc(pe_did, size("own", u))

                def body(back, front):
                    size = PE.sizes(back, front)
                    half(front, EARLY, size)
                    half(front, LATE, size)

                pe.sem_inc(pe_did, PE.per_iteration)
                pe.wait_ge(setup_did, 3)
                buffered_bodies(pe, N_ITERS, body)

            @block.scalar
            def _(act):
                def half(i_early, early, i_late, late, i_post, size):
                    for u in early if i_early is not None else ():
                        act.wait_ge(pe_did, PE.done("turn", i_early, u))
                        nc.scalar.activation(xt[u][:], A[u][:], ACT.Copy).then_inc(act_did, size("xt", u))
                    p.norm_apply_act(act, i_post, early, res, p.out, DV, "out", size,
                                     lambda i, u: act.wait_ge(p.stored[u], p.stores(i)))
                    p.norm_std(act, i_late, late, DV, "out", size)

                def body(back, front):
                    size = AC.sizes(back, front)
                    p.sqrt_table(act)
                    half(front, EARLY, back, LATE, back, size)
                    half(front, LATE, front, EARLY, back, size)

                act.sem_inc(act_did, AC.per_iteration)
                act.wait_ge(dve_did, DV.per_iteration)
                buffered_bodies(act, N_ITERS, body)

            @block.vector
            def _(dve):
                def half(i_early, early, i_late, late, size):
                    p.norm_stats(dve, i_late, late, res, "out", size,
                                 lambda i, u: dve.wait_ge(dve_did, DV.done("res", i, u)))
                    p.norm_moments(dve, i_late, late, DV, "out", size)
                    for u in early if i_early is not None else ():
                        dve.wait_ge(pool_did, PO.done("more", i_early, u))
                        dve.wait_ge(pe_did, PE.done("own", i_early, u))
                        nc.vector.tensor_tensor(both[u][:], tiles(B[u]), more[u][:], ALU.add
                                                ).then_inc(dve_did, size("both", u))
                    p.norm_rstd(dve, i_late, late, AC, "out", size)
                    p.norm_shift(dve, i_late, late, DV, "out", size)
                    for u in early if i_early is not None else ():
                        dve.wait_ge(dve_did, DV.done("both", i_early, u))
                        dve.wait_ge(act_did, AC.before("out_apply", i_early, u))
                        nc.vector.scalar_tensor_tensor(out=flat(res[u]), in0=flat(both[u]), scalar=0.0,
                                                       in1=flat(p.rows[i_early.buffer][u]), op0=ALU.max, op1=ALU.add
                                                       ).then_inc(dve_did, size("res", u))

                def body(back, front):
                    size = DV.sizes(back, front)
                    half(front, EARLY, back, LATE, size)
                    half(front, LATE, front, EARLY, size)

                dve.wait_ge(p.weights, 32)
                nc.vector.tensor_tensor(two[:], w[:, 0:2, :], w[:, 2:4, :], ALU.add).then_inc(setup_did, 1)
                dve.wait_ge(setup_did, 1)
                nc.vector.tensor_tensor(wm[:], two[:, 0, :], two[:, 1, :], ALU.add).then_inc(setup_did, 1)
                dve.wait_ge(setup_did, 2)
                nc.vector.tensor_scalar(wm[:], wm[:], 1.0 / H3, None, ALU.mult).then_inc(setup_did, 1)
                nc.vector.memset(p.eps[:], EPS).then_inc(dve_did, DV.per_iteration)
                buffered_bodies(dve, N_ITERS, body)






def resident(nc, ctx):
    return {
        "gather_index": ctx.enter_context(nc.sbuf_tensor("gather_index", [ET, E // EC, 2 * TILES], I32)),
        "scatter_index": ctx.enter_context(nc.sbuf_tensor("scatter_index", [ET, E // EC, TILES], I32)),
        "ident": ctx.enter_context(nc.sbuf_tensor("ident", [128, 128], F32)),
        "zeros": ctx.enter_context(nc.sbuf_tensor("zeros", [96, N * ROW // 96 // FILLS], F32)),
    }


def scratch(nc):
    made = {n: nc.dram_tensor(n, [N, D], F32, kind="Internal").ap() for n in ("x1", "h1", "h2", "x2", "x3")}
    made["agg_rows"] = nc.dram_tensor("agg_rows", [N, ROW], F32, kind="Internal").ap()
    return made


def four_graph_layers(nc, t):
    with ExitStack() as sems, ExitStack() as ctx:
        keep = resident(nc, ctx)
        keep["small"] = t["ident"][0:16, 0:16]
        keep["passed"] = sems.enter_context(nc.semaphore("passed"))
        keep["filled"] = sems.enter_context(nc.semaphore("filled"))
        keep["stored"] = [sems.enter_context(nc.semaphore(f"stored{u}")) for u in NODE_SLOTS]
        keep["stored_before"] = [0]
        t = {**t, **scratch(nc)}
        setup_pass(nc, sems, keep, t)
        layer0_edges(nc, sems, keep, t)
        layer0_nodes(nc, sems, keep, t)
        states = ["x1", "h1", "h2", "x2"]
        for l in range(3):
            layer1_edges(nc, sems, keep, t, l, t[states[l]])
            (layer1_last_nodes if l == 2 else layer1_nodes)(nc, sems, keep, t, l, t[states[l]], t[states[l + 1]])
        layer2_edges(nc, sems, keep, t)
        layer2_nodes(nc, sems, keep, t)
        layer3_edges(nc, sems, keep, t)
        layer3_nodes(nc, sems, keep, t)


def laid_out(inputs):
    import numpy as np

    a = {n: np.asarray(v) for n, v in inputs.items()}
    dst = a["dst"]
    edge = np.full(1, -1, dst.dtype)
    tiles = lambda v: np.ascontiguousarray(v.reshape(E // ET, ET).T)
    chunks = lambda v: np.ascontiguousarray(v.reshape(E // EC, EC))
    of_head = (np.arange(D)[:, None] // (D // H0) == np.arange(H0)[None, :]).astype(np.float32)
    head_spread = np.zeros((64 + 32 + H0, 2, D), np.float32)
    for u in range(2):
        for first in (32 * u, 64 + 32 * u):
            head_spread[first:first + H0, u, :] = of_head.T
    head_spread = head_spread.reshape(-1, 2 * D)
    head_pick = np.zeros((64 + 32 + H3, 2, H3, D), np.float32)
    for u in range(2):
        for h in range(H3):
            head_pick[[32 * u + h, 64 + 32 * u + h], u, h, :] = 1.0
    head_pick = head_pick.reshape(-1, 2 * H3 * D)
    out = {
        "x": a["x"],
        "src_tiles": tiles(a["src"]), "dst_tiles": tiles(dst),
        "next_tiles": tiles(np.concatenate([dst[1:], edge])),
        "dst_rows": chunks(dst), "prev_rows": chunks(np.concatenate([edge, dst[:-1]])),
        "type_rows": chunks(a["edge_type_8"]), "edge_weight_rows": chunks(a["edge_weight"]),
        "ident": np.eye(128, dtype=np.float32),
        "head_mask": np.concatenate([of_head / np.sqrt(np.float32(D // H0)), np.zeros((D, 32 - H0), np.float32)], 1),
        "head_spread": head_spread,
        "head_pick": head_pick,
        "L0_Wg": np.ascontiguousarray(a["L0_gnn_Wg"].reshape(3, D).T),
        "L0_Ws_turned": np.ascontiguousarray(a["L0_gnn_Ws"].T),
        "L0_alpha": a["L0_gnn_alpha"].reshape(1, 1), "L0_bg": a["L0_gnn_bg"].reshape(1, 1),
        "L0_bs_row": a["L0_gnn_bs"].reshape(1, D),
        "L1_ew1": a["L1_gnn_ew1"], "L1_ew2": a["L1_gnn_ew2"],
        "L1_nw1": a["L1_gnn_nw1"], "L1_nw2": a["L1_gnn_nw2"],
        "L1_eb1": a["L1_gnn_eb1"].reshape(3, D, 1), "L1_eb2": a["L1_gnn_eb2"].reshape(3, D, 1),
        "L1_nb1": a["L1_gnn_nb1"].reshape(3, D, 1), "L1_nb2": a["L1_gnn_nb2"].reshape(3, 1, D),
        "L1_nb2_rows": np.tile(a["L1_gnn_nb2"].reshape(3, D), (1, 4)),
        "L2_W": a["L2_gnn_W"], "L2_W0": a["L2_gnn_W0"],
        "L3_W": a["L3_gnn_W"], "L3_bias": a["L3_gnn_bias"].reshape(1, D),
        "L3_att_src": a["L3_gnn_att_src"].reshape(1, H3 * D),
        "L3_att_dst": a["L3_gnn_att_dst"].reshape(1, H3 * D),
    }
    for n in ("Wq", "Wk", "Wv", "Ws"):
        out[f"L0_{n}"] = a[f"L0_gnn_{n}"]
    for n in ("bq", "bk", "bv", "bs"):
        out[f"L0_{n}"] = a[f"L0_gnn_{n}"].reshape(D, 1)
    for layer in ("L0", "L1"):
        for n in ("gamma", "beta"):
            out[f"{layer}_{n}"] = a[f"{layer}_gnn_{n}"].reshape(D, 1)
    return out


def kernel(**inputs):
    import numpy as _np
    import concourse.bacc as _bacc
    from concourse import mybir as _mybir
    from concourse.bass_utils import run_bass_kernel_spmd as _run

    nc = _bacc.Bacc("TRN2", target_bir_lowering=False, num_devices=1)
    arrays = {f"in_{n}": _np.ascontiguousarray(a) for n, a in laid_out(inputs).items()}
    t = {n[3:]: nc.dram_tensor(n, a.shape, _mybir.dt.from_np(a.dtype), kind="ExternalInput").ap()
         for n, a in arrays.items()}
    t["out"] = nc.dram_tensor("out", [N, D], F32, kind="ExternalOutput").ap()
    four_graph_layers(nc, t)
    r = _run(nc, [arrays], core_ids=[0])
    return r.results[0]["out"]
```
